# Optimizing a Trainium2 kernel written in Bass

```python
import numpy as np
import jax
import jax.numpy as jnp

def _softmax(x, axis=-1):
    return jax.nn.softmax(x, axis=axis)

def _gelu(x):
    return jax.nn.gelu(x, approximate=True)

def _silu(x):
    return jax.nn.silu(x)

def _sigmoid(x):
    return jax.nn.sigmoid(x)

def _layernorm(x, axis=-1, eps=1e-05):
    m = jnp.mean(x, axis=axis, keepdims=True)
    v = jnp.var(x, axis=axis, keepdims=True)
    return (x - m) / jnp.sqrt(v + eps)

def _scatter_add(tgt, idx, src, axis=0):
    return tgt.at[idx].add(src)

def _segment_sum(src, seg, n):
    return jax.ops.segment_sum(src, seg, n)
kernel_name = 'mk_flamingo_gated_d2_seqx_r8_e468dd'

def setup_inputs(seed: int=0):
    np.random.seed(seed)
    _w = jnp.asarray

    def _rec_inputs():
        import jax
        import jax.numpy as jnp
        _rk = jax.random.key(seed)
        x = -0.0005207 + 1.001 * jax.random.normal(jax.random.fold_in(_rk, 1), (8, 100, 512), jnp.float32)
        _lenS = 100 - jax.random.randint(jax.random.fold_in(_rk, 7), (8,), 0, max(1, 100 // 4) + 1, jnp.int32)
        _lenS2 = 1444 - jax.random.randint(jax.random.fold_in(_rk, 8), (8,), 0, max(1, 1444 // 4) + 1, jnp.int32)
        _ctx_4096P = jax.random.normal(jax.random.fold_in(_rk, 11), (8, 16, 512), jnp.float32)
        _ctx_4096c = jax.random.dirichlet(jax.random.fold_in(_rk, 511), 0.3 * jnp.ones((16,), jnp.float32), (8, 1444))
        _ctx_4096t = jnp.einsum('bsk,bkd->bsd', _ctx_4096c, _ctx_4096P)
        _ctx_4096t = _ctx_4096t * jax.lax.rsqrt(jnp.mean(jnp.square(_ctx_4096t)) + 1e-12) * 0.953939
        ctx_4096 = -0.00010331 + 0.999899 * (_ctx_4096t + 0.3 * jax.random.normal(jax.random.fold_in(_rk, 611), (8, 1444, 512), jnp.float32))
        _g = jax.random.normal(jax.random.fold_in(_rk, 9001), (2, 2), jnp.float32)
        _g = jnp.sign(_g) * jnp.maximum(jnp.abs(_g), 1.0) + (_g == 0) * 1.0
        g_xattn = _g[0]
        g_ffn = _g[1]
        return (x, ctx_4096, g_xattn, g_ffn)
    x, ctx_4096, g_xattn, g_ffn = _rec_inputs()

    def _L0_xattn_setup():
        import jax, jax.numpy as jnp
        import numpy as np
        B, Q, D = (8, 64, 512)
        CTX = 512
        H, KV, HD = (16, 4, 96)
        G = H // KV
        key = jax.random.key(seed)
        ks = jax.random.split(key, 6)
        s = 0.02
        return {'latents': jax.random.normal(ks[0], (B, Q, D), jnp.float32), 'context': jax.random.normal(ks[1], (B, CTX, D), jnp.float32), 'Wq': jax.random.normal(ks[2], (H * HD, D), jnp.float32) * s, 'Wk': jax.random.normal(ks[3], (KV * HD, D), jnp.float32) * s, 'Wv': jax.random.normal(ks[4], (KV * HD, D), jnp.float32) * s, 'Wo': jax.random.normal(ks[5], (D, H * HD), jnp.float32) * s}
    _L0_xattn_all = _L0_xattn_setup()
    _L0_xattn_in = {k: v for k, v in _L0_xattn_all.items() if k in ('Wq', 'Wk', 'Wv', 'Wo')}
    del _L0_xattn_all

    def _L0_ffn_setup():
        import jax, jax.numpy as jnp
        import numpy as np
        N_STREAMS = 4
        DIM = 128
        SINKHORN_ITERS = 50
        SINKHORN_TAU = 0.1
        RMS_EPS = 1.1920929e-07

        def sinkhorn_log(logits, num_iters=SINKHORN_ITERS, tau=SINKHORN_TAU):
            Z = logits / tau
            u0 = jnp.zeros(Z.shape[:-1], Z.dtype)
            v0 = jnp.zeros_like(u0)

            def step(carry, _):
                u, v = carry
                u = -jax.nn.logsumexp(Z + v[..., None, :], axis=-1)
                v = -jax.nn.logsumexp(Z + u[..., :, None], axis=-2)
                return ((u, v), None)
            (u, v), _ = jax.lax.scan(step, (u0, v0), None, length=num_iters)
            return jnp.exp(Z + u[..., :, None] + v[..., None, :])
        key = jax.random.key(seed)
        ks = jax.random.split(key, 6)
        B, T = (4, 256)
        n, C = (N_STREAMS, DIM)
        wd = n * C
        x = jax.random.normal(ks[0], (B, T, wd), dtype=jnp.float32)
        W_res = 0.01 * jax.random.normal(ks[1], (n * n, wd), dtype=jnp.float32)
        W_pre = 0.01 * jax.random.normal(ks[2], (n, wd), dtype=jnp.float32)
        W_post = 0.01 * jax.random.normal(ks[3], (n, wd), dtype=jnp.float32)
        H_res_base = jnp.full((n, n), -0.5, dtype=jnp.float32)
        H_res_base = H_res_base.at[jnp.arange(n), jnp.arange(n)].set(0.0)
        H_pre_base = jnp.zeros((n,), dtype=jnp.float32).at[0].set(1.0)
        H_post_base = jnp.zeros((n,), dtype=jnp.float32)
        gate = jnp.array([5.0], dtype=jnp.float32)
        W_branch = 1.0 / np.sqrt(C) * jax.random.normal(ks[4], (C, C), dtype=jnp.float32)
        return {'x': x, 'W_res': W_res, 'W_pre': W_pre, 'W_post': W_post, 'H_res_base': H_res_base, 'H_pre_base': H_pre_base, 'H_post_base': H_post_base, 'gate': gate, 'W_branch': W_branch}
    _L0_ffn_all = _L0_ffn_setup()
    _L0_ffn_in = {k: v for k, v in _L0_ffn_all.items() if k in ('W_res', 'W_pre', 'W_post', 'H_res_base', 'H_pre_base', 'H_post_base', 'gate', 'W_branch')}
    del _L0_ffn_all

    def _L1_xattn_setup():
        import jax, jax.numpy as jnp
        import numpy as np
        TEXT_DIM = 512
        FEATURE_DIM = 512

        def _xavier_uniform(key, shape):
            fan_in, fan_out = (shape[1], shape[0])
            limit = float(np.sqrt(6.0 / (fan_in + fan_out)))
            return jax.random.uniform(key, shape, jnp.float32, -limit, limit)
        key = jax.random.key(seed)
        k1, k2, k3, k4 = jax.random.split(key, 4)
        text = jax.random.normal(k1, (8, 256, TEXT_DIM), jnp.float32)
        features = jax.random.normal(k2, (8, 72, FEATURE_DIM), jnp.float32)
        Wq = _xavier_uniform(k3, (FEATURE_DIM, TEXT_DIM))
        bq = jnp.zeros((FEATURE_DIM,), jnp.float32)
        Wk = _xavier_uniform(k4, (FEATURE_DIM, FEATURE_DIM))
        bk = jnp.zeros((FEATURE_DIM,), jnp.float32)
        return {'text': text, 'features': features, 'Wq': Wq, 'bq': bq, 'Wk': Wk, 'bk': bk}
    _L1_xattn_all = _L1_xattn_setup()
    _L1_xattn_in = {k: v for k, v in _L1_xattn_all.items() if k in ('Wq', 'bq', 'Wk', 'bk')}
    del _L1_xattn_all

    def _L1_ffn_setup():
        import jax, jax.numpy as jnp
        import numpy as np
        D_MODEL = 512
        D_FF = 1376
        key = jax.random.key(seed)
        k1, k2, k3, k4 = jax.random.split(key, 4)
        x = jax.random.normal(k1, (2, 256, D_MODEL), dtype=jnp.float32)
        W_gate = jax.random.normal(k2, (D_FF, D_MODEL), dtype=jnp.float32) * D_MODEL ** (-0.5)
        W_up = jax.random.normal(k3, (D_FF, D_MODEL), dtype=jnp.float32) * D_MODEL ** (-0.5)
        W_down = jax.random.normal(k4, (D_MODEL, D_FF), dtype=jnp.float32) * D_FF ** (-0.5)
        return {'x': x, 'W_gate': W_gate, 'W_up': W_up, 'W_down': W_down}
    _L1_ffn_all = _L1_ffn_setup()
    _L1_ffn_in = {k: v for k, v in _L1_ffn_all.items() if k in ('W_gate', 'W_up', 'W_down')}
    del _L1_ffn_all
    return {'x': x, 'ctx_4096': ctx_4096, 'g_xattn': g_xattn, 'g_ffn': g_ffn, 'L0_xattn_Wq': _L0_xattn_in['Wq'], 'L0_xattn_Wk': _L0_xattn_in['Wk'], 'L0_xattn_Wv': _L0_xattn_in['Wv'], 'L0_xattn_Wo': _L0_xattn_in['Wo'], 'L0_ffn_W_res': _L0_ffn_in['W_res'], 'L0_ffn_W_pre': _L0_ffn_in['W_pre'], 'L0_ffn_W_post': _L0_ffn_in['W_post'], 'L0_ffn_H_res_base': _L0_ffn_in['H_res_base'], 'L0_ffn_H_pre_base': _L0_ffn_in['H_pre_base'], 'L0_ffn_H_post_base': _L0_ffn_in['H_post_base'], 'L0_ffn_gate': _L0_ffn_in['gate'], 'L0_ffn_W_branch': _L0_ffn_in['W_branch'], 'L1_xattn_Wq': _L1_xattn_in['Wq'], 'L1_xattn_bq': _L1_xattn_in['bq'], 'L1_xattn_Wk': _L1_xattn_in['Wk'], 'L1_xattn_bk': _L1_xattn_in['bk'], 'L1_ffn_W_gate': _L1_ffn_in['W_gate'], 'L1_ffn_W_up': _L1_ffn_in['W_up'], 'L1_ffn_W_down': _L1_ffn_in['W_down']}

def reference(x, ctx_4096, g_xattn, g_ffn, L0_xattn_Wq, L0_xattn_Wk, L0_xattn_Wv, L0_xattn_Wo, L0_ffn_W_res, L0_ffn_W_pre, L0_ffn_W_post, L0_ffn_H_res_base, L0_ffn_H_pre_base, L0_ffn_H_post_base, L0_ffn_gate, L0_ffn_W_branch, L1_xattn_Wq, L1_xattn_bq, L1_xattn_Wk, L1_xattn_bk, L1_ffn_W_gate, L1_ffn_W_up, L1_ffn_W_down):
    import jax
    import jax.numpy as jnp

    def _L0_xattn_ref(latents, context, Wq, Wk, Wv, Wo):
        import jax, jax.numpy as jnp
        import numpy as np
        B, Q, D = (8, 64, 512)
        CTX = 512
        H, KV, HD = (16, 4, 96)
        G = H // KV
        b, q_len, _ = latents.shape
        hidden = jnp.concatenate([context, latents], axis=1)
        s_len = hidden.shape[1]
        q = (latents @ Wq.T).reshape(b, q_len, H, HD)
        k = (hidden @ Wk.T).reshape(b, s_len, KV, HD)
        v = (hidden @ Wv.T).reshape(b, s_len, KV, HD)
        q = q.transpose(0, 2, 1, 3).reshape(b, KV, G, q_len, HD)
        k = k.transpose(0, 2, 1, 3)
        v = v.transpose(0, 2, 1, 3)
        scale = 1.0 / jnp.sqrt(jnp.asarray(HD, q.dtype))
        scores = jnp.einsum('bkgqd,bksd->bkgqs', q, k) * scale
        attn = jax.nn.softmax(scores.astype(jnp.float32), axis=-1).astype(q.dtype)
        out = jnp.einsum('bkgqs,bksd->bkgqd', attn, v)
        out = out.reshape(b, H, q_len, HD).transpose(0, 2, 1, 3).reshape(b, q_len, H * HD)
        return out @ Wo.T

    def _L0_ffn_ref(x, W_res, W_pre, W_post, H_res_base, H_pre_base, H_post_base, gate, W_branch):
        import jax, jax.numpy as jnp
        import numpy as np
        N_STREAMS = 4
        DIM = 128
        SINKHORN_ITERS = 50
        SINKHORN_TAU = 0.1
        RMS_EPS = 1.1920929e-07

        def sinkhorn_log(logits, num_iters=SINKHORN_ITERS, tau=SINKHORN_TAU):
            Z = logits / tau
            u0 = jnp.zeros(Z.shape[:-1], Z.dtype)
            v0 = jnp.zeros_like(u0)

            def step(carry, _):
                u, v = carry
                u = -jax.nn.logsumexp(Z + v[..., None, :], axis=-1)
                v = -jax.nn.logsumexp(Z + u[..., :, None], axis=-2)
                return ((u, v), None)
            (u, v), _ = jax.lax.scan(step, (u0, v0), None, length=num_iters)
            return jnp.exp(Z + u[..., :, None] + v[..., None, :])
        B, T, nC = x.shape
        n = N_STREAMS
        C = nC // n
        x_norm = x * jax.lax.rsqrt(jnp.mean(x * x, axis=-1, keepdims=True) + RMS_EPS)
        H_res_logits = (x_norm @ W_res.T).reshape(B, T, n, n) + H_res_base
        H_pre_logits = x_norm @ W_pre.T + H_pre_base
        H_post_logits = x_norm @ W_post.T + H_post_base
        H_res = sinkhorn_log(H_res_logits)
        H_pre = jax.nn.softmax(H_pre_logits, axis=-1)
        H_post = jax.nn.softmax(H_post_logits, axis=-1)
        g = jax.nn.sigmoid(gate)[0]
        I = jnp.eye(n, dtype=H_res.dtype)
        H_res = (1.0 - g) * I + g * H_res
        x_streams = x.reshape(B, T, n, C)
        x_pre = jnp.einsum('btnc,btn->btc', x_streams, H_pre)
        y = x_pre @ W_branch
        x_mixed = jnp.einsum('btij,btjc->btic', H_res, x_streams)
        y_distributed = jnp.einsum('btc,btn->btnc', y, H_post)
        return (x_mixed + y_distributed).reshape(B, T, nC)

    def _L1_xattn_ref(text, features, Wq, bq, Wk, bk):
        import jax, jax.numpy as jnp
        import numpy as np
        TEXT_DIM = 512
        FEATURE_DIM = 512

        def _xavier_uniform(key, shape):
            fan_in, fan_out = (shape[1], shape[0])
            limit = float(np.sqrt(6.0 / (fan_in + fan_out)))
            return jax.random.uniform(key, shape, jnp.float32, -limit, limit)
        Q = jnp.einsum('btx,dx->btd', text, Wq) + bq
        K = jnp.einsum('bpx,dx->bpd', features, Wk) + bk
        scale = 1.0 / jnp.sqrt(jnp.asarray(K.shape[-1], K.dtype))
        scores = jnp.einsum('btd,bpd->btp', Q, K) * scale
        attn = jax.nn.softmax(scores, axis=-1)
        attended = jnp.einsum('btp,bpd->btd', attn, features)
        return attended

    def _L1_ffn_ref(x, W_gate, W_up, W_down):
        import jax, jax.numpy as jnp
        import numpy as np
        D_MODEL = 512
        D_FF = 1376
        out_shape = x.shape[:-1] + (W_down.shape[0],)
        xf = x.reshape(-1, x.shape[-1])
        up = jnp.einsum('td,fd->tf', xf, W_up)
        gate = jax.nn.silu(jnp.einsum('td,fd->tf', xf, W_gate))
        h = gate * up
        y = jnp.einsum('tf,df->td', h, W_down)
        return y.reshape(out_shape)
    x = x + jnp.tanh(g_xattn[0]) * _L0_xattn_ref(_layernorm(x, axis=-1), ctx_4096, L0_xattn_Wq, L0_xattn_Wk, L0_xattn_Wv, L0_xattn_Wo)
    x = x + jnp.tanh(g_ffn[0]) * _L0_ffn_ref(_layernorm(x, axis=-1), L0_ffn_W_res, L0_ffn_W_pre, L0_ffn_W_post, L0_ffn_H_res_base, L0_ffn_H_pre_base, L0_ffn_H_post_base, L0_ffn_gate, L0_ffn_W_branch)
    x = x + jnp.tanh(g_xattn[1]) * _L1_xattn_ref(_layernorm(x, axis=-1), ctx_4096, L1_xattn_Wq, L1_xattn_bq, L1_xattn_Wk, L1_xattn_bk)
    x = x + jnp.tanh(g_ffn[1]) * _L1_ffn_ref(_layernorm(x, axis=-1), L1_ffn_W_gate, L1_ffn_W_up, L1_ffn_W_down)
    return x

_drawn_inputs = setup_inputs


def setup_inputs(seed=0):
    import zlib

    import numpy as np

    out = dict(_drawn_inputs(seed))
    spreads = {'g_ffn': (-1.0, 0.2),
     'L0_ffn_H_post_base': (0.0, 0.561),
     'L1_xattn_bq': (0.0, 0.1),
     'L1_xattn_bk': (0.0, 0.8)}
    factors = {'L0_xattn_Wq': 6.842, 'L0_xattn_Wk': 6.849}
    for name, (base, spread) in spreads.items():
        noise = np.random.default_rng([zlib.crc32(name.encode()), seed]).standard_normal(out[name].shape)
        drawn = base * np.exp(spread * noise) if base else spread * noise
        out[name] = jnp.asarray(drawn.astype(out[name].dtype))
    for name, factor in factors.items():
        out[name] = (out[name] * factor).astype(out[name].dtype)
    return out
```

```python
from contextlib import ExitStack

import concourse.bass as bass
from concourse import mybir

ALU = mybir.AluOpType
ACT = mybir.ActivationFunctionType
AX = mybir.AxisListType
F32 = mybir.dt.float32
F32R = mybir.dt.float32r

B, T, D, CTX = 8, 100, 512, 1444
H, KV, HD = 16, 4, 96
G = H // KV
STREAMS, SW = 4, 128
SINKHORN_STEPS, TAU = 50, 0.1
RMS_EPS, LN_EPS = 1.1920929e-07, 1e-05
FF = 1376
NTOK = B * T
NK = D // 128
HALF = NTOK // 2
BANK = 512


def split_product(pe, out, a_hi, a_lo, b_hi, b_lo, start, stop):
    pe.matmul(out, a_hi, b_hi, start=start, stop=False)
    pe.matmul(out, a_hi, b_lo, start=False, stop=False)
    return pe.matmul(out, a_lo, b_hi, start=False, stop=stop)


def chunk_sizes(n, size):
    return [(i, min(size, n - i)) for i in range(0, n, size)]


def layer_norm_stats(nc, dve, link, stats, mv, var, x_of, loaded, eps):
    for b in range(B):
        dve.wait_ge(loaded, 16 * (b + 1))
        link(nc.vector.bn_stats(stats[:, b, :], x_of(b)))
        link(nc.vector.bn_aggr(mv[:, b, :], stats[:, b, :]))
    return link(nc.vector.tensor_scalar(var, mv[:, :, 1], eps, None, ALU.add))


def refined_rsqrt(nc, link, rstd, sd, var, tmp):
    link(nc.vector.reciprocal(rstd, sd))
    link(nc.vector.tensor_tensor(tmp, rstd, rstd, ALU.mult))
    link(nc.vector.tensor_tensor(tmp, tmp, var, ALU.mult))
    link(nc.vector.tensor_scalar(tmp, tmp, -0.5, 1.5, ALU.mult, ALU.add))
    link(nc.vector.tensor_tensor(rstd, rstd, tmp, ALU.mult))


def project_queries(nc, whole, io, keep):
    with ExitStack() as ctx:
        def sb(name, shape, dt=F32):
            return ctx.enter_context(nc.sbuf_tensor(name, shape, dt))

        def sem(name):
            return whole.enter_context(nc.semaphore(name))

        x_rows = sb("q_x", [T, B, D])
        xnT = sb("q_xnT", [128, NK, NTOK])
        xnT_hi = sb("q_xnT_hi", [128, NK, NTOK], F32R)
        xnT_lo = sb("q_xnT_lo", [128, NK, NTOK], F32R)
        wq = sb("q_wq", [128, NK, H * HD])
        wq_hi = sb("q_wq_hi", [128, NK, H * HD], F32R)
        wq_lo = sb("q_wq_lo", [128, NK, H * HD], F32R)
        wkv = sb("q_wkv", [128, 2, NK, KV * HD])
        QR = 4
        q_hi = sb("q_q_hi", [HD, QR, HALF], F32R)
        q_lo = sb("q_q_lo", [HD, QR, HALF], F32R)
        stats = sb("q_stats", [T, B, 6])
        mv = sb("q_mv", [T, B, 2])
        var, sd, rstd, tmp = (sb("q_" + n, [T, B]) for n in ("var", "sd", "rstd", "tmp"))
        ps = ctx.enter_context(nc.psum_tensor("q_ps", [128, 8, BANK], F32))

        x_loaded, wq_loaded, wkv_loaded, small_loaded = (sem("q_" + n) for n in ("x_in", "wq_in", "wkv_in", "small_in"))
        step, var_ready, sd_ready, xn_ready = (sem("q_" + n) for n in ("step", "var", "sd", "xn"))
        ident_ready, turned, xnT_ready, xnT_hi_ready, xnT_lo_ready = (
            sem("q_" + n) for n in ("ident", "turned", "xnT", "xnT_hi", "xnT_lo"))
        wq_hi_ready, wq_lo_ready, wkv_hi_ready, wkv_lo_ready = (sem("q_" + n) for n in ("wqh", "wql", "wkvh", "wkvl"))
        q_done, q_hi_ready, q_lo_ready, lat_stored, gate_ready = (
            sem("q_" + n) for n in ("done", "qh", "ql", "lat", "gate"))
        q_stored = [sem(f"q_stored{i}") for i in range(QR)]

        with nc.Block() as block:
            @block.sync
            def _(sp):
                sp.dma_start(x_rows[:, :, :], io["x4"].rearrange("b t d -> t b d")).then_inc(x_loaded, 16)
                sp.wait_ge(xnT_ready, B)
                sp.dma_start(io["latT"], xnT[:, :, :]).then_inc(lat_stored, 16)
                for i in range(2 * H):
                    h, half, slot = i // 2, i % 2, i % QR
                    sp.wait_ge(q_lo_ready, i + 1)
                    for q, to in ((q_hi, io["q_hi"]), (q_lo, io["q_lo"])):
                        sp.dma_start(to[:, half * (B // 2):(half + 1) * (B // 2), h, :],
                                     q[:, slot, :].bitcast(F32).rearrange("d (b t) -> d b t", t=T)).then_inc(q_stored[slot], 16)
                sp.wait_ge(small_loaded, 16)
                sp.wait_ge(lat_stored, 16)
                for i in range(QR):
                    sp.wait_ge(q_stored[i], 32 * (2 * H // QR))

            @block.gpsimd
            def _(pool):
                nc.gpsimd.memset(keep["ident"][:, :], 0.0).then_inc(ident_ready, 1)
                pool.wait_ge(ident_ready, 1)
                nc.gpsimd.affine_select(out=keep["ident"][:, :], in_=keep["ident"][:, :], compare_op=ALU.not_equal,
                                        fill=1.0, base=0, pattern=[[-1, 128]], channel_multiplier=1).then_inc(ident_ready, 1)
                for k in range(NK):
                    pool.wait_ge(wq_hi_ready, k + 1)
                    nc.gpsimd.tensor_tensor(wq_lo[:, k, :], wq[:, k, :], wq_hi[:, k, :].bitcast(F32),
                                            ALU.subtract).then_inc(wq_lo_ready, 1)
                for b in range(B):
                    cols = slice(b * T, (b + 1) * T)
                    pool.wait_ge(xnT_hi_ready, b + 1)
                    nc.gpsimd.tensor_tensor(xnT_lo[:, :, cols], xnT[:, :, cols], xnT_hi[:, :, cols].bitcast(F32),
                                            ALU.subtract).then_inc(xnT_lo_ready, 1)
                pool.wait_ge(wkv_loaded, 32)
                for i, name in enumerate(("wk", "wv")):
                    nc.gpsimd.tensor_copy(keep[name + "_hi"][:, :, :], wkv[:, i, :, :]).then_inc(wkv_hi_ready, 1)
                    pool.wait_ge(wkv_hi_ready, i + 1)
                    nc.gpsimd.tensor_tensor(keep[name + "_lo"][:, :, :], wkv[:, i, :, :],
                                            keep[name + "_hi"][:, :, :].bitcast(F32), ALU.subtract).then_inc(wkv_lo_ready, 1)

            @block.scalar
            def _(act):
                act.dma_start(wq[:, :, :], io["wqT"]).then_inc(wq_loaded, 16)
                act.dma_start(wkv[:, 0, :, :], io["wkT"]).then_inc(wkv_loaded, 16)
                act.dma_start(wkv[:, 1, :, :], io["wvT"]).then_inc(wkv_loaded, 16)
                act.dma_start(keep["gates"][:, 0:5], io["gates"].partition_broadcast(128)).then_inc(small_loaded, 16)
                act.wait_ge(wq_loaded, 16)
                for k in range(NK):
                    nc.scalar.activation(wq_hi[:, k, :], wq[:, k, :], ACT.Copy).then_inc(wq_hi_ready, 1)
                act.wait_ge(var_ready, 1)
                nc.scalar.activation(sd[:, :], var[:, :], ACT.Sqrt).then_inc(sd_ready, 1)
                for b in range(B):
                    act.wait_ge(turned, b + 1)
                    nc.scalar.activation(xnT[:, :, b * T:(b + 1) * T],
                                         ps[:, b % 2, 0:NK * T].rearrange("p (k t) -> p k t", t=T),
                                         ACT.Copy).then_inc(xnT_ready, 1)
                act.wait_ge(small_loaded, 16)
                nc.scalar.activation(keep["tanh"][:, 0:4], keep["gates"][:, 0:4], ACT.Tanh).then_inc(gate_ready, 1)
                nc.scalar.activation(keep["gates"][:, 5:6], keep["gates"][:, 4:5], ACT.Exp, scale=-1.0).then_inc(gate_ready, 1)
                for i in range(2 * H):
                    act.wait_ge(q_done, i + 1)
                    if i >= QR:
                        act.wait_ge(q_stored[i % QR], 32 * (i // QR))
                    nc.scalar.activation(q_hi[:, i % QR, :], ps[0:HD, 2 + i % 4, 0:HALF], ACT.Copy).then_inc(q_hi_ready, 1)

            @block.vector
            def _(dve):
                done = [0]

                def link(ins):
                    done[0] += 1
                    ins.then_inc(step, 1)
                    dve.wait_ge(step, done[0])

                dve.wait_ge(x_loaded, 16)
                for b in range(B):
                    link(nc.vector.bn_stats(stats[:, b, :], x_rows[:, b, :]))
                    link(nc.vector.bn_aggr(mv[:, b, :], stats[:, b, :]))
                nc.vector.tensor_scalar(var[:, :], mv[:, :, 1], LN_EPS, None, ALU.add).then_inc(var_ready, 1)
                dve.wait_ge(var_ready, 1)
                dve.wait_ge(sd_ready, 1)
                refined_rsqrt(nc, link, rstd[:, :], sd[:, :], var[:, :], tmp[:, :])
                for b in range(B):
                    nc.vector.tensor_scalar(x_rows[:, b, :], x_rows[:, b, :], mv[:, b, 0:1], rstd[:, b:b + 1],
                                            ALU.subtract, ALU.mult).then_inc(xn_ready, 1)
                for b in range(B):
                    cols = slice(b * T, (b + 1) * T)
                    dve.wait_ge(xnT_ready, b + 1)
                    nc.vector.tensor_copy(xnT_hi[:, :, cols], xnT[:, :, cols]).then_inc(xnT_hi_ready, 1)
                dve.wait_ge(gate_ready, 2)
                link(nc.vector.tensor_scalar(keep["gates"][:, 6:7], keep["gates"][:, 5:6], 1.0, None, ALU.add))
                link(nc.vector.reciprocal(keep["sigmoid"][:, 0:1], keep["gates"][:, 6:7]))
                link(nc.vector.tensor_scalar(keep["sigmoid"][:, 1:2], keep["sigmoid"][:, 0:1], -1.0, 1.0, ALU.mult, ALU.add))
                for i in range(2 * H):
                    dve.wait_ge(q_hi_ready, i + 1)
                    nc.vector.tensor_tensor(q_lo[:, i % QR, :], ps[0:HD, 2 + i % 4, 0:HALF],
                                            q_hi[:, i % QR, :].bitcast(F32), ALU.subtract).then_inc(q_lo_ready, 1)

            @block.tensor
            def _(pe):
                pe.wait_ge(ident_ready, 2)
                for b in range(B):
                    pe.wait_ge(xn_ready, b + 1)
                    if b >= 2:
                        pe.wait_ge(xnT_ready, b - 1)
                    for k in range(NK):
                        mm = pe.transpose(ps[:, b % 2, k * T:(k + 1) * T], x_rows[:, b, k * 128:(k + 1) * 128],
                                          keep["ident"][0:T, 0:T])
                    mm.then_inc(turned, 1)
                pe.wait_ge(wq_lo_ready, NK)
                for i in range(2 * H):
                    h, half = i // 2, i % 2
                    pe.wait_ge(xnT_lo_ready, (half + 1) * (B // 2) if i < 2 else B)
                    if i >= 4:
                        pe.wait_ge(q_lo_ready, i - 3)
                    for k in range(NK):
                        w, t = slice(h * HD, (h + 1) * HD), slice(half * HALF, (half + 1) * HALF)
                        mm = split_product(pe, ps[0:HD, 2 + i % 4, 0:HALF], wq_hi[:, k, w], wq_lo[:, k, w],
                                           xnT_hi[:, k, t], xnT_lo[:, k, t], k == 0, k == NK - 1)
                    mm.then_inc(q_done, 1)


NKEY = CTX + T
KEY_TILES = [(128 * i, 128) for i in range(11)] + [(1408, 68), (1476, 68)]
NT = len(KEY_TILES)
CHUNKS = [(0, 384, 0, 3), (384, 384, 3, 3), (768, 384, 6, 3), (1152, 392, 9, 4)]
NCH = len(CHUNKS)
CHUNK_MAX = 392
GROUPS = NCH * KV + NT
MAXIMA = NCH * H
STEPS = KV * NT
RING = 3
LAG = 3
TURN_AT, SPREAD_AT, OUT_AT, MAX_ROW_AT = 4, 6, 8, 11
NEGATE_AT = 9
MAX_GROUPS = {c * (KV + 3) + kv + 1: (c, kv) for c in range(NCH) for kv in range(KV)}
ROUND_AFTER = {KV + 2: 2, 2 * (KV + 3) - 1: 3}
AHEAD = (6, 14)
assert sum(n for _, n in KEY_TILES) == NKEY


def attend_context(nc, whole, io, keep):
    scale = float(HD) ** -0.5
    with ExitStack() as ctx:
        def sb(name, shape, dt=F32):
            return ctx.enter_context(nc.sbuf_tensor(name, shape, dt))

        def sem(name):
            return whole.enter_context(nc.semaphore("a_" + name))

        raw = sb("a_raw", [128, NK, CHUNK_MAX])
        c_hi = sb("a_c_hi", [128, 2, NK, CHUNK_MAX], F32R)
        c_lo = sb("a_c_lo", [128, 2, NK, CHUNK_MAX], F32R)
        k_hi = sb("a_k_hi", [HD + 1, KV, NKEY], F32R)
        k_lo = sb("a_k_lo", [HD + 1, KV, NKEY], F32R)
        v_hi = sb("a_v_hi", [128, NT, KV, HD + 1], F32R)
        v_lo = sb("a_v_lo", [128, NT, KV, HD + 1], F32R)
        q_hi = sb("a_q_hi", [HD + 1, H, T], F32R)
        q_lo = sb("a_q_lo", [HD + 1, H, T], F32R)
        p = sb("a_p", [128, 2, G * T])
        p_hi = sb("a_p_hi", [128, RING, G * T], F32R)
        p_lo = sb("a_p_lo", [128, RING, G * T], F32R)
        maxima = sb("a_max", [T, H, NCH])
        head_max = sb("a_hmax", [T, G])
        neg_max = sb("a_nmax", [T, G, HD + 1])
        ones = sb("a_ones", [128, HD])
        recip = sb("a_recip", [T, G])
        diag = sb("a_diag", [T, G, T])
        o_sb = sb("a_o", [HD + 1, G * T])
        x_rows = sb("a_x", [T, D])
        wo = sb("a_wo", [HD, H, D])
        ps = ctx.enter_context(nc.psum_tensor("a_ps", [128, 8, BANK], F32))
        S0, M0, O_BANK, B_BANK, Y_BANK = 0, 3, 5, 6, 7

        raw_loaded, chunk_hi, chunk_ready, preset, wo_loaded = (
            sem(n) for n in ("raw", "chunk_hi", "chunk_ready", "preset", "wo_in"))
        q_loaded, x_loaded, x1_ready, x1_stored = (sem(n) for n in ("q_in", "x_in", "x1", "x1_out"))
        proj_done, proj_hi, proj_lo = sem("proj"), sem("proj_hi"), sem("proj_lo")
        rough_done, rough_max, max_ready, neg_ready, row_placed, row_ready = (
            sem(n) for n in ("rough", "rough_max", "max", "neg", "row_placed", "row"))
        scores, exp_done, p_hi_ready, p_lo_ready, pv_done = (sem(n) for n in ("scores", "exp", "p_hi", "p_lo", "pv"))
        o_copied, sums_turned, recip_ready, diag_ready, spread, normal, wo_done = (
            sem(n) for n in ("o_copied", "turned", "recip", "diag", "spread", "normal", "wo"))

        def group_place(gi):
            c, i = (min(gi // (KV + 3), NCH - 1), gi - (KV + 3) * min(gi // (KV + 3), NCH - 1))
            k0, n, t0, _ = CHUNKS[c]
            if i < KV:
                return (ps[0:HD, M0 + gi % 2, 0:n], k_hi[0:HD, i, k0:k0 + n], k_lo[0:HD, i, k0:k0 + n])
            t = t0 + i - KV
            rows = KEY_TILES[t][1]
            return (ps[0:rows, M0 + gi % 2, 0:KV * HD].rearrange("p (h d) -> p h d", d=HD),
                    v_hi[0:rows, t, :, 0:HD], v_lo[0:rows, t, :, 0:HD])

        with nc.Block() as block:
            @block.sync
            def _(sp):
                def load_chunk(b, c):
                    sp.wait_ge(chunk_ready, NCH * b + c)
                    k0, n, _, _ = CHUNKS[c]
                    own = min(n, CTX - k0)
                    sp.dma_start(raw[:, :, 0:own], io["ctxT"][b, :, :, k0:k0 + own]).then_inc(raw_loaded, 16)
                    if own < n:
                        sp.dma_start(raw[:, :, own:n], io["latT4"][b]).then_inc(raw_loaded, 16)

                def load_queries(b):
                    sp.wait_ge(scores, STEPS * b)
                    sp.dma_start(q_hi[0:HD, :, :].bitcast(F32), io["q_hi4"][b]).then_inc(q_loaded, 16)
                    sp.dma_start(q_lo[0:HD, :, :].bitcast(F32), io["q_lo4"][b]).then_inc(q_loaded, 16)

                def store_x1(b):
                    sp.wait_ge(x1_ready, b + 1)
                    sp.dma_start(io["x1_4"][b], x_rows[:, :]).then_inc(x1_stored, 16)
                    sp.wait_ge(x1_stored, 16 * b + 16)

                def batch(b, first, last):
                    load_chunk(b, 2)
                    if not first:
                        store_x1(b - 1)
                    sp.dma_start(x_rows[:, :], io["x4"][b]).then_inc(x_loaded, 16)
                    load_chunk(b, 3)
                    if not last:
                        load_chunk(b + 1, 0)
                        load_chunk(b + 1, 1)
                        load_queries(b + 1)

                load_chunk(0, 0)
                load_queries(0)
                load_chunk(0, 1)
                sp.dma_start(wo[:, :, :], io["woT"]).then_inc(wo_loaded, 16)
                batch(0, True, False)
                with sp.Fori(1, B - 1) as b:
                    batch(b, False, False)
                batch(B - 1, False, True)
                store_x1(B - 1)

            @block.gpsimd
            def _(pool):
                def split_chunk(b, c):
                    n, slot = CHUNKS[c][1], c % 2
                    pool.wait_ge(chunk_hi, NCH * b + (c + 1))
                    nc.gpsimd.tensor_tensor(c_lo[:, slot, :, 0:n], raw[:, :, 0:n],
                                            c_hi[:, slot, :, 0:n].bitcast(F32), ALU.subtract).then_inc(chunk_ready, 1)

                def batch(b, last):
                    split_chunk(b, 2)
                    split_chunk(b, 3)
                    if not last:
                        split_chunk(b + 1, 0)
                        split_chunk(b + 1, 1)

                split_chunk(0, 0)
                split_chunk(0, 1)
                with pool.Fori(0, B - 1) as b:
                    batch(b, False)
                batch(B - 1, True)

            @block.scalar
            def _(act):
                def project(b, gi):
                    act.wait_ge(proj_done, GROUPS * b + (gi + 1))
                    place, out_hi, _ = group_place(gi)
                    nc.scalar.activation(out_hi, place, ACT.Copy).then_inc(proj_hi, 1)

                def max_row(b, kv):
                    act.wait_ge(row_placed, KV * b + (kv + 1))
                    nc.scalar.activation(q_hi[HD:HD + 1, kv * G:(kv + 1) * G, :],
                                         ps[HD:HD + 1, B_BANK, 0:G * T].rearrange("p (g t) -> p g t", t=T),
                                         ACT.Copy).then_inc(row_ready, 1)

                def copy_o(b, kv):
                    act.wait_ge(pv_done, STEPS * b + NT * (kv + 1))
                    act.wait_ge(wo_done, KV * b + kv)
                    nc.scalar.activation(o_sb[:, :], ps[0:HD + 1, O_BANK, 0:G * T], ACT.Copy).then_inc(o_copied, 1)

                def batch(b, first):
                    if not first:
                        copy_o(b - 1, KV - 1)
                    for gi in range(GROUPS - 1):
                        project(b, gi)
                    max_row(b, 0)
                    project(b, GROUPS - 1)
                    for g in range(STEPS):
                        kv, t, n = g // NT, g % NT, KEY_TILES[g % NT][1]
                        act.wait_ge(scores, STEPS * b + (g + 1))
                        act.wait_ge(p_lo_ready, STEPS * b + max(g - 1, 0))
                        nc.scalar.activation(p[0:n, g % 2, :], ps[0:n, S0 + g % 3, 0:G * T], ACT.Exp,
                                             scale=scale).then_inc(exp_done, 1)
                        act.wait_ge(exp_done, STEPS * b + (g + 1))
                        act.wait_ge(pv_done, STEPS * b + max(g - RING + 1, 0))
                        nc.scalar.activation(p_hi[0:n, g % RING, :], p[0:n, g % 2, :], ACT.Copy).then_inc(p_hi_ready, 1)
                        if kv and t == LAG - 1:
                            copy_o(b, kv - 1)
                        if kv < KV - 1 and t == MAX_ROW_AT:
                            max_row(b, kv + 1)

                batch(0, True)
                with act.Fori(1, B) as b:
                    batch(b, False)
                copy_o(B - 1, KV - 1)

            @block.vector
            def _(dve):
                nc.vector.memset(ones[:, :], 1.0).then_inc(preset, 1)
                nc.vector.memset(neg_max[:, :, :], 0.0).then_inc(preset, 1)
                nc.vector.memset(k_hi[HD:HD + 1, :, :].bitcast(F32), 1.0).then_inc(preset, 1)
                nc.vector.memset(k_lo[HD:HD + 1, :, :].bitcast(F32), 0.0).then_inc(preset, 1)
                nc.vector.memset(q_lo[HD:HD + 1, :, :].bitcast(F32), 0.0).then_inc(preset, 1)
                nc.vector.memset(v_hi[:, :, :, HD:HD + 1].bitcast(F32), 1.0).then_inc(preset, 1)
                nc.vector.memset(v_lo[:, :, :, HD:HD + 1].bitcast(F32), 0.0).then_inc(preset, 1)

                def project(b, gi):
                    dve.wait_ge(proj_hi, GROUPS * b + (gi + 1))
                    place, out_hi, out_lo = group_place(gi)
                    nc.vector.tensor_tensor(out_lo, place, out_hi.bitcast(F32), ALU.subtract).then_inc(proj_lo, 1)

                def round_chunk(b, c, before=None):
                    loads = NCH + 1
                    n, slot = CHUNKS[c][1], c % 2
                    if c >= 2:
                        dve.wait_ge(proj_done, GROUPS * b + (KV + 3) * (c - 1))
                    elif before is not None:
                        dve.wait_ge(proj_done, GROUPS * before + GROUPS)
                    dve.wait_ge(raw_loaded, 16 * loads * b + 16 * (loads if c == NCH - 1 else c + 1))
                    nc.vector.tensor_copy(c_hi[:, slot, :, 0:n], raw[:, :, 0:n]).then_inc(chunk_hi, 1)

                def rough_maximum(b, c, head):
                    n = H * c + head
                    dve.wait_ge(rough_done, MAXIMA * b + (n + 1))
                    nc.vector.tensor_reduce(maxima[:, head, c:c + 1], ps[0:T, S0 + n % 3, 0:CHUNKS[c][1]],
                                            AX.X, ALU.max).then_inc(rough_max, 1)

                def negate(b, kv):
                    if kv == 0:
                        dve.wait_ge(rough_max, MAXIMA * b + MAXIMA)
                    nc.vector.tensor_reduce(head_max[:, :], maxima[:, kv * G:(kv + 1) * G, :], AX.X,
                                            ALU.max).then_inc(max_ready, 1)
                    dve.wait_ge(max_ready, KV * b + (kv + 1))
                    dve.wait_ge(row_placed, KV * b + kv)
                    nc.vector.tensor_scalar(neg_max[:, :, HD], head_max[:, :], -1.0, None, ALU.mult).then_inc(neg_ready, 1)

                def invert_sums(b, kv):
                    dve.wait_ge(sums_turned, KV * b + (kv + 1))
                    nc.vector.reciprocal(recip[:, :], ps[0:T, B_BANK, G * T:G * T + G]).then_inc(recip_ready, 1)
                    dve.wait_ge(recip_ready, KV * b + (kv + 1))
                    nc.vector.tensor_tensor(diag[:, :, :], keep["ident"][0:T, 0:T].unsqueeze(1).to_broadcast([T, G, T]),
                                            recip[:, :].unsqueeze(2).to_broadcast([T, G, T]), ALU.mult).then_inc(diag_ready, 1)

                def normalise(b, kv):
                    dve.wait_ge(spread, KV * b + (kv + 1))
                    nc.vector.tensor_tensor(o_sb[0:HD, :], ps[0:HD, B_BANK, 0:G * T], o_sb[0:HD, :], ALU.mult).then_inc(normal, 1)

                def residual(b):
                    dve.wait_ge(wo_done, KV * b + KV)
                    dve.wait_ge(x_loaded, 16 * b + 16)
                    nc.vector.scalar_tensor_tensor(out=x_rows[:, :], in0=ps[0:T, Y_BANK, :], scalar=keep["tanh"][0:T, 0:1],
                                                   in1=x_rows[:, :], op0=ALU.mult, op1=ALU.add).then_inc(x1_ready, 1)

                def batch(b, first, last):
                    for gi in range(GROUPS):
                        if gi in MAX_GROUPS:
                            c, kv = MAX_GROUPS[gi]
                            for i in range(G):
                                rough_maximum(b, c, kv * G + i)
                        project(b, gi)
                        if gi in ROUND_AFTER:
                            round_chunk(b, ROUND_AFTER[gi])
                        if not first and gi == 0:
                            invert_sums(b - 1, KV - 1)
                        if not first and gi == 1:
                            normalise(b - 1, KV - 1)
                        if not first and gi == 4:
                            residual(b - 1)
                        if gi == GROUPS - 2:
                            negate(b, 0)
                    for s in range(STEPS):
                        kv, t, n = s // NT, s % NT, KEY_TILES[s % NT][1]
                        dve.wait_ge(p_hi_ready, STEPS * b + (s + 1))
                        nc.vector.tensor_tensor(p_lo[0:n, s % RING, :], p[0:n, s % 2, :],
                                                p_hi[0:n, s % RING, :].bitcast(F32), ALU.subtract).then_inc(p_lo_ready, 1)
                        if not last and s in AHEAD:
                            round_chunk(b + 1, AHEAD.index(s), b)
                        if kv < KV - 1 and t == NEGATE_AT:
                            negate(b, kv + 1)
                        if kv and t == TURN_AT:
                            invert_sums(b, kv - 1)
                        if kv and t == SPREAD_AT:
                            normalise(b, kv - 1)

                round_chunk(0, 0)
                round_chunk(0, 1)
                batch(0, True, False)
                with dve.Fori(1, B - 1) as b:
                    batch(b, False, False)
                batch(B - 1, False, True)
                invert_sums(B - 1, KV - 1)
                normalise(B - 1, KV - 1)
                residual(B - 1)

            @block.tensor
            def _(pe):
                pe.wait_ge(preset, 7)
                pe.wait_ge(wo_loaded, 16)

                def rough_scores(b, c, head):
                    n = H * c + head
                    kv = head // G
                    pe.wait_ge(rough_max, MAXIMA * b + max(n - 2, 0))
                    if head % G == 0:
                        pe.wait_ge(proj_hi, GROUPS * b + (c * (KV + 3) + kv + 1))
                    if n == 0:
                        pe.wait_ge(exp_done, STEPS * b)
                        pe.wait_ge(q_loaded, 32 * b + 32)
                    k0, keys, _, _ = CHUNKS[c]
                    pe.matmul(ps[0:T, S0 + n % 3, 0:keys], q_hi[0:HD, head, :], k_hi[0:HD, kv, k0:k0 + keys],
                              start=True, stop=True).then_inc(rough_done, 1)

                def place_max_row(b, kv):
                    pe.wait_ge(neg_ready, KV * b + (kv + 1))
                    pe.wait_ge(row_ready, KV * b + kv)
                    pe.wait_ge(normal, KV * b + max(kv - 1, 0))
                    for i in range(G):
                        mm = pe.matmul(ps[0:HD + 1, B_BANK, i * T:(i + 1) * T], neg_max[:, i, :],
                                       keep["ident"][0:T, 0:T], start=True, stop=True)
                    mm.then_inc(row_placed, 1)

                def project(b, gi):
                    c, i = (min(gi // (KV + 3), NCH - 1), gi - (KV + 3) * min(gi // (KV + 3), NCH - 1))
                    k0, n, t0, _ = CHUNKS[c]
                    slot = c % 2
                    if i == 0:
                        pe.wait_ge(chunk_ready, NCH * b + (c + 1))
                    pe.wait_ge(proj_lo, GROUPS * b + max(gi - 1, 0))
                    place = group_place(gi)[0]
                    for k in range(NK):
                        if i < KV:
                            w = slice(i * HD, (i + 1) * HD)
                            mm = split_product(pe, place, keep["wk_hi"][:, k, w], keep["wk_lo"][:, k, w],
                                               c_hi[:, slot, k, 0:n], c_lo[:, slot, k, 0:n], k == 0, k == NK - 1)
                        else:
                            key0, rows = KEY_TILES[t0 + i - KV]
                            keys = slice(key0 - k0, key0 - k0 + rows)
                            mm = split_product(pe, ps[0:rows, M0 + gi % 2, 0:KV * HD], c_hi[:, slot, k, keys],
                                               c_lo[:, slot, k, keys], keep["wv_hi"][:, k, :], keep["wv_lo"][:, k, :],
                                               k == 0, k == NK - 1)
                        if gi in MAX_GROUPS:
                            rough_scores(b, MAX_GROUPS[gi][0], MAX_GROUPS[gi][1] * G + k)
                        if (gi, k) == (GROUPS - 1, NK - 2):
                            place_max_row(b, 0)
                    mm.then_inc(proj_done, 1)

                def score(b, g):
                    kv, t = g // NT, g % NT
                    k0, n = KEY_TILES[t]
                    pe.wait_ge(exp_done, STEPS * b + max(g - 2, 0))
                    if g == 0:
                        pe.wait_ge(rough_max, MAXIMA * b + MAXIMA)
                        pe.wait_ge(proj_lo, GROUPS * b + GROUPS)
                    if t == 0:
                        pe.wait_ge(row_ready, KV * b + (kv + 1))
                    q = slice(kv * G, (kv + 1) * G)
                    split_product(pe, ps[0:n, S0 + g % 3, 0:G * T], k_hi[:, kv, k0:k0 + n], k_lo[:, kv, k0:k0 + n],
                                  q_hi[:, q, :], q_lo[:, q, :], True, True).then_inc(scores, 1)

                def weigh_values(b, g):
                    kv, t = g // NT, g % NT
                    n = KEY_TILES[t][1]
                    pe.wait_ge(p_lo_ready, STEPS * b + (g + 1))
                    if t == 0:
                        pe.wait_ge(o_copied, KV * b + kv)
                    split_product(pe, ps[0:HD + 1, O_BANK, 0:G * T], v_hi[0:n, t, kv, :], v_lo[0:n, t, kv, :],
                                  p_hi[0:n, g % RING, :], p_lo[0:n, g % RING, :], t == 0, t == NT - 1).then_inc(pv_done, 1)

                def turn_sums(b, kv):
                    pe.wait_ge(o_copied, KV * b + (kv + 1))
                    pe.wait_ge(row_ready, KV * b + min(kv + 2, KV))
                    for i in range(G):
                        mm = pe.matmul(ps[0:T, B_BANK, G * T + i:G * T + i + 1], o_sb[HD:HD + 1, i * T:(i + 1) * T],
                                       ones[HD:HD + 1, 0:1], start=True, stop=True)
                    mm.then_inc(sums_turned, 1)

                def spread_recip(b, kv):
                    pe.wait_ge(diag_ready, KV * b + (kv + 1))
                    pe.matmul(ps[0:HD, B_BANK, 0:G * T], ones[0:T, :], diag[:, :, :],
                              start=True, stop=True).then_inc(spread, 1)

                def project_out(b, kv):
                    pe.wait_ge(normal, KV * b + (kv + 1))
                    if kv == 0:
                        pe.wait_ge(x1_ready, b)
                    for i in range(G):
                        mm = pe.matmul(ps[0:T, Y_BANK, :], o_sb[0:HD, i * T:(i + 1) * T], wo[:, kv * G + i, :],
                                       start=(kv == 0 and i == 0), stop=(kv == KV - 1 and i == G - 1))
                    mm.then_inc(wo_done, 1)

                def batch(b, first):
                    for gi in range(GROUPS):
                        project(b, gi)
                        if not first and gi < 3:
                            (turn_sums, spread_recip, project_out)[gi](b - 1, KV - 1)
                    for s in range(STEPS + LAG):
                        kv, t = s // NT, s % NT
                        if s < STEPS:
                            score(b, s)
                            if kv < KV - 1 and t == MAX_ROW_AT:
                                place_max_row(b, kv + 1)
                        if s >= LAG:
                            weigh_values(b, s - LAG)
                        if 0 < kv < KV and t == TURN_AT:
                            turn_sums(b, kv - 1)
                        if 0 < kv < KV and t == SPREAD_AT:
                            spread_recip(b, kv - 1)
                        if 0 < kv < KV and t == OUT_AT:
                            project_out(b, kv - 1)

                batch(0, True)
                with pe.Fori(1, B) as b:
                    batch(b, False)
                for end in (turn_sums, spread_recip, project_out):
                    end(B - 1, KV - 1)


def hyper_connection(nc, whole, io, keep):
    with ExitStack() as ctx:
        def sb(name, shape, dt=F32):
            return ctx.enter_context(nc.sbuf_tensor("b_" + name, shape, dt))

        def sem(name):
            return whole.enter_context(nc.semaphore("b_" + name))

        x_rows = keep["x_rows"]
        xn = sb("xn", [T, B, D])
        xnT = sb("xnT", [128, 2, NK, T])
        yn = sb("yn", [T, B, STREAMS, SW])
        y = sb("y", [T, B, SW])
        squares = sb("sq", [T, D])
        w_h = sb("w", [128, NK, 24])
        w_branch = sb("wb", [SW, SW])
        h_base = sb("base", [T, 24])
        mixer = sb("mixer", [T, 2])
        raw = sb("raw", [128, 2, NK, D])
        stats, mv = sb("stats", [T, B, 6]), sb("mv", [T, B, 2])
        var, sd, tmp, rstd = (sb("s%d" % i, [T, B]) for i in range(4))
        square_sum, mean_sq, sd2, rstd2 = (sb("r%d" % i, [T, B]) for i in range(4))
        z = sb("z", [T, B, 6, 4])
        row_max, row_sum = sb("rmax", [T, B, 6]), sb("rsum", [T, B, 6])
        row_recip = sb("rrecip", [T, B, 2])
        row_ln = sb("rln", [T, B, 4])
        h_pp = sb("pp", [T, B, 2, 4])
        sink = sb("sink", [T, B, 4, 4])
        h_res = sb("res", [T, B, 4, 4])
        marginal = sb("marginal", [T, B, 4])
        ps = ctx.enter_context(nc.psum_tensor("b_ps", [128, 8, BANK], F32))
        L_BANK, Y0 = 2, 4

        x_loaded, small_loaded, raw_loaded, w_hi_ready, w_lo_ready = (sem(n) for n in ("x_in", "small", "raw", "w_hi", "w_lo"))
        step, var_ready, sd_ready, xn_ready, turned, xnT_ready = (sem(n) for n in ("step", "var", "sd", "xn", "turned", "xnT"))
        squared, logits_done, branch_done, yn_ready = (sem(n) for n in ("squared", "logits", "branch", "yn"))
        mean_ready, sd2_ready, z_ready, e_ready, sums_ready, ln_ready, m_ready, e2_ready = (
            sem(n) for n in ("mean", "sd2", "z", "e", "sums", "ln", "m", "e2"))

        with nc.Block() as block:
            @block.sync
            def _(sp):
                sp.dma_start(x_rows[:, :, :], io["x1_4"].rearrange("b t d -> t b d")).then_inc(x_loaded, 16)
                sp.dma_start(raw[:, 0, :, :], io["wq1T"]).then_inc(raw_loaded, 16)
                sp.dma_start(raw[:, 1, :, :], io["wk1"]).then_inc(raw_loaded, 16)
                sp.dma_start(keep["bq1"][:, :], io["bq1"]).then_inc(raw_loaded, 16)
                sp.dma_start(keep["bk1"][:, :], io["bk1"]).then_inc(raw_loaded, 16)
                sp.wait_ge(raw_loaded, 64)

            @block.gpsimd
            def _(pool):
                for i, name in enumerate(("wq1", "wk1")):
                    pool.wait_ge(w_hi_ready, i + 1)
                    nc.gpsimd.tensor_tensor(keep[name + "_lo"][:, :, :], raw[:, i, :, :],
                                            keep[name + "_hi"][:, :, :].bitcast(F32), ALU.subtract).then_inc(w_lo_ready, 1)

            @block.scalar
            def _(act):
                act.dma_start(w_h[:, :, :], io["whT"]).then_inc(small_loaded, 16)
                act.dma_start(w_branch[:, :], io["w_branch"]).then_inc(small_loaded, 16)
                act.dma_start(h_base[:, :], io["h_base"].partition_broadcast(T)).then_inc(small_loaded, 16)
                act.wait_ge(var_ready, 1)
                nc.scalar.activation(sd[:, :], var[:, :], ACT.Sqrt).then_inc(sd_ready, 1)
                for b in range(B):
                    act.wait_ge(turned, b + 1)
                    nc.scalar.activation(xnT[:, b % 2, :, :], ps[:, b % 2, 0:NK * T].rearrange("p (k t) -> p k t", t=T),
                                         ACT.Copy).then_inc(xnT_ready, 1)
                    if b:
                        act.wait_ge(squared, b)
                    nc.scalar.activation(squares[:, :], xn[:, b, :], ACT.Square,
                                         accum_out=square_sum[:, b:b + 1]).then_inc(squared, 1)
                act.wait_ge(mean_ready, 1)
                nc.scalar.activation(sd2[:, :], mean_sq[:, :], ACT.Sqrt).then_inc(sd2_ready, 1)
                act.wait_ge(z_ready, 2)
                nc.scalar.activation(z[:, :, :, :], z[:, :, :, :], ACT.Exp).then_inc(e_ready, 1)
                act.wait_ge(sums_ready, 1)
                nc.scalar.activation(row_ln[:, :, :], row_sum[:, :, 0:4], ACT.Ln).then_inc(ln_ready, 1)
                act.wait_ge(m_ready, 1)
                nc.scalar.activation(sink[:, :, :, :], h_res[:, :, :, :], ACT.Exp).then_inc(e2_ready, 1)
                act.wait_ge(raw_loaded, 64)
                for i, name in enumerate(("wq1", "wk1")):
                    nc.scalar.activation(keep[name + "_hi"][:, :, :], raw[:, i, :, :], ACT.Copy).then_inc(w_hi_ready, 1)

            @block.vector
            def _(dve):
                done = [0]

                def link(ins):
                    done[0] += 1
                    ins.then_inc(step, 1)
                    dve.wait_ge(step, done[0])

                def along_rows(v):
                    return v.unsqueeze(3).to_broadcast([T, B, v.shape[2], 4])

                def along_cols(v):
                    return v.unsqueeze(2).to_broadcast([T, B, 4, 4])

                def columns(m):
                    return m.rearrange("p b i j -> p b j i")

                dve.wait_ge(x_loaded, 16)
                for b in range(B):
                    link(nc.vector.bn_stats(stats[:, b, :], x_rows[:, b, :]))
                    link(nc.vector.bn_aggr(mv[:, b, :], stats[:, b, :]))
                nc.vector.tensor_scalar(var[:, :], mv[:, :, 1], LN_EPS, None, ALU.add).then_inc(var_ready, 1)
                dve.wait_ge(var_ready, 1)
                dve.wait_ge(sd_ready, 1)
                refined_rsqrt(nc, link, rstd[:, :], sd[:, :], var[:, :], tmp[:, :])
                for b in range(B):
                    nc.vector.tensor_scalar(xn[:, b, :], x_rows[:, b, :], mv[:, b, 0:1], rstd[:, b:b + 1],
                                            ALU.subtract, ALU.mult).then_inc(xn_ready, 1)
                for b in range(B):
                    dve.wait_ge(branch_done, b + 1)
                    nc.vector.tensor_copy(yn[:, b, :, :], ps[0:T, Y0 + b % 2, :].rearrange("p (n c) -> p n c", c=SW)).then_inc(yn_ready, 1)
                dve.wait_ge(squared, B)
                nc.vector.tensor_scalar(mean_sq[:, :], square_sum[:, :], 1.0 / D, RMS_EPS, ALU.mult, ALU.add).then_inc(mean_ready, 1)
                dve.wait_ge(mean_ready, 1)
                dve.wait_ge(sd2_ready, 1)
                refined_rsqrt(nc, link, rstd2[:, :], sd2[:, :], mean_sq[:, :], tmp[:, :])
                dve.wait_ge(logits_done, B)
                dve.wait_ge(small_loaded, 48)
                zf = z[:, :, :, :].rearrange("p b i j -> p b (i j)")
                link(nc.vector.tensor_tensor(zf, ps[0:T, L_BANK, 0:24 * B].rearrange("p (b n) -> p b n", n=24),
                                             rstd2[:, :].unsqueeze(2).to_broadcast([T, B, 24]), ALU.mult))
                link(nc.vector.tensor_tensor(zf, zf, h_base[:, :].unsqueeze(1).to_broadcast([T, B, 24]), ALU.add))
                link(nc.vector.tensor_scalar(zf[:, :, 0:16], zf[:, :, 0:16], 1.0 / TAU, None, ALU.mult))
                link(nc.vector.tensor_reduce(row_max[:, :, :], z[:, :, :, :], AX.X, ALU.max))
                nc.vector.tensor_tensor(z[:, :, :, :], z[:, :, :, :], along_rows(row_max[:, :, :]), ALU.subtract).then_inc(z_ready, 1)
                dve.wait_ge(z_ready, 1)
                nc.vector.tensor_copy(h_res[:, :, :, :], z[:, :, 0:4, :]).then_inc(z_ready, 1)
                dve.wait_ge(e_ready, 1)
                nc.vector.tensor_reduce(row_sum[:, :, :], z[:, :, :, :], AX.X, ALU.add).then_inc(sums_ready, 1)
                dve.wait_ge(sums_ready, 1)
                link(nc.vector.reciprocal(row_recip[:, :, :], row_sum[:, :, 4:6]))
                link(nc.vector.tensor_tensor(h_pp[:, :, :, :], z[:, :, 4:6, :], along_rows(row_recip[:, :, :]), ALU.mult))
                link(nc.vector.tensor_scalar(h_pp[:, :, 1, :], h_pp[:, :, 1, :], keep["tanh"][0:T, 2:3], None, ALU.mult))
                link(nc.vector.tensor_scalar(mixer[:, :], keep["sigmoid"][0:T, :], keep["tanh"][0:T, 2:3], None, ALU.mult))
                dve.wait_ge(ln_ready, 1)
                link(nc.vector.tensor_tensor(h_res[:, :, :, :], h_res[:, :, :, :], along_rows(row_ln[:, :, :]), ALU.subtract))
                link(nc.vector.tensor_reduce(marginal[:, :, :], columns(h_res[:, :, :, :]), AX.X, ALU.max))
                nc.vector.tensor_tensor(h_res[:, :, :, :], h_res[:, :, :, :], along_cols(marginal[:, :, :]), ALU.subtract).then_inc(m_ready, 1)
                dve.wait_ge(e2_ready, 1)

                def sum_to_one(m, spread):
                    link(nc.vector.tensor_reduce(marginal[:, :, :], m, AX.X, ALU.add))
                    link(nc.vector.reciprocal(marginal[:, :, :], marginal[:, :, :]))
                    link(nc.vector.tensor_tensor(sink[:, :, :, :], sink[:, :, :, :], spread(marginal[:, :, :]), ALU.mult))

                sum_to_one(columns(sink[:, :, :, :]), along_cols)
                for _ in range(SINKHORN_STEPS - 1):
                    sum_to_one(sink[:, :, :, :], along_rows)
                    sum_to_one(columns(sink[:, :, :, :]), along_cols)
                flat = h_res[:, :, :, :].rearrange("p b i j -> p b (i j)")
                link(nc.vector.tensor_scalar(h_res[:, :, :, :], sink[:, :, :, :], mixer[:, 0:1], None, ALU.mult))
                link(nc.vector.tensor_scalar(flat[:, :, 0:16:5], flat[:, :, 0:16:5], mixer[:, 1:2], None, ALU.add))
                for j in range(STREAMS):
                    for b in range(B):
                        if j == 0:
                            ins = nc.vector.tensor_scalar(y[:, b, :], yn[:, b, 0, :], h_pp[:, b, 0, 0:1], None, ALU.mult)
                        else:
                            dve.wait_ge(step, done[0] - B + 1)
                            ins = nc.vector.scalar_tensor_tensor(out=y[:, b, :], in0=yn[:, b, j, :], scalar=h_pp[:, b, 0, j:j + 1],
                                                                 in1=y[:, b, :], op0=ALU.mult, op1=ALU.add)
                        done[0] += 1
                        ins.then_inc(step, 1)
                for b in range(B):
                    for j in range(STREAMS + 1):
                        for i in range(STREAMS):
                            stream = slice(i * SW, (i + 1) * SW)
                            by, of = ((h_pp[:, b, 1, i:i + 1], y[:, b, :]) if j == STREAMS else
                                      (h_res[:, b, i, j:j + 1], xn[:, b, j * SW:(j + 1) * SW]))
                            dve.wait_ge(step, done[0] - STREAMS + 1)
                            nc.vector.scalar_tensor_tensor(out=x_rows[:, b, stream], in0=of, scalar=by,
                                                           in1=x_rows[:, b, stream], op0=ALU.mult, op1=ALU.add).then_inc(step, 1)
                            done[0] += 1
                dve.wait_ge(step, done[0])

            @block.tensor
            def _(pe):
                pe.wait_ge(small_loaded, 48)

                def products(b):
                    pe.wait_ge(xnT_ready, b + 1)
                    for k in range(NK):
                        mm = pe.matmul(ps[0:T, L_BANK, 24 * b:24 * (b + 1)], xnT[:, b % 2, k, :], w_h[:, k, :],
                                       start=(k == 0), stop=(k == NK - 1))
                    mm.then_inc(logits_done, 1)
                    if b >= 2:
                        pe.wait_ge(yn_ready, b - 1)
                    for k in range(NK):
                        mm = pe.matmul(ps[0:T, Y0 + b % 2, k * SW:(k + 1) * SW], xnT[:, b % 2, k, :], w_branch[:, :],
                                       start=True, stop=True)
                    mm.then_inc(branch_done, 1)

                for b in range(B):
                    pe.wait_ge(xn_ready, b + 1)
                    for k in range(NK):
                        mm = pe.transpose(ps[:, b % 2, k * T:(k + 1) * T], xn[:, b, k * 128:(k + 1) * 128],
                                          keep["ident"][0:T, 0:T])
                    mm.then_inc(turned, 1)
                    if b:
                        products(b - 1)
                products(B - 1)


def layer_norm_turned(nc, whole, name, keep, x_nT):
    with ExitStack() as ctx:
        def sb(n, shape, dt=F32):
            return ctx.enter_context(nc.sbuf_tensor(name + n, shape, dt))

        def sem(n):
            return whole.enter_context(nc.semaphore(name + n))

        x_rows = keep["x_rows"]
        xn = sb("xn", [T, B, D])
        stats, mv = sb("stats", [T, B, 6]), sb("mv", [T, B, 2])
        var, sd, tmp, rstd = (sb("s%d" % i, [T, B]) for i in range(4))
        ps = ctx.enter_context(nc.psum_tensor(name + "ps", [128, 8, BANK], F32))
        step, var_ready, sd_ready, xn_ready, turned, hi_ready, lo_ready = (
            sem(n) for n in ("step", "var", "sd", "xn", "turned", "hi", "lo"))
        TURN_BANKS = 4

        with nc.Block() as block:
            @block.scalar
            def _(act):
                act.wait_ge(var_ready, 1)
                nc.scalar.activation(sd[:, :], var[:, :], ACT.Sqrt).then_inc(sd_ready, 1)
                for b in range(B):
                    act.wait_ge(turned, b + 1)
                    nc.scalar.activation(x_nT[0][:, :, b * T:(b + 1) * T],
                                         ps[:, b % TURN_BANKS, 0:NK * T].rearrange("p (k t) -> p k t", t=T),
                                         ACT.Copy).then_inc(hi_ready, 1)

            @block.vector
            def _(dve):
                done = [0]

                def link(ins):
                    done[0] += 1
                    ins.then_inc(step, 1)
                    dve.wait_ge(step, done[0])

                for b in range(B):
                    link(nc.vector.bn_stats(stats[:, b, :], x_rows[:, b, :]))
                    link(nc.vector.bn_aggr(mv[:, b, :], stats[:, b, :]))
                nc.vector.tensor_scalar(var[:, :], mv[:, :, 1], LN_EPS, None, ALU.add).then_inc(var_ready, 1)
                dve.wait_ge(var_ready, 1)
                dve.wait_ge(sd_ready, 1)
                refined_rsqrt(nc, link, rstd[:, :], sd[:, :], var[:, :], tmp[:, :])
                for b in range(B):
                    nc.vector.tensor_scalar(xn[:, b, :], x_rows[:, b, :], mv[:, b, 0:1], rstd[:, b:b + 1],
                                            ALU.subtract, ALU.mult).then_inc(xn_ready, 1)
                for b in range(B):
                    cols = slice(b * T, (b + 1) * T)
                    dve.wait_ge(hi_ready, b + 1)
                    nc.vector.tensor_tensor(x_nT[1][:, :, cols],
                                            ps[:, b % TURN_BANKS, 0:NK * T].rearrange("p (k t) -> p k t", t=T),
                                            x_nT[0][:, :, cols].bitcast(F32), ALU.subtract).then_inc(lo_ready, 1)

            @block.tensor
            def _(pe):
                for b in range(B):
                    pe.wait_ge(xn_ready, b + 1)
                    if b >= TURN_BANKS:
                        pe.wait_ge(lo_ready, b - TURN_BANKS + 1)
                    for k in range(NK):
                        mm = pe.transpose(ps[:, b % TURN_BANKS, k * T:(k + 1) * T], xn[:, b, k * 128:(k + 1) * 128],
                                          keep["ident"][0:T, 0:T])
                    mm.then_inc(turned, 1)


def project_features(nc, whole, io, keep):
    with ExitStack() as ctx:
        def sb(name, shape, dt=F32):
            return ctx.enter_context(nc.sbuf_tensor("c_" + name, shape, dt))

        def sem(name):
            return whole.enter_context(nc.semaphore("c_" + name))

        x_nT = [sb(n, [128, NK, NTOK], F32R) for n in ("xnT_hi", "xnT_lo")]
        layer_norm_turned(nc, whole, "cn_", keep, x_nT)
        q = sb("q", [128, NK, NTOK])
        q_hi, q_lo = (sb(n, [128, NK, NTOK], F32R) for n in ("q_hi", "q_lo"))
        ps = ctx.enter_context(nc.psum_tensor("c_ps", [128, 8, BANK], F32))
        Q_BANKS, QBK = 6, 7
        q_done, q_copied, q_hi_ready, q_lo_ready, f_done, f_copied, qbk_done, qbk_ready = (
            sem(n) for n in ("q", "q_copied", "qh", "ql", "f", "f_copied", "qbk", "qbk_ready"))
        PRODUCTS = [(half, m) for half in range(2) for m in range(NK)]

        with nc.Block() as block:
            @block.scalar
            def _(act):
                for i, (half, m) in enumerate(PRODUCTS):
                    cols = slice(half * HALF, (half + 1) * HALF)
                    act.wait_ge(q_done, i + 1)
                    nc.scalar.activation(q[:, m, cols], ps[:, i % Q_BANKS, 0:HALF], ACT.Identity,
                                         bias=keep["bq1"][:, m:m + 1]).then_inc(q_copied, 1)
                for i, (half, m) in enumerate(PRODUCTS):
                    cols = slice(half * HALF, (half + 1) * HALF)
                    act.wait_ge(f_done, i + 1)
                    nc.scalar.activation(keep["queries"][:, m, cols], ps[:, (i + len(PRODUCTS)) % Q_BANKS, 0:HALF],
                                         ACT.Copy).then_inc(f_copied, 1)
                act.wait_ge(qbk_done, 1)
                nc.scalar.activation(keep["qbk"][:, :], ps[0:T, QBK, 0:B], ACT.Copy).then_inc(qbk_ready, 1)

            @block.vector
            def _(dve):
                for i, (half, m) in enumerate(PRODUCTS):
                    cols = slice(half * HALF, (half + 1) * HALF)
                    dve.wait_ge(q_copied, i + 1)
                    nc.vector.tensor_copy(q_hi[:, m, cols], q[:, m, cols]).then_inc(q_hi_ready, 1)
                    dve.wait_ge(q_hi_ready, i + 1)
                    nc.vector.tensor_tensor(q_lo[:, m, cols], q[:, m, cols], q_hi[:, m, cols].bitcast(F32),
                                            ALU.subtract).then_inc(q_lo_ready, 1)

            @block.tensor
            def _(pe):
                def product(i, w, of, done):
                    half, m = PRODUCTS[i % len(PRODUCTS)]
                    cols = slice(half * HALF, (half + 1) * HALF)
                    for k in range(NK):
                        to = slice(m * 128, (m + 1) * 128)
                        mm = split_product(pe, ps[:, i % Q_BANKS, 0:HALF], keep[w + "_hi"][:, k, to], keep[w + "_lo"][:, k, to],
                                           of[0][:, k, cols], of[1][:, k, cols], k == 0, k == NK - 1)
                    mm.then_inc(done, 1)

                for i in range(len(PRODUCTS)):
                    if i >= Q_BANKS:
                        pe.wait_ge(q_copied, i - Q_BANKS + 1)
                    product(i, "wq1", x_nT, q_done)
                for i in range(len(PRODUCTS)):
                    pe.wait_ge(q_lo_ready, NK * (PRODUCTS[i][0] + 1))
                    if i + len(PRODUCTS) - Q_BANKS < len(PRODUCTS):
                        pe.wait_ge(q_copied, i + len(PRODUCTS) - Q_BANKS + 1)
                    else:
                        pe.wait_ge(f_copied, i - Q_BANKS + 1)
                    product(i + len(PRODUCTS), "wk1", (q_hi, q_lo), f_done)
                for b in range(B):
                    for k in range(NK):
                        mm = pe.matmul(ps[0:T, QBK, b:b + 1], q[:, k, b * T:(b + 1) * T], keep["bk1"][:, k:k + 1],
                                       start=(k == 0), stop=(k == NK - 1))
                mm.then_inc(qbk_done, 1)


FT = [(128 * i, 128) for i in range(10)] + [(1280, 82), (1362, 82)]
NF = len(FT)
SB = chunk_sizes(CTX, BANK)
NSB = len(SB)
TG = NF // NSB
SCORES_AT, WEIGH_LAG, NATURAL_RING = 3, 3, 6
SCORE_PRODUCTS = [(k, part) for k in range(NK) for part in range(3)]
PER_STEP = len(SCORE_PRODUCTS) // ((NF - SCORES_AT) // NSB)
TURN_STEPS = (2, 6, 10)
EXP_STEP, QUERY_STEP, GAIN_STEP, UPDATE_STEP = 0, 1, 4, 3
MAX_STEPS = {6: 0, 9: 1}
SPLIT_STEPS = {1: (1, 1), 4: (2, 1), 9: (0, 2)}


def attend_features(nc, whole, io, keep):
    scale = float(D) ** -0.5
    with ExitStack() as ctx:
        def sb(name, shape, dt=F32):
            return ctx.enter_context(nc.sbuf_tensor("f_" + name, shape, dt))

        def sem(name):
            return whole.enter_context(nc.semaphore("f_" + name))

        x_rows = keep["x_rows"]
        feats = sb("feats", [128, 2, NK, CTX])
        c_hi, c_lo = (sb(n, [128, NSB, NK, BANK], F32R) for n in ("c_hi", "c_lo"))
        qs_hi, qs_lo = (sb(n, [128, NK, T], F32R) for n in ("q_hi", "q_lo"))
        n_hi, n_lo = (sb(n, [128, NATURAL_RING, D], F32R) for n in ("n_hi", "n_lo"))
        p = sb("p", [T, CTX])
        pT_hi, pT_lo = (sb(n, [128, NSB, TG, T], F32R) for n in ("pT_hi", "pT_lo"))
        bank_max = sb("bmax", [T, NSB])
        top, bias = sb("top", [T, 1]), sb("bias", [T, 1])
        sums, total, recip, gain = sb("sums", [T, NSB]), sb("total", [T, 1]), sb("recip", [T, 1]), sb("gain", [T, 1])
        ps = ctx.enter_context(nc.psum_tensor("f_ps", [128, 8, BANK], F32))
        S0, N0, P_BANK, O0 = 0, 3, 5, 6

        c_hi_ready, c_ready, qs_hi_ready, qs_ready, scored, maxed, top_ready, shifted, bias_ready = (
            sem(n) for n in ("c_hi", "c", "qs_hi", "qs", "scored", "maxed", "top", "shifted", "bias"))
        exp_done, p_turned, pT_hi_ready, pT_ready, n_turned, n_hi_ready, n_ready, weighed = (
            sem(n) for n in ("exp", "p_turned", "pT_hi", "pT", "n_turned", "n_hi", "n", "weighed"))
        total_ready, recip_ready, gain_ready, x3_ready = (sem(n) for n in ("total", "recip", "gain", "x3"))
        loaded = [sem("in%d" % c) for c in range(NSB)]

        def run(engine, batch):
            batch(0, 0, True, False)
            with engine.Fori(0, (B - 4) // 2) as pair:
                for i in range(2):
                    batch(2 * pair + (i + 1), (i + 1) % 2, False, False)
            for b in range(B - 3, B):
                batch(b, b % 2, False, b == B - 1)

        with nc.Block() as block:
            @block.sync
            def _(sp):
                def load(b, slot, c):
                    f0, n = SB[c]
                    sp.dma_start(feats[:, slot, :, f0:f0 + n], io["ctxT"][b, :, :, f0:f0 + n]).then_inc(loaded[c], 16)

                def reload(b, slot):
                    for c in range(NSB):
                        sp.wait_ge(scored, NSB * b - (NSB - c - 1))
                        load(b, slot, c)

                for b in range(2):
                    for c in range(NSB):
                        if b:
                            sp.wait_ge(loaded[c], 16)
                        load(b, b, c)
                with sp.Fori(1, B // 2) as pair:
                    for i in range(2):
                        reload(2 * pair + i, i)

            @block.gpsimd
            def _(pool):
                with pool.Fori(0, B // 2) as pair:
                    for slot in range(2):
                        for c, (f0, n) in enumerate(SB):
                            number = 2 * NSB * pair + (NSB * slot + c + 1)
                            pool.wait_ge(c_hi_ready, number)
                            nc.gpsimd.tensor_tensor(c_lo[:, c, :, 0:n], feats[:, slot, :, f0:f0 + n],
                                                    c_hi[:, c, :, 0:n].bitcast(F32), ALU.subtract).then_inc(c_ready, 1)

            @block.scalar
            def _(act):
                def take_queries(b, start):
                    act.wait_ge(scored, NSB * b)
                    nc.scalar.activation(qs_hi[:, :, :], keep["queries"][:, :, start:start + T] if isinstance(start, int)
                                         else keep["queries"][:, :, bass.ds(start, T)], ACT.Copy).then_inc(qs_hi_ready, 1)

                def batch(b, slot, first, last):
                    for t in range(NF):
                        n = FT[t][1]
                        act.wait_ge(n_turned, NF * b + (t + 1))
                        if not first or t >= NATURAL_RING:
                            act.wait_ge(weighed, NF * b + (t - NATURAL_RING + 1))
                        nc.scalar.activation(n_hi[0:n, t % NATURAL_RING, :], ps[0:n, N0 + t % 2, :], ACT.Copy).then_inc(n_hi_ready, 1)
                        if t == EXP_STEP:
                            act.wait_ge(bias_ready, b + 1)
                            for c, (f0, n) in enumerate(SB):
                                nc.scalar.activation(p[:, f0:f0 + n], ps[0:T, S0 + c, 0:n], ACT.Exp, scale=scale, bias=bias[:, :],
                                                     accum_out=sums[:, c:c + 1]).then_inc(exp_done, 1)
                        if t == QUERY_STEP and not last:
                            take_queries(b + 1, b * T + T)
                        if t in TURN_STEPS:
                            g = TURN_STEPS.index(t)
                            act.wait_ge(p_turned, NSB * b + (g + 1))
                            act.wait_ge(weighed, NF * b)
                            nc.scalar.activation(pT_hi[:, g, :, :], ps[:, P_BANK, 0:TG * T].rearrange("p (i t) -> p i t", t=T),
                                                 ACT.Copy).then_inc(pT_hi_ready, 1)

                take_queries(0, 0)
                run(act, batch)

            @block.vector
            def _(dve):
                def round_bank(b, slot, c):
                    f0, n = SB[c]
                    dve.wait_ge(loaded[c], 16 * b + 16)
                    if not (isinstance(b, int) and b == 0):
                        dve.wait_ge(scored, NSB * b + (c + 1 - NSB))
                    nc.vector.tensor_copy(c_hi[:, c, :, 0:n], feats[:, slot, :, f0:f0 + n]).then_inc(c_hi_ready, 1)

                def split_queries(b, start):
                    dve.wait_ge(qs_hi_ready, b + 1)
                    nc.vector.tensor_tensor(qs_lo[:, :, :], keep["queries"][:, :, start:start + T] if isinstance(start, int)
                                            else keep["queries"][:, :, bass.ds(start, T)],
                                            qs_hi[:, :, :].bitcast(F32), ALU.subtract).then_inc(qs_ready, 1)

                def bank_maximum(b, c):
                    dve.wait_ge(scored, NSB * b + (c + 1))
                    nc.vector.tensor_reduce(bank_max[:, c:c + 1], ps[0:T, S0 + c, 0:SB[c][1]], AX.X, ALU.max).then_inc(maxed, 1)

                def softmax_bias(b):
                    qbk = keep["qbk"][:, b:b + 1] if isinstance(b, int) else keep["qbk"][:, bass.ds(b, 1)]
                    dve.wait_ge(maxed, NSB * b + NSB)
                    nc.vector.tensor_reduce(top[:, :], bank_max[:, :], AX.X, ALU.max).then_inc(top_ready, 1)
                    dve.wait_ge(top_ready, b + 1)
                    nc.vector.tensor_tensor(top[:, :], top[:, :], qbk, ALU.add).then_inc(shifted, 1)
                    dve.wait_ge(shifted, 2 * b + 1)
                    nc.vector.tensor_tensor(top[:, :], qbk, top[:, :], ALU.subtract).then_inc(shifted, 1)
                    dve.wait_ge(shifted, 2 * b + 2)
                    dve.wait_ge(exp_done, NSB * b)
                    nc.vector.tensor_scalar(bias[:, :], top[:, :], scale, None, ALU.mult).then_inc(bias_ready, 1)

                def softmax_gain(b):
                    dve.wait_ge(exp_done, NSB * b + NSB)
                    nc.vector.tensor_reduce(total[:, :], sums[:, :], AX.X, ALU.add).then_inc(total_ready, 1)
                    dve.wait_ge(total_ready, b + 1)
                    nc.vector.reciprocal(recip[:, :], total[:, :]).then_inc(recip_ready, 1)
                    dve.wait_ge(recip_ready, b + 1)
                    dve.wait_ge(x3_ready, b)
                    nc.vector.tensor_scalar(gain[:, :], recip[:, :], keep["tanh"][0:T, 1:2], None, ALU.mult).then_inc(gain_ready, 1)

                def update(b, slot):
                    rows = x_rows[:, b, :]
                    dve.wait_ge(weighed, NF * b + NF)
                    dve.wait_ge(gain_ready, b + 1)
                    nc.vector.scalar_tensor_tensor(out=rows, in0=ps[0:T, O0 + slot, :], scalar=gain[:, :], in1=rows,
                                                   op0=ALU.mult, op1=ALU.add).then_inc(x3_ready, 1)

                def batch(b, slot, first, last):
                    bank_maximum(b, NSB - 1)
                    softmax_bias(b)
                    for t in range(NF):
                        n = FT[t][1]
                        dve.wait_ge(n_hi_ready, NF * b + (t + 1))
                        nc.vector.tensor_tensor(n_lo[0:n, t % NATURAL_RING, :], ps[0:n, N0 + t % 2, :],
                                                n_hi[0:n, t % NATURAL_RING, :].bitcast(F32), ALU.subtract).then_inc(n_ready, 1)
                        if t == QUERY_STEP and not last:
                            split_queries(b + 1, b * T + T)
                        if t in TURN_STEPS:
                            g = TURN_STEPS.index(t)
                            dve.wait_ge(pT_hi_ready, NSB * b + (g + 1))
                            nc.vector.tensor_tensor(pT_lo[:, g, :, :], ps[:, P_BANK, 0:TG * T].rearrange("p (i t) -> p i t", t=T),
                                                    pT_hi[:, g, :, :].bitcast(F32), ALU.subtract).then_inc(pT_ready, 1)
                        if t == UPDATE_STEP and not first:
                            update(b - 1, 1 - slot)
                        if t == GAIN_STEP:
                            softmax_gain(b)
                        if t in SPLIT_STEPS:
                            c, ahead = SPLIT_STEPS[t]
                            if not last and not (isinstance(b, int) and b + ahead >= B):
                                round_bank(b + ahead, (slot + ahead) % 2, c)
                        if t in MAX_STEPS and not last:
                            bank_maximum(b + 1, MAX_STEPS[t])

                for c in range(NSB):
                    round_bank(0, 0, c)
                split_queries(0, 0)
                for c in range(NSB - 1):
                    bank_maximum(0, c)
                round_bank(1, 1, 0)
                run(dve, batch)
                update(B - 1, (B - 1) % 2)
                dve.wait_ge(x3_ready, B)

            @block.tensor
            def _(pe):
                def scores(b, c, products):
                    f0, n = SB[c]
                    for i in products:
                        k, part = SCORE_PRODUCTS[i]
                        if i == 0:
                            pe.wait_ge(c_ready, NSB * b + (c + 1))
                            if c == 0:
                                pe.wait_ge(qs_ready, b + 1)
                            pe.wait_ge(exp_done, NSB * b)
                        mm = pe.matmul(ps[0:T, S0 + c, 0:n], (qs_lo if part == 2 else qs_hi)[:, k, :],
                                       (c_lo if part == 1 else c_hi)[:, c, k, 0:n],
                                       start=(i == 0), stop=(i == len(SCORE_PRODUCTS) - 1))
                        if i == len(SCORE_PRODUCTS) - 1:
                            mm.then_inc(scored, 1)

                def weigh(b, slot, t, first=False):
                    n, g = FT[t][1], t // TG
                    pe.wait_ge(n_ready, NF * b + (t + 1))
                    if t % TG == 0:
                        pe.wait_ge(pT_ready, NSB * b + (g + 1))
                    if t == 0 and not first:
                        pe.wait_ge(gain_ready, b)
                    split_product(pe, ps[0:T, O0 + slot, :], pT_hi[0:n, g, t % TG, :], pT_lo[0:n, g, t % TG, :],
                                  n_hi[0:n, t % NATURAL_RING, :], n_lo[0:n, t % NATURAL_RING, :], t == 0, t == NF - 1).then_inc(weighed, 1)

                def batch(b, slot, first, last):
                    for t in range(NF):
                        f0, n = FT[t]
                        if not first or t >= 2:
                            pe.wait_ge(n_ready, NF * b + (t - 1))
                        for k in range(NK):
                            mm = pe.transpose(ps[0:n, N0 + t % 2, k * 128:(k + 1) * 128], feats[:, slot, k, f0:f0 + n],
                                              keep["ident"][:, :])
                        mm.then_inc(n_turned, 1)
                        if t in TURN_STEPS:
                            g = TURN_STEPS.index(t)
                            pe.wait_ge(exp_done, NSB * b + min(NSB, g + 1))
                            pe.wait_ge(pT_ready, NSB * b + g)
                            for i in range(TG):
                                g0, rows = FT[g * TG + i]
                                mm = pe.transpose(ps[0:rows, P_BANK, i * T:(i + 1) * T], p[:, g0:g0 + rows],
                                                  keep["ident"][0:T, 0:T])
                            mm.then_inc(p_turned, 1)
                        if t >= SCORES_AT and not last:
                            at = (t - SCORES_AT) * PER_STEP
                            c, start = at // len(SCORE_PRODUCTS), at % len(SCORE_PRODUCTS)
                            scores(b + 1, c, range(start, start + PER_STEP))
                        if t >= WEIGH_LAG:
                            weigh(b, slot, t - WEIGH_LAG, first)
                        elif not first:
                            weigh(b - 1, 1 - slot, NF - WEIGH_LAG + t)

                for c in range(NSB):
                    scores(0, c, range(len(SCORE_PRODUCTS)))
                run(pe, batch)
                for t in range(NF - WEIGH_LAG, NF):
                    weigh(B - 1, (B - 1) % 2, t)


FC = chunk_sizes(FF, 128)
NFC = len(FC)
W_RING, H_RING = 2, 3


def feed_forward(nc, whole, io, keep):
    with ExitStack() as ctx:
        def sb(name, shape, dt=F32):
            return ctx.enter_context(nc.sbuf_tensor("d_" + name, shape, dt))

        def sem(name):
            return whole.enter_context(nc.semaphore("d_" + name))

        x_rows = keep["x_rows"]
        x_nT = [sb(n, [128, NK, NTOK], F32R) for n in ("xnT_hi", "xnT_lo")]
        layer_norm_turned(nc, whole, "dn_", keep, x_nT)
        raw_in = sb("raw_in", [128, W_RING, 2, NK, 128])
        raw_down = sb("raw_down", [128, W_RING, D])
        win_hi, win_lo = (sb(n, [128, NFC, 2, NK, 128], F32R) for n in ("win_hi", "win_lo"))
        wd_hi, wd_lo = (sb(n, [128, NFC, D], F32R) for n in ("wd_hi", "wd_lo"))
        gate = sb("gate", [128, 2, HALF])
        h = sb("h", [128, 2, HALF])
        h_hi, h_lo = (sb(n, [128, H_RING, HALF], F32R) for n in ("h_hi", "h_lo"))
        yT = sb("yT", [128, NK, HALF])
        ps = ctx.enter_context(nc.psum_tensor("d_ps", [128, 8, BANK], F32))
        G0, Y0 = 0, 4

        loaded = [sem("in%d" % i) for i in range(W_RING)]
        w_hi_ready, w_ready, gu_done, gate_ready, h_ready, h_hi_ready, h_lo_ready, down_done = (
            sem(n) for n in ("w_hi", "w", "gu", "gate", "h", "h_hi", "h_lo", "down"))
        y_copied, y_turned, out_ready, stored = (sem(n) for n in ("y", "y_turned", "out_ready", "out"))

        with nc.Block() as block:
            @block.sync
            def _(sp):
                for f, (f0, n) in enumerate(FC):
                    slot = f % W_RING
                    if f >= W_RING:
                        sp.wait_ge(w_ready, 2 * (f - W_RING + 1))
                    for i, w in enumerate(("wgT", "wuT")):
                        sp.dma_start(raw_in[:, slot, i, :, 0:n], io[w][:, :, f0:f0 + n]).then_inc(loaded[slot], 16)
                    sp.dma_start(raw_down[0:n, slot, :], io["wdT"][f0:f0 + n, :]).then_inc(loaded[slot], 16)
                for b in range(B):
                    sp.wait_ge(out_ready, b + 1)
                    sp.dma_start(io["out4"][b], x_rows[:, b, :]).then_inc(stored, 16)
                sp.wait_ge(stored, 16 * B)

            @block.gpsimd
            def _(pool):
                for f, (f0, n) in enumerate(FC):
                    slot = f % W_RING
                    pool.wait_ge(w_hi_ready, 2 * f + 1)
                    nc.gpsimd.tensor_tensor(win_lo[:, f, :, :, 0:n], raw_in[:, slot, :, :, 0:n],
                                            win_hi[:, f, :, :, 0:n].bitcast(F32), ALU.subtract).then_inc(w_ready, 1)
                    pool.wait_ge(w_hi_ready, 2 * f + 2)
                    nc.gpsimd.tensor_tensor(wd_lo[0:n, f, :], raw_down[0:n, slot, :],
                                            wd_hi[0:n, f, :].bitcast(F32), ALU.subtract).then_inc(w_ready, 1)

            @block.scalar
            def _(act):
                def copy_half(half):
                    for d in range(NK):
                        act.wait_ge(down_done, NFC * (half + 1))
                        act.wait_ge(y_turned, half * (B // 2))
                        nc.scalar.activation(yT[:, d, :], ps[:, Y0 + d, 0:HALF], ACT.Copy).then_inc(y_copied, 1)

                for i in range(2 * NFC):
                    n = FC[i % NFC][1]
                    act.wait_ge(gu_done, i + 1)
                    if i >= 2:
                        act.wait_ge(h_ready, i - 1)
                    nc.scalar.activation(gate[0:n, i % 2, :], ps[0:n, G0 + 2 * (i % 2), 0:HALF], ACT.Silu).then_inc(gate_ready, 1)
                    act.wait_ge(h_ready, i + 1)
                    if i >= H_RING:
                        act.wait_ge(down_done, i - H_RING + 1)
                    nc.scalar.activation(h_hi[0:n, i % H_RING, :], h[0:n, i % 2, :], ACT.Copy).then_inc(h_hi_ready, 1)
                    if i == NFC:
                        copy_half(0)
                copy_half(1)

            @block.vector
            def _(dve):
                def round_weights(f):
                    n, slot = FC[f][1], f % W_RING
                    dve.wait_ge(loaded[slot], 48 * (f // W_RING + 1))
                    nc.vector.tensor_copy(win_hi[:, f, :, :, 0:n], raw_in[:, slot, :, :, 0:n]).then_inc(w_hi_ready, 1)
                    nc.vector.tensor_copy(wd_hi[0:n, f, :], raw_down[0:n, slot, :]).then_inc(w_hi_ready, 1)

                def add_half(half):
                    for b in range(half * (B // 2), (half + 1) * (B // 2)):
                        dve.wait_ge(y_turned, b + 1)
                        nc.vector.scalar_tensor_tensor(out=x_rows[:, b, :], in0=ps[0:T, G0 + b % 4, :], scalar=keep["tanh"][0:T, 3:4],
                                                       in1=x_rows[:, b, :], op0=ALU.mult, op1=ALU.add).then_inc(out_ready, 1)

                for f in range(W_RING):
                    round_weights(f)
                for i in range(2 * NFC):
                    n = FC[i % NFC][1]
                    dve.wait_ge(gate_ready, i + 1)
                    if i >= 2:
                        dve.wait_ge(h_lo_ready, i - 1)
                    nc.vector.tensor_tensor(h[0:n, i % 2, :], ps[0:n, G0 + 2 * (i % 2) + 1, 0:HALF], gate[0:n, i % 2, :],
                                            ALU.mult).then_inc(h_ready, 1)
                    dve.wait_ge(h_hi_ready, i + 1)
                    nc.vector.tensor_tensor(h_lo[0:n, i % H_RING, :], h[0:n, i % 2, :], h_hi[0:n, i % H_RING, :].bitcast(F32),
                                            ALU.subtract).then_inc(h_lo_ready, 1)
                    if i + W_RING < NFC:
                        round_weights(i + W_RING)
                    if i == NFC + 1:
                        add_half(0)
                add_half(1)

            @block.tensor
            def _(pe):
                def gate_up(i):
                    half, f, n = i // NFC, i % NFC, FC[i % NFC][1]
                    pe.wait_ge(w_ready, 2 * f + 2)
                    if i >= 2:
                        pe.wait_ge(h_ready, i - 1)
                    cols = slice(half * HALF, (half + 1) * HALF)
                    for j in range(2):
                        for k in range(NK):
                            mm = split_product(pe, ps[0:n, G0 + 2 * (i % 2) + j, 0:HALF], win_hi[:, f, j, k, 0:n], win_lo[:, f, j, k, 0:n],
                                               x_nT[0][:, k, cols], x_nT[1][:, k, cols], k == 0, k == NK - 1)
                    mm.then_inc(gu_done, 1)

                def down(i):
                    f, n = i % NFC, FC[i % NFC][1]
                    pe.wait_ge(h_lo_ready, i + 1)
                    for d in range(NK):
                        if i == NFC:
                            pe.wait_ge(y_copied, d + 1)
                        to = slice(d * 128, (d + 1) * 128)
                        mm = split_product(pe, ps[:, Y0 + d, 0:HALF], wd_hi[0:n, f, to], wd_lo[0:n, f, to],
                                           h_hi[0:n, i % H_RING, :], h_lo[0:n, i % H_RING, :], f == 0, f == NFC - 1)
                    mm.then_inc(down_done, 1)

                def turn_back(half):
                    for b in range(half * (B // 2), (half + 1) * (B // 2)):
                        i = b % (B // 2)
                        if i == 0:
                            pe.wait_ge(y_copied, NK * (half + 1))
                            pe.wait_ge(h_ready, NFC + 2 if half == 0 else 2 * NFC)
                        for d in range(NK):
                            mm = pe.transpose(ps[0:T, G0 + i, d * 128:(d + 1) * 128], yT[:, d, i * T:(i + 1) * T], keep["ident"][:, :])
                        mm.then_inc(y_turned, 1)

                for i in range(2 * NFC):
                    if i == NFC + 2:
                        turn_back(0)
                        pe.wait_ge(out_ready, B // 2)
                    gate_up(i)
                    if i:
                        down(i - 1)
                down(2 * NFC - 1)
                turn_back(1)


def flamingo(nc, a, out):
    with ExitStack() as whole:
        def dram(name, shape, dt=F32):
            return nc.dram_tensor(name, shape, dt, kind="Internal").ap()

        def keep_sb(stack, name, shape, dt=F32):
            keep[name] = stack.enter_context(nc.sbuf_tensor("keep_" + name, shape, dt))

        latT = dram("latT_scratch", [128, NK, NTOK])
        q_hi, q_lo = (dram(n, [HD, B, H, T]) for n in ("q_hi_scratch", "q_lo_scratch"))
        x1 = dram("x1_scratch", [NTOK, D])
        io = dict(a)
        io.update(
            latT=latT, latT4=latT.rearrange("p k (b t) -> b p k t", t=T),
            q_hi=q_hi, q_lo=q_lo, q_hi4=q_hi.rearrange("d b h t -> b d h t"), q_lo4=q_lo.rearrange("d b h t -> b d h t"),
            x4=a["x"].rearrange("(b t) d -> b t d", t=T), x1_4=x1.rearrange("(b t) d -> b t d", t=T),
            out4=out.rearrange("(b t) d -> b t d", t=T))
        keep = {}
        for n, s in (("ident", [128, 128]), ("gates", [128, 8]), ("tanh", [128, 4]), ("sigmoid", [128, 2])):
            keep_sb(whole, n, s)
        with ExitStack() as early:
            for n in ("wk_hi", "wk_lo", "wv_hi", "wv_lo"):
                keep_sb(early, n, [128, NK, KV * HD], F32R)
            project_queries(nc, whole, io, keep)
            attend_context(nc, whole, io, keep)
        keep_sb(whole, "x_rows", [T, B, D])
        with ExitStack() as late:
            for n in ("bq1", "bk1"):
                keep_sb(late, n, [128, NK])
            keep_sb(late, "queries", [128, NK, NTOK])
            keep_sb(late, "qbk", [T, B])
            with ExitStack() as weights:
                for n in ("wq1_hi", "wq1_lo", "wk1_hi", "wk1_lo"):
                    keep_sb(weights, n, [128, NK, D], F32R)
                hyper_connection(nc, whole, io, keep)
                project_features(nc, whole, io, keep)
            attend_features(nc, whole, io, keep)
        feed_forward(nc, whole, io, keep)


def kernel(x, ctx_4096, g_xattn, g_ffn, L0_xattn_Wq, L0_xattn_Wk, L0_xattn_Wv, L0_xattn_Wo, L0_ffn_W_res,
           L0_ffn_W_pre, L0_ffn_W_post, L0_ffn_H_res_base, L0_ffn_H_pre_base, L0_ffn_H_post_base, L0_ffn_gate,
           L0_ffn_W_branch, L1_xattn_Wq, L1_xattn_bq, L1_xattn_Wk, L1_xattn_bk, L1_ffn_W_gate, L1_ffn_W_up,
           L1_ffn_W_down):
    import numpy as np
    import concourse.bacc as bacc
    from concourse.bass_utils import run_bass_kernel_spmd

    def by_k(w):
        w = np.asarray(w)
        return np.ascontiguousarray(w.T.reshape(w.shape[1] // 128, 128, w.shape[0]).transpose(1, 0, 2))

    def column(v):
        return np.ascontiguousarray(np.asarray(v).reshape(-1, 128).T)

    flat = [np.asarray(v).reshape(-1) for v in (g_xattn, g_ffn, L0_ffn_gate)]
    arrays = {
        "x": np.asarray(x).reshape(NTOK, D),
        "ctxT": np.ascontiguousarray(np.asarray(ctx_4096).transpose(0, 2, 1).reshape(B, NK, 128, CTX).transpose(0, 2, 1, 3)),
        "gates": np.concatenate(flat).reshape(1, 5),
        "wqT": by_k(L0_xattn_Wq), "wkT": by_k(L0_xattn_Wk), "wvT": by_k(L0_xattn_Wv),
        "woT": np.ascontiguousarray(np.asarray(L0_xattn_Wo).T.reshape(H, HD, D).transpose(1, 0, 2)),
        "whT": by_k(np.concatenate([np.asarray(w) for w in (L0_ffn_W_res, L0_ffn_W_pre, L0_ffn_W_post)])),
        "h_base": np.concatenate([np.asarray(v).reshape(-1) for v in
                                  (L0_ffn_H_res_base, L0_ffn_H_pre_base, L0_ffn_H_post_base)]).reshape(1, 24),
        "w_branch": np.asarray(L0_ffn_W_branch),
        "wq1T": by_k(L1_xattn_Wq), "wk1": np.ascontiguousarray(np.asarray(L1_xattn_Wk).reshape(NK, 128, D).transpose(1, 0, 2)),
        "bq1": column(L1_xattn_bq), "bk1": column(L1_xattn_bk),
        "wgT": by_k(L1_ffn_W_gate), "wuT": by_k(L1_ffn_W_up),
        "wdT": np.ascontiguousarray(np.asarray(L1_ffn_W_down).T),
    }
    nc = bacc.Bacc("TRN2", target_bir_lowering=False, num_devices=1)
    maps, aps = {}, {}
    for name, a in arrays.items():
        maps[f"in_{name}"] = a
        aps[name] = nc.dram_tensor(f"in_{name}", a.shape, mybir.dt.from_np(a.dtype), kind="ExternalInput").ap()
    out = nc.dram_tensor("out_0", (NTOK, D), F32, kind="ExternalOutput").ap()
    flamingo(nc, aps, out)
    r = run_bass_kernel_spmd(nc, [maps], core_ids=[0])
    return r.results[0]["out_0"].reshape(B, T, D)
```

```python
from contextlib import ExitStack

import concourse.bass as bass
from concourse import mybir

ALU = mybir.AluOpType
ACT = mybir.ActivationFunctionType
AX = mybir.AxisListType
F32 = mybir.dt.float32
F32R = mybir.dt.float32r

B, T, D, CTX = 8, 100, 512, 1444
H, KV, HD = 16, 4, 96
G = H // KV
STREAMS, SW = 4, 128
SINKHORN_STEPS, TAU = 50, 0.1
RMS_EPS, LN_EPS = 1.1920929e-07, 1e-05
FF = 1376
NTOK = B * T
NK = D // 128
HALF = NTOK // 2
BANK = 512


def split_product(pe, out, a_hi, a_lo, b_hi, b_lo, start, stop):
    pe.matmul(out, a_hi, b_hi, start=start, stop=False)
    pe.matmul(out, a_hi, b_lo, start=False, stop=False)
    return pe.matmul(out, a_lo, b_hi, start=False, stop=stop)


def chunk_sizes(n, size):
    return [(i, min(size, n - i)) for i in range(0, n, size)]


def layer_norm_stats(nc, dve, link, stats, mv, var, x_of, loaded, eps):
    for b in range(B):
        dve.wait_ge(loaded, 16 * (b + 1))
        link(nc.vector.bn_stats(stats[:, b, :], x_of(b)))
        link(nc.vector.bn_aggr(mv[:, b, :], stats[:, b, :]))
    return link(nc.vector.tensor_scalar(var, mv[:, :, 1], eps, None, ALU.add))


def refined_rsqrt(nc, link, rstd, sd, var, tmp):
    link(nc.vector.reciprocal(rstd, sd))
    link(nc.vector.tensor_tensor(tmp, rstd, rstd, ALU.mult))
    link(nc.vector.tensor_tensor(tmp, tmp, var, ALU.mult))
    link(nc.vector.tensor_scalar(tmp, tmp, -0.5, 1.5, ALU.mult, ALU.add))
    link(nc.vector.tensor_tensor(rstd, rstd, tmp, ALU.mult))


NKEY = CTX + T
KEY_TILES = [(128 * i, 128) for i in range(11)] + [(1408, 68), (1476, 68)]
NT = len(KEY_TILES)
CHUNKS = [(256 * c, 256, 2 * c, 2) for c in range(5)] + [(1280, 264, 10, 3)]
NCH = len(CHUNKS)
CHUNK_MAX = max(n for _, n, _, _ in CHUNKS)
KG = KV - 1
GROUP_OF = [(c, i) for c in range(NCH) for i in range(KG + CHUNKS[c][3])]
GROUPS = len(GROUP_OF)
FIRST_GROUP = [GROUP_OF.index((c, 0)) for c in range(NCH)] + [GROUPS]
PIECES_BEFORE = [sum(2 if i < KG else 1 for _, i in GROUP_OF[:g]) for g in range(GROUPS + 1)]
PIECES = PIECES_BEFORE[GROUPS]
MAXIMA = NCH * H
STEPS = KV * NT
RING = 3
LAG = 3
TURN_AT, SPREAD_AT, OUT_AT, MAX_ROW_AT = 5, 7, 9, 11
NEGATE_AT = 9
END_TURN, END_SPREAD, END_OUT = 1, 2, 4
ROUGH_AT = {(1, 1): (0,), (1, 2): (1,), (1, 3): (2,), (2, 1): (3,), (2, 2): (4,), (2, 3): (5,), (3, 0): (6,), (3, 1): (7,),
            (3, 2): (8, 9), (3, 3): (10,), (4, 0): (11,), (4, 1): (12,), (4, 2): (13, 14), (4, 3): (15,)}
ROUND_AFTER = {FIRST_GROUP[c + 1] - 1: c + 2 for c in range(NCH - 2)}
AHEAD = (6, 14)
HY_RESIDUAL, HY_STATS, HY_RSTD, HY_NORM, HY_TURN, HY_COPY, HY_LOGITS, HY_MEAN, HY_YN, HY_RSTD2, HY_LOGIT_ROWS = (
    5, 9, 10, 14, 17, 18, 19, 20, 20, 21, 24)
OP_STATS, OP_NEWTON, OP_NEWTON2, HYPER_OPS = 0, 2, 6, 10
EARLY = B - 2
SK_ROWS, SK_EXP, SK_SUMS, SK_LN, SK_COLS, SK_EXP2, SK_START = 25, 26, 27, 28, 29, 30, 31
NORMS = 1 + 2 * (SINKHORN_STEPS - 1)
IN_GROUPS = (GROUPS - SK_START) + GROUPS
IN_TILES = NORMS - IN_GROUPS
TILE_SLOTS = [i * (2 * STEPS - 4) // IN_TILES for i in range(IN_TILES)]
SK_SLOTS = ([("group", B - 2, gi) for gi in range(SK_START, GROUPS)] + [("tile", B - 2, s) for s in TILE_SLOTS if s < STEPS]
            + [("group", B - 1, gi) for gi in range(GROUPS)] + [("tile", B - 1, s - STEPS) for s in TILE_SLOTS if s >= STEPS])
assert len(SK_SLOTS) == NORMS
assert sum(n for _, n in KEY_TILES) == NKEY


def load_chunk(sp, io, keep, b, c):
    k0, n, _, _ = CHUNKS[c]
    own = min(n, CTX - k0)
    if not (isinstance(b, int) and b + c == 0):
        sp.wait_ge(keep["chunk_ready"], NCH * b + c)
    sp.dma_start(keep["raw"][:, :, 0:own], io["ctxT"][b, :, :, k0:k0 + own]).then_inc(keep["raw_loaded"], 16)
    if own < n:
        sp.dma_start(keep["raw"][:, :, own:n], io["latT4"][b]).then_inc(keep["raw_loaded"], 16)


def round_chunk(nc, dve, keep, b, c):
    loads = NCH + 1
    n, slot = CHUNKS[c][1], c % 2
    dve.wait_ge(keep["raw_loaded"], 16 * loads * b + 16 * (loads if c == NCH - 1 else c + 1))
    nc.vector.tensor_copy(keep["c_hi"][:, slot, :, 0:n], keep["raw"][:, :, 0:n]).then_inc(keep["chunk_hi"], 1)


def split_chunk(nc, pool, keep, b, c):
    n, slot = CHUNKS[c][1], c % 2
    pool.wait_ge(keep["chunk_hi"], NCH * b + (c + 1))
    nc.gpsimd.tensor_tensor(keep["c_lo"][:, slot, :, 0:n], keep["raw"][:, :, 0:n],
                            keep["c_hi"][:, slot, :, 0:n].bitcast(F32), ALU.subtract).then_inc(keep["chunk_ready"], 1)

SK_SEMS = ("chain", "z", "kept", "e", "sums", "ln", "m", "e2", "pairs", "marginal", "inverse", "norm")
SK_LINKS = 7


class Sinkhorn:

    def __init__(self, keep, turn, first, last):
        part, n = slice(first, last), last - first
        self.n, self.tanh = n, keep["tanh"][0:T, 2:3]
        self.z = keep["logits"][:, first * 24:last * 24].rearrange("p (b i j) -> p b i j", i=6, j=4)
        self.zf = keep["logits"][:, first * 24:last * 24].rearrange("p (b n) -> p b n", n=24)
        self.row_max, self.row_sum, self.row_ln = (keep[k][:, part, :] for k in ("row_max", "row_sum", "row_ln"))
        self.h_pp, self.log_res, self.sink = (keep[k][:, part, :, :] for k in ("h_pp", "log_res", "sink"))
        self.pairs, self.marginal, self.inverse = (keep[k][:, part, :] for k in ("pairs", "marginal", "inverse"))
        (self.chain, self.z_ready, self.kept, self.e_ready, self.sums_ready, self.ln_ready, self.m_ready, self.e2_ready,
         self.pairs_ready, self.marginal_ready, self.inverse_ready, self.norm_done) = keep["sinkhorn_sems"]
        self.turn, self.links = turn, SK_LINKS * turn

    def link(self, dve, ins):
        self.links += 1
        ins.then_inc(self.chain, 1)
        dve.wait_ge(self.chain, self.links)

    def along_rows(self, v):
        return v.unsqueeze(3).to_broadcast([T, self.n, v.shape[2], 4])

    def along_cols(self, v):
        return v.unsqueeze(2).to_broadcast([T, self.n, 4, 4])

    def softmax_rows(self, nc, dve, at):
        if at == SK_ROWS:
            self.link(dve, nc.vector.tensor_scalar(self.zf[:, :, 0:16], self.zf[:, :, 0:16], 1.0 / TAU, None, ALU.mult))
            self.link(dve, nc.vector.tensor_reduce(self.row_max, self.z, AX.X, ALU.max))
            nc.vector.tensor_tensor(self.z, self.z, self.along_rows(self.row_max), ALU.subtract).then_inc(self.z_ready, 1)
            dve.wait_ge(self.z_ready, self.turn + 1)
            nc.vector.tensor_copy(self.log_res, self.z[:, :, 0:4, :]).then_inc(self.kept, 1)
        if at == SK_SUMS:
            dve.wait_ge(self.e_ready, self.turn + 1)
            nc.vector.tensor_reduce(self.row_sum, self.z, AX.X, ALU.add).then_inc(self.sums_ready, 1)
            dve.wait_ge(self.sums_ready, self.turn + 1)
            self.link(dve, nc.vector.reciprocal(self.row_max[:, :, 4:6], self.row_sum[:, :, 4:6]))
            self.link(dve, nc.vector.tensor_tensor(self.h_pp, self.z[:, :, 4:6, :], self.along_rows(self.row_max[:, :, 4:6]), ALU.mult))
            self.link(dve, nc.vector.tensor_scalar(self.h_pp[:, :, 1, :], self.h_pp[:, :, 1, :], self.tanh, None, ALU.mult))
        if at == SK_COLS:
            dve.wait_ge(self.ln_ready, self.turn + 1)
            self.link(dve, nc.vector.tensor_tensor(self.log_res, self.log_res, self.along_rows(self.row_ln), ALU.subtract))
            self.link(dve, nc.vector.tensor_reduce(self.marginal, self.log_res.rearrange("p b i j -> p b j i"), AX.X, ALU.max))
            nc.vector.tensor_tensor(self.log_res, self.log_res, self.along_cols(self.marginal), ALU.subtract).then_inc(self.m_ready, 1)

    def exponentials(self, nc, act, at):
        if at == SK_EXP:
            act.wait_ge(self.kept, self.turn + 1)
            nc.scalar.activation(self.z, self.z, ACT.Exp).then_inc(self.e_ready, 1)
        if at == SK_LN:
            act.wait_ge(self.sums_ready, self.turn + 1)
            nc.scalar.activation(self.row_ln, self.row_sum[:, :, 0:4], ACT.Ln).then_inc(self.ln_ready, 1)
        if at == SK_EXP2:
            act.wait_ge(self.m_ready, self.turn + 1)
            nc.scalar.activation(self.sink, self.log_res, ACT.Exp).then_inc(self.e2_ready, 1)

    def normalise(self, nc, pool, n):
        if n == 0:
            pool.wait_ge(self.e2_ready, self.turn + 1)
        else:
            pool.wait_ge(self.norm_done, n)
        if n % 2 == 0:
            halves = self.sink[:, :, 0:2, :], self.sink[:, :, 2:4, :]
            pairs = self.pairs.rearrange("p b (i j) -> p b i j", j=4)
            ends, inverses = (pairs[:, :, 0, :], pairs[:, :, 1, :]), self.along_cols(self.inverse)
        else:
            halves = self.sink[:, :, :, 0:2], self.sink[:, :, :, 2:4]
            pairs = self.pairs.rearrange("p b (i j) -> p b i j", j=2)
            ends, inverses = (pairs[:, :, :, 0], pairs[:, :, :, 1]), self.along_rows(self.inverse)
        nc.gpsimd.tensor_tensor(pairs, halves[0], halves[1], ALU.add).then_inc(self.pairs_ready, 1)
        pool.wait_ge(self.pairs_ready, n + 1)
        nc.gpsimd.tensor_tensor(self.marginal, ends[0], ends[1], ALU.add).then_inc(self.marginal_ready, 1)
        pool.wait_ge(self.inverse_ready, n + 1)
        nc.gpsimd.tensor_tensor(self.sink, self.sink, inverses, ALU.mult).then_inc(self.norm_done, 1)

    def invert(self, nc, dve, n):
        dve.wait_ge(self.marginal_ready, n + 1)
        nc.vector.reciprocal(self.inverse, self.marginal).then_inc(self.inverse_ready, 1)


def project_queries(nc, whole, io, keep):
    with ExitStack() as ctx:
        def sb(name, shape, dt=F32):
            return ctx.enter_context(nc.sbuf_tensor(name, shape, dt))

        def sem(name):
            return whole.enter_context(nc.semaphore(name))

        x_rows = sb("q_x", [T, B, D])
        xnT = sb("q_xnT", [128, NK, NTOK])
        xnT_hi = sb("q_xnT_hi", [128, NK, NTOK], F32R)
        xnT_lo = sb("q_xnT_lo", [128, NK, NTOK], F32R)
        wq = sb("q_wq", [128, NK, H * HD])
        wq_hi = sb("q_wq_hi", [128, NK, H * HD], F32R)
        wq_lo = sb("q_wq_lo", [128, NK, H * HD], F32R)
        wkv = sb("q_wkv", [128, 2, NK, KV * HD])
        QR = 4
        q_hi = sb("q_q_hi", [HD, QR, HALF], F32R)
        q_lo = sb("q_q_lo", [HD, QR, HALF], F32R)
        stats = sb("q_stats", [T, B, 6])
        mv = sb("q_mv", [T, B, 2])
        var, sd, rstd, tmp = (sb("q_" + n, [T, B]) for n in ("var", "sd", "rstd", "tmp"))
        ps = ctx.enter_context(nc.psum_tensor("q_ps", [128, 8, BANK], F32))

        x_loaded = [sem("q_x_in%d" % i) for i in range(2)]
        wq_loaded = [sem("q_wq_in%d" % k) for k in range(NK)]
        wkv_loaded, small_loaded = sem("q_wkv_in"), sem("q_small_in")
        step, var_ready, sd_ready, xn_ready = (sem("q_" + n) for n in ("step", "var", "sd", "xn"))
        ident_ready, turned, xnT_ready, xnT_hi_ready, xnT_lo_ready = (
            sem("q_" + n) for n in ("ident", "turned", "xnT", "xnT_hi", "xnT_lo"))
        stats_ready, aggregated = sem("q_stats"), sem("q_aggr")
        wq_hi_ready, wkv_hi_ready, wkv_lo_ready = (sem("q_" + n) for n in ("wqh", "wkvh", "wkvl"))
        wq_lo_ready = [sem("q_wql%d" % i) for i in range(2)]
        q_done, q_hi_ready, q_lo_ready, lat_stored, gate_ready = (
            sem("q_" + n) for n in ("done", "qh", "ql", "lat", "gate"))
        q_stored = [sem(f"q_stored{i}") for i in range(QR)]

        with nc.Block() as block:
            @block.sync
            def _(sp):
                for i in range(2):
                    part = slice(i * (B // 2), (i + 1) * (B // 2))
                    sp.dma_start(x_rows[:, part, :], io["x4"][part].rearrange("b t d -> t b d")).then_inc(x_loaded[i], 16)
                for k in range(NK):
                    sp.dma_start(wq[:, k, :], io["wqT"][:, k, :]).then_inc(wq_loaded[k], 16)
                load_chunk(sp, io, keep, 0, 0)
                sp.dma_start(wkv[:, 0, :, :], io["wkT"]).then_inc(wkv_loaded, 16)
                sp.dma_start(wkv[:, 1, :, :], io["wvT"]).then_inc(wkv_loaded, 16)
                sp.wait_ge(xnT_ready, B)
                sp.dma_start(io["latT"], xnT[:, :, :]).then_inc(lat_stored, 16)
                for i in range(2 * H):
                    h, half, slot = i // 2, i % 2, i % QR
                    if i == H:
                        load_chunk(sp, io, keep, 0, 1)
                    sp.wait_ge(q_lo_ready, i + 1)
                    for q, to in ((q_hi, io["q_hi"]), (q_lo, io["q_lo"])):
                        sp.dma_start(to[:, half * (B // 2):(half + 1) * (B // 2), h, :],
                                     q[:, slot, :].bitcast(F32).rearrange("d (b t) -> d b t", t=T)).then_inc(q_stored[slot], 16)
                sp.wait_ge(small_loaded, 16)
                sp.wait_ge(lat_stored, 16)
                for i in range(QR):
                    sp.wait_ge(q_stored[i], 32 * (2 * H // QR))

            @block.gpsimd
            def _(pool):
                nc.gpsimd.memset(keep["ident"][:, :], 0.0).then_inc(ident_ready, 1)
                pool.wait_ge(ident_ready, 1)
                nc.gpsimd.affine_select(out=keep["ident"][:, :], in_=keep["ident"][:, :], compare_op=ALU.not_equal,
                                        fill=1.0, base=0, pattern=[[-1, 128]], channel_multiplier=1).then_inc(ident_ready, 1)
                for k in (0, 2):
                    pool.wait_ge(wq_hi_ready, k + 1)
                    nc.gpsimd.tensor_tensor(wq_lo[:, k, :], wq[:, k, :], wq_hi[:, k, :].bitcast(F32),
                                            ALU.subtract).then_inc(wq_lo_ready[0], 1)
                pool.wait_ge(wkv_loaded, 32)
                for i, name in enumerate(("wk", "wv")):
                    nc.gpsimd.tensor_copy(keep[name + "_hi"][:, :, :], wkv[:, i, :, :]).then_inc(wkv_hi_ready, 1)
                    pool.wait_ge(wkv_hi_ready, i + 1)
                    nc.gpsimd.tensor_tensor(keep[name + "_lo"][:, :, :], wkv[:, i, :, :],
                                            keep[name + "_hi"][:, :, :].bitcast(F32), ALU.subtract).then_inc(wkv_lo_ready, 1)
                    split_chunk(nc, pool, keep, 0, i)

            @block.scalar
            def _(act):
                act.dma_start(keep["gates"][:, 0:5], io["gates"].partition_broadcast(128)).then_inc(small_loaded, 16)
                def root(i):
                    part = slice(i * (B // 2), (i + 1) * (B // 2))
                    act.wait_ge(var_ready, i + 1)
                    nc.scalar.activation(sd[:, part], var[:, part], ACT.Sqrt).then_inc(sd_ready, 1)

                root(0)
                for k in range(NK):
                    act.wait_ge(wq_loaded[k], 16)
                    nc.scalar.activation(wq_hi[:, k, :], wq[:, k, :], ACT.Copy).then_inc(wq_hi_ready, 1)
                    if k == 0:
                        root(1)
                for b in range(B):
                    act.wait_ge(turned, b + 1)
                    nc.scalar.activation(xnT[:, :, b * T:(b + 1) * T],
                                         ps[:, b % 2, 0:NK * T].rearrange("p (k t) -> p k t", t=T),
                                         ACT.Copy).then_inc(xnT_ready, 1)
                act.wait_ge(small_loaded, 16)
                nc.scalar.activation(keep["tanh"][:, 0:4], keep["gates"][:, 0:4], ACT.Tanh).then_inc(gate_ready, 1)
                nc.scalar.activation(keep["gates"][:, 5:6], keep["gates"][:, 4:5], ACT.Exp, scale=-1.0).then_inc(gate_ready, 1)
                for i in range(2 * H):
                    act.wait_ge(q_done, i + 1)
                    if i >= QR:
                        act.wait_ge(q_stored[i % QR], 32 * (i // QR))
                    nc.scalar.activation(q_hi[:, i % QR, :], ps[0:HD, 2 + i % 4, 0:HALF], ACT.Copy).then_inc(q_hi_ready, 1)

            @block.vector
            def _(dve):
                done = [0]

                def link(ins):
                    done[0] += 1
                    ins.then_inc(step, 1)
                    dve.wait_ge(step, done[0])

                def split_latents(batches):
                    for b in batches:
                        cols = slice(b * T, (b + 1) * T)
                        dve.wait_ge(xnT_ready, b + 1)
                        nc.vector.tensor_copy(xnT_hi[:, :, cols], xnT[:, :, cols]).then_inc(xnT_hi_ready, 1)
                        dve.wait_ge(xnT_hi_ready, b + 1)
                        nc.vector.tensor_tensor(xnT_lo[:, :, cols], xnT[:, :, cols], xnT_hi[:, :, cols].bitcast(F32),
                                                ALU.subtract).then_inc(xnT_lo_ready, 1)

                for i in range(2):
                    part = slice(i * (B // 2), (i + 1) * (B // 2))
                    dve.wait_ge(x_loaded[i], 16)
                    for b in range(part.start, part.stop):
                        nc.vector.bn_stats(stats[:, b, :], x_rows[:, b, :]).then_inc(stats_ready, 1)
                    for b in range(part.start, part.stop):
                        dve.wait_ge(stats_ready, b + 1)
                        nc.vector.bn_aggr(mv[:, b, :], stats[:, b, :]).then_inc(aggregated, 1)
                    dve.wait_ge(aggregated, part.stop)
                    nc.vector.tensor_scalar(var[:, part], mv[:, part, 1], LN_EPS, None, ALU.add).then_inc(var_ready, 1)
                    dve.wait_ge(var_ready, i + 1)
                    dve.wait_ge(sd_ready, i + 1)
                    refined_rsqrt(nc, link, rstd[:, part], sd[:, part], var[:, part], tmp[:, part])
                    for b in range(part.start, part.stop):
                        nc.vector.tensor_scalar(x_rows[:, b, :], x_rows[:, b, :], mv[:, b, 0:1], rstd[:, b:b + 1],
                                                ALU.subtract, ALU.mult).then_inc(xn_ready, 1)
                for k in (1, 3):
                    dve.wait_ge(wq_hi_ready, k + 1)
                    nc.vector.tensor_tensor(wq_lo[:, k, :], wq[:, k, :], wq_hi[:, k, :].bitcast(F32),
                                            ALU.subtract).then_inc(wq_lo_ready[1], 1)
                split_latents(range(B))
                dve.wait_ge(gate_ready, 2)
                link(nc.vector.tensor_scalar(keep["gates"][:, 6:7], keep["gates"][:, 5:6], 1.0, None, ALU.add))
                link(nc.vector.reciprocal(keep["sigmoid"][:, 0:1], keep["gates"][:, 6:7]))
                link(nc.vector.tensor_scalar(keep["sigmoid"][:, 1:2], keep["sigmoid"][:, 0:1], -1.0, 1.0, ALU.mult, ALU.add))
                for i in range(2 * H):
                    if i in (H // 2, H):
                        round_chunk(nc, dve, keep, 0, 0 if i < H else 1)
                    dve.wait_ge(q_hi_ready, i + 1)
                    nc.vector.tensor_tensor(q_lo[:, i % QR, :], ps[0:HD, 2 + i % 4, 0:HALF],
                                            q_hi[:, i % QR, :].bitcast(F32), ALU.subtract).then_inc(q_lo_ready, 1)

            @block.tensor
            def _(pe):
                pe.wait_ge(ident_ready, 2)
                for b in range(B):
                    pe.wait_ge(xn_ready, b + 1)
                    if b >= 2:
                        pe.wait_ge(xnT_ready, b - 1)
                    for k in range(NK):
                        mm = pe.transpose(ps[:, b % 2, k * T:(k + 1) * T], x_rows[:, b, k * 128:(k + 1) * 128],
                                          keep["ident"][0:T, 0:T])
                    mm.then_inc(turned, 1)
                for i in range(2):
                    pe.wait_ge(wq_lo_ready[i], NK // 2)
                for i in range(2 * H):
                    h, half = i // 2, i % 2
                    pe.wait_ge(xnT_lo_ready, (half + 1) * (B // 2) if i < 2 else B)
                    if i >= 4:
                        pe.wait_ge(q_lo_ready, i - 3)
                    for k in range(NK):
                        w, t = slice(h * HD, (h + 1) * HD), slice(half * HALF, (half + 1) * HALF)
                        mm = split_product(pe, ps[0:HD, 2 + i % 4, 0:HALF], wq_hi[:, k, w], wq_lo[:, k, w],
                                           xnT_hi[:, k, t], xnT_lo[:, k, t], k == 0, k == NK - 1)
                    mm.then_inc(q_done, 1)


def attend_context(nc, whole, io, keep):
    scale = float(HD) ** -0.5
    with ExitStack() as ctx:
        def sb(name, shape, dt=F32):
            return ctx.enter_context(nc.sbuf_tensor(name, shape, dt))

        def sem(name):
            return whole.enter_context(nc.semaphore("a_" + name))

        c_hi, c_lo = keep["c_hi"], keep["c_lo"]
        k_hi = sb("a_k_hi", [HD + 1, KV, NKEY], F32R)
        k_lo = sb("a_k_lo", [HD + 1, KV, NKEY], F32R)
        v_hi = sb("a_v_hi", [128, NT, KV, HD + 1], F32R)
        v_lo = sb("a_v_lo", [128, NT, KV, HD + 1], F32R)
        q_hi = sb("a_q_hi", [HD + 1, H, T], F32R)
        q_lo = sb("a_q_lo", [HD + 1, H, T], F32R)
        p = sb("a_p", [128, 2, G * T])
        p_hi = sb("a_p_hi", [128, RING, G * T], F32R)
        p_lo = sb("a_p_lo", [128, RING, G * T], F32R)
        maxima = sb("a_max", [T, H, NCH])
        head_max = sb("a_hmax", [T, G])
        neg_max = sb("a_nmax", [T, G, HD + 1])
        ones = sb("a_ones", [128, HD])
        recip = sb("a_recip", [T, G])
        diag = sb("a_diag", [T, G, T])
        o_sb = sb("a_o", [HD + 1, G * T])
        x_rows = sb("a_x", [T, D])
        xn = sb("h_xn", [T, D])
        xnT = sb("h_xnT", [128, NK, T])
        yn = sb("h_yn", [T, STREAMS, SW])
        w_h = sb("h_w", [128, NK, 24])
        w_branch = sb("h_wb", [SW, SW])
        h_base = sb("h_base", [T, 24])
        stats, mv = sb("h_stats", [T, 6]), sb("h_mv", [T, 2])
        var, root, newton_t, rstd, square_sum, mean_sq, rstd2 = (sb("h_s%d" % i, [T, 1]) for i in range(7))
        wo = sb("a_wo", [HD, H, D])
        ps = ctx.enter_context(nc.psum_tensor("a_ps", [128, 8, BANK], F32))
        S0, M0, O_BANK, B_BANK, Y_BANK = 0, 3, 5, 6, 7
        LOGITS = G * T + 8

        chunk_ready = keep["chunk_ready"]
        preset, pool_preset, wo_loaded = (sem(n) for n in ("preset", "pool_preset", "wo_in"))
        q_loaded, q_last_loaded, x_loaded, x1_ready, stored = (sem(n) for n in ("q_in", "q_last_in", "x_in", "x1", "stored"))
        proj_done, proj_hi, proj_lo = sem("proj"), sem("proj_hi"), sem("proj_lo")
        rough_done, rough_max, max_ready, neg_ready, row_placed, row_ready = (
            sem(n) for n in ("rough", "rough_max", "max", "neg", "row_placed", "row"))
        scores, exp_done, p_hi_ready, p_lo_ready, pv_done = (sem(n) for n in ("scores", "exp", "p_hi", "p_lo", "pv"))
        o_copied, sums_turned, recip_ready, diag_ready, spread, normal, wo_done = (
            sem(n) for n in ("o_copied", "turned", "recip", "diag", "spread", "normal", "wo"))

        weights_in, hyper, settled, var_ready, root_ready, xn_ready, x_turned, xnT_ready, square_ready = (
            sem("h_" + n) for n in ("w_in", "ops", "settled", "var", "root", "xn", "xturn", "xnT", "sq"))
        mean_ready, root2_ready, logits_done, branch_done, yn_ready, logit_rows_ready = (
            sem("h_" + n) for n in ("mean", "root2", "logits", "branch", "yn", "z"))
        sk = Sinkhorn(keep, 0, 0, EARLY)

        def o_bank(kv):
            return O_BANK if kv % 2 else M0 + 1

        def group_pieces(gi):
            c, i = GROUP_OF[gi]
            k0, n, t0, _ = CHUNKS[c]
            bank = ps[:, M0 + gi % 2, :]
            if i < KG:
                keys, last = slice(k0, k0 + n), slice(32 * i, 32 * (i + 1))
                return [(bank[0:HD, 0:n], k_hi[0:HD, i, keys], k_lo[0:HD, i, keys]),
                        (bank[HD:128, 0:n], k_hi[last, KV - 1, keys], k_lo[last, KV - 1, keys])]
            t = t0 + i - KG
            rows = KEY_TILES[t][1]
            return [(bank[0:rows, 0:KV * HD].rearrange("p (h d) -> p h d", d=HD), v_hi[0:rows, t, :, 0:HD], v_lo[0:rows, t, :, 0:HD])]

        with nc.Block() as block:
            @block.sync
            def _(sp):
                def load_queries(b, first=False):
                    for heads, loaded, after in ((slice(0, H - G), q_loaded, STEPS * b - NT), (slice(H - G, H), q_last_loaded, STEPS * b)):
                        if not first:
                            sp.wait_ge(scores, after)
                        for q, name in ((q_hi, "q_hi4"), (q_lo, "q_lo4")):
                            sp.dma_start(q[0:HD, heads, :].bitcast(F32), io[name][b, :, heads, :]).then_inc(loaded, 16)

                def store(b, ready, what, to):
                    sp.wait_ge(ready, b + 1)
                    sp.dma_start(to[b], what).then_inc(stored, 16)

                def batch(b, first, last):
                    load_chunk(sp, io, keep, b, 2)
                    if not first:
                        store(b - 1, x1_ready, x_rows[:, :], io["x1_4"])
                    load_chunk(sp, io, keep, b, 3)
                    load_chunk(sp, io, keep, b, 4)
                    if not first:
                        store(b - 1, xn_ready, xn[:, :], io["xn_4"])
                    load_chunk(sp, io, keep, b, NCH - 1)
                    if not first:
                        store(b - 1, yn_ready, yn[:, :, :].rearrange("p n c -> p (n c)"), io["yn_4"])
                        sp.wait_ge(stored, 48 * b)
                    sp.dma_start(x_rows[:, :], io["x4"][b]).then_inc(x_loaded, 16)
                    if first:
                        sp.dma_start(wo[:, :, :], io["woT"]).then_inc(wo_loaded, 16)
                        sp.dma_start(w_h[:, :, :], io["whT"]).then_inc(weights_in, 16)
                        sp.dma_start(w_branch[:, :], io["w_branch"]).then_inc(weights_in, 16)
                        sp.dma_start(h_base[:, :], io["h_base"].partition_broadcast(T)).then_inc(weights_in, 16)
                    if not last:
                        load_chunk(sp, io, keep, b + 1, 0)
                        load_chunk(sp, io, keep, b + 1, 1)
                        load_queries(b + 1)

                load_queries(0, True)
                batch(0, True, False)
                with sp.Fori(1, B - 1) as b:
                    batch(b, False, False)
                batch(B - 1, False, True)
                store(B - 1, x1_ready, x_rows[:, :], io["x1_4"])
                store(B - 1, xn_ready, xn[:, :], io["xn_4"])
                store(B - 1, yn_ready, yn[:, :, :].rearrange("p n c -> p (n c)"), io["yn_4"])
                sp.wait_ge(stored, 48 * B)

            @block.gpsimd
            def _(pool):
                for i, row in enumerate((k_lo[HD:HD + 1, :, :], q_lo[HD:HD + 1, :, :], v_lo[:, :, :, HD:HD + 1])):
                    nc.gpsimd.memset(row.bitcast(F32), 0.0).then_inc(pool_preset, 1)
                    pool.wait_ge(pool_preset, i + 1)

                def batch(b, last):
                    for gi in range(GROUPS):
                        if gi in ROUND_AFTER:
                            split_chunk(nc, pool, keep, b, ROUND_AFTER[gi])
                        if isinstance(b, int) and ("group", b, gi) in SK_SLOTS:
                            sk.normalise(nc, pool, SK_SLOTS.index(("group", b, gi)))
                    for s in range(STEPS):
                        if not last and s in AHEAD:
                            split_chunk(nc, pool, keep, b + 1, AHEAD.index(s))
                        if isinstance(b, int) and ("tile", b, s) in SK_SLOTS:
                            sk.normalise(nc, pool, SK_SLOTS.index(("tile", b, s)))

                with pool.Fori(0, EARLY) as b:
                    batch(b, False)
                batch(B - 2, False)
                batch(B - 1, True)

            @block.scalar
            def _(act):
                def project(b, gi):
                    act.wait_ge(proj_done, GROUPS * b + (gi + 1))
                    for place, out_hi, _ in group_pieces(gi):
                        nc.scalar.activation(out_hi, place, ACT.Copy).then_inc(proj_hi, 1)

                def max_row(b, kv):
                    act.wait_ge(row_placed, KV * b + (kv + 1))
                    nc.scalar.activation(q_hi[HD:HD + 1, kv * G:(kv + 1) * G, :],
                                         ps[HD:HD + 1, B_BANK, 0:G * T].rearrange("p (g t) -> p g t", t=T),
                                         ACT.Copy).then_inc(row_ready, 1)

                def copy_o(b, kv):
                    act.wait_ge(pv_done, STEPS * b + NT * (kv + 1))
                    act.wait_ge(wo_done, KV * b + kv)
                    nc.scalar.activation(o_sb[:, :], ps[0:HD + 1, o_bank(kv), 0:G * T], ACT.Copy).then_inc(o_copied, 1)

                def power(to, of, ready, wanted, b):
                    act.wait_ge(wanted, b + 1)
                    nc.scalar.activation(to, of, ACT.Ln).then_inc(ready, 1)
                    act.wait_ge(ready, 2 * b + 1)
                    nc.scalar.activation(to, to, ACT.Exp, scale=-0.5).then_inc(ready, 1)

                def hyper_part(b, at):
                    if at == HY_RSTD:
                        power(root[:, :], var[:, :], root_ready, var_ready, b)
                    if at == HY_COPY:
                        act.wait_ge(xn_ready, b + 1)
                        nc.scalar.activation(yn[:, :, :], xn[:, :].rearrange("p (n c) -> p n c", c=SW), ACT.Square,
                                             accum_out=square_sum[:, :]).then_inc(square_ready, 1)
                        act.wait_ge(x_turned, b + 1)
                        nc.scalar.activation(xnT[:, :, :], ps[:, Y_BANK, 0:NK * T].rearrange("p (k t) -> p k t", t=T),
                                             ACT.Copy).then_inc(xnT_ready, 1)
                    if at == HY_YN:
                        act.wait_ge(branch_done, b + 1)
                        act.wait_ge(square_ready, b + 1)
                        nc.scalar.activation(yn[:, :, :], ps[0:T, Y_BANK, :].rearrange("p (n c) -> p n c", c=SW),
                                             ACT.Copy).then_inc(yn_ready, 1)
                    if at == HY_RSTD2:
                        power(root[:, :], mean_sq[:, :], root2_ready, mean_ready, b)

                def batch(b, first):
                    if not first:
                        copy_o(b - 1, KV - 1)
                    for gi in range(GROUPS):
                        if gi == GROUPS - 1:
                            max_row(b, 0)
                        project(b, gi)
                        if gi in ROUND_AFTER:
                            c = ROUND_AFTER[gi]
                            n = CHUNKS[c][1]
                            act.wait_ge(keep["raw_loaded"], 16 * (NCH + 1) * b + 16 * (NCH + 1 if c == NCH - 1 else c + 1))
                            nc.scalar.activation(c_hi[:, c % 2, :, 0:n], keep["raw"][:, :, 0:n], ACT.Copy).then_inc(keep["chunk_hi"], 1)
                        if not first:
                            hyper_part(b - 1, gi)
                        if isinstance(b, int) and b == EARLY:
                            sk.exponentials(nc, act, gi)
                    for g in range(STEPS):
                        kv, t, n = g // NT, g % NT, KEY_TILES[g % NT][1]
                        act.wait_ge(scores, STEPS * b + (g + 1))
                        act.wait_ge(p_lo_ready, STEPS * b + max(g - 1, 0))
                        nc.scalar.activation(p[0:n, g % 2, :], ps[0:n, S0 + g % 3, 0:G * T], ACT.Exp,
                                             scale=scale).then_inc(exp_done, 1)
                        act.wait_ge(exp_done, STEPS * b + (g + 1))
                        act.wait_ge(pv_done, STEPS * b + max(g - RING + 1, 0))
                        nc.scalar.activation(p_hi[0:n, g % RING, :], p[0:n, g % 2, :], ACT.Copy).then_inc(p_hi_ready, 1)
                        if kv and t == LAG - 1:
                            copy_o(b, kv - 1)
                        if kv < KV - 1 and t == MAX_ROW_AT:
                            max_row(b, kv + 1)

                nc.scalar.preload_act_table_set("natural_log_exp_and_others")
                batch(0, True)
                with act.Fori(1, EARLY) as b:
                    batch(b, False)
                for b in range(EARLY, B):
                    batch(b, False)
                copy_o(B - 1, KV - 1)
                for at in range(GROUPS):
                    hyper_part(B - 1, at)

            @block.vector
            def _(dve):
                nc.vector.memset(ones[:, :], 1.0).then_inc(preset, 1)
                nc.vector.memset(neg_max[:, :, :], 0.0).then_inc(preset, 1)
                nc.vector.memset(k_hi[HD:HD + 1, :, :].bitcast(F32), 1.0).then_inc(preset, 1)
                nc.vector.memset(v_hi[:, :, :, HD:HD + 1].bitcast(F32), 1.0).then_inc(preset, 1)

                def project(b, gi):
                    for i, (place, out_hi, out_lo) in enumerate(group_pieces(gi)):
                        dve.wait_ge(proj_hi, PIECES * b + (PIECES_BEFORE[gi] + i + 1))
                        nc.vector.tensor_tensor(out_lo, place, out_hi.bitcast(F32), ALU.subtract).then_inc(proj_lo, 1)

                def round_next(b, c, before):
                    dve.wait_ge(proj_done, GROUPS * before + GROUPS)
                    round_chunk(nc, dve, keep, b, c)

                def rough_maximum(b, c, head):
                    n = H * c + head
                    dve.wait_ge(rough_done, MAXIMA * b + (n + 1))
                    nc.vector.tensor_reduce(maxima[:, head, c:c + 1], ps[0:T, S0 + n % 3, 0:CHUNKS[c][1]],
                                            AX.X, ALU.max).then_inc(rough_max, 1)

                def negate(b, kv):
                    if kv == 0:
                        dve.wait_ge(rough_max, MAXIMA * b + MAXIMA)
                    nc.vector.tensor_reduce(head_max[:, :], maxima[:, kv * G:(kv + 1) * G, :], AX.X,
                                            ALU.max).then_inc(max_ready, 1)
                    dve.wait_ge(max_ready, KV * b + (kv + 1))
                    dve.wait_ge(row_placed, KV * b + kv)
                    nc.vector.tensor_scalar(neg_max[:, :, HD], head_max[:, :], -1.0, None, ALU.mult).then_inc(neg_ready, 1)

                def invert_sums(b, kv):
                    dve.wait_ge(sums_turned, KV * b + (kv + 1))
                    nc.vector.reciprocal(recip[:, :], ps[0:T, B_BANK, G * T:G * T + G]).then_inc(recip_ready, 1)
                    dve.wait_ge(recip_ready, KV * b + (kv + 1))
                    nc.vector.tensor_tensor(diag[:, :, :], keep["ident"][0:T, 0:T].unsqueeze(1).to_broadcast([T, G, T]),
                                            recip[:, :].unsqueeze(2).to_broadcast([T, G, T]), ALU.mult).then_inc(diag_ready, 1)

                def normalise(b, kv):
                    dve.wait_ge(spread, KV * b + (kv + 1))
                    nc.vector.tensor_tensor(o_sb[0:HD, :], ps[0:HD, B_BANK, 0:G * T], o_sb[0:HD, :], ALU.mult).then_inc(normal, 1)

                def residual(b):
                    dve.wait_ge(wo_done, KV * b + KV)
                    dve.wait_ge(x_loaded, 16 * b + 16)
                    nc.vector.scalar_tensor_tensor(out=x_rows[:, :], in0=ps[0:T, Y_BANK, :], scalar=keep["tanh"][0:T, 0:1],
                                                   in1=x_rows[:, :], op0=ALU.mult, op1=ALU.add).then_inc(x1_ready, 1)

                def newton(b, op, result, of):
                    for i, (to, a, c) in enumerate(((newton_t, root, root), (newton_t, newton_t, of))):
                        nc.vector.tensor_tensor(to[:, :], a[:, :], c[:, :], ALU.mult).then_inc(hyper, 1)
                        dve.wait_ge(hyper, HYPER_OPS * b + (op + i + 1))
                    nc.vector.tensor_scalar(newton_t[:, :], newton_t[:, :], -0.5, 1.5, ALU.mult, ALU.add).then_inc(hyper, 1)
                    dve.wait_ge(hyper, HYPER_OPS * b + (op + 3))
                    nc.vector.tensor_tensor(result[:, :], root[:, :], newton_t[:, :], ALU.mult).then_inc(hyper, 1)
                    dve.wait_ge(hyper, HYPER_OPS * b + (op + 4))

                def hyper_part(b, at):
                    base = HYPER_OPS * b
                    if at == HY_RESIDUAL:
                        residual(b)
                    if at == HY_STATS:
                        dve.wait_ge(x1_ready, b + 1)
                        nc.vector.bn_stats(stats[:, :], x_rows[:, :]).then_inc(hyper, 1)
                        dve.wait_ge(hyper, base + (OP_STATS + 1))
                        dve.sem_inc(settled, 1)
                        nc.vector.bn_aggr(mv[:, :], stats[:, :]).then_inc(hyper, 1)
                        dve.wait_ge(hyper, base + (OP_STATS + 2))
                        nc.vector.tensor_scalar(var[:, :], mv[:, 1:2], LN_EPS, None, ALU.add).then_inc(var_ready, 1)
                    if at == HY_NORM:
                        dve.wait_ge(var_ready, b + 1)
                        dve.wait_ge(root_ready, 2 * b + 2)
                        newton(b, OP_NEWTON, rstd, var)
                        nc.vector.tensor_scalar(xn[:, :], x_rows[:, :], mv[:, 0:1], rstd[:, :], ALU.subtract,
                                                ALU.mult).then_inc(xn_ready, 1)
                    if at == HY_MEAN:
                        dve.wait_ge(square_ready, b + 1)
                        nc.vector.tensor_scalar(mean_sq[:, :], square_sum[:, :], 1.0 / D, RMS_EPS, ALU.mult,
                                                ALU.add).then_inc(mean_ready, 1)
                    if at == HY_LOGIT_ROWS:
                        dve.wait_ge(mean_ready, b + 1)
                        dve.wait_ge(root2_ready, 2 * b + 2)
                        newton(b, OP_NEWTON2, rstd2, mean_sq)
                        dve.wait_ge(logits_done, b + 1)
                        start = b * 24
                        rows = keep["logits"][:, start:start + 24] if isinstance(b, int) else keep["logits"][:, bass.ds(start, 24)]
                        nc.vector.scalar_tensor_tensor(out=rows, in0=ps[0:T, B_BANK, LOGITS:LOGITS + 24], scalar=rstd2[:, :],
                                                       in1=h_base[:, :], op0=ALU.mult, op1=ALU.add).then_inc(logit_rows_ready, 1)

                def batch(b, first, last):
                    for gi in range(GROUPS):
                        c, i = GROUP_OF[gi]
                        for k in range(NK):
                            if (i, k) in ROUGH_AT:
                                for head in ROUGH_AT[i, k]:
                                    rough_maximum(b, c, head)
                        if gi == GROUPS - 2:
                            negate(b, 0)
                        project(b, gi)
                        if not first and gi == END_TURN:
                            invert_sums(b - 1, KV - 1)
                        if not first and gi == END_SPREAD:
                            normalise(b - 1, KV - 1)
                        if not first:
                            hyper_part(b - 1, gi)
                        if isinstance(b, int) and b == EARLY:
                            if gi == SK_ROWS:
                                dve.wait_ge(logit_rows_ready, EARLY)
                            sk.softmax_rows(nc, dve, gi)
                        if isinstance(b, int) and ("group", b, gi) in SK_SLOTS:
                            sk.invert(nc, dve, SK_SLOTS.index(("group", b, gi)))
                    for s in range(STEPS):
                        kv, t, n = s // NT, s % NT, KEY_TILES[s % NT][1]
                        dve.wait_ge(p_hi_ready, STEPS * b + (s + 1))
                        nc.vector.tensor_tensor(p_lo[0:n, s % RING, :], p[0:n, s % 2, :],
                                                p_hi[0:n, s % RING, :].bitcast(F32), ALU.subtract).then_inc(p_lo_ready, 1)
                        if not last and s in AHEAD:
                            round_next(b + 1, AHEAD.index(s), b)
                        if kv < KV - 1 and t == NEGATE_AT:
                            negate(b, kv + 1)
                        if kv and t == TURN_AT:
                            invert_sums(b, kv - 1)
                        if kv and t == SPREAD_AT:
                            normalise(b, kv - 1)
                        if isinstance(b, int) and ("tile", b, s) in SK_SLOTS:
                            sk.invert(nc, dve, SK_SLOTS.index(("tile", b, s)))

                batch(0, True, False)
                dve.wait_ge(weights_in, 48)
                with dve.Fori(1, EARLY) as b:
                    batch(b, False, False)
                batch(B - 2, False, False)
                batch(B - 1, False, True)
                invert_sums(B - 1, KV - 1)
                normalise(B - 1, KV - 1)
                for at in range(GROUPS):
                    hyper_part(B - 1, at)
                dve.wait_ge(logit_rows_ready, B)

            @block.tensor
            def _(pe):

                def rough_scores(b, c, head):
                    n = H * c + head
                    kv = head // G
                    pe.wait_ge(rough_max, MAXIMA * b + max(n - 2, 0))
                    if head % G == 0:
                        pe.wait_ge(proj_hi, PIECES * b + PIECES_BEFORE[FIRST_GROUP[c] + min(kv, KG - 1) + 1])
                    if n == 0:
                        pe.wait_ge(exp_done, STEPS * b)
                        pe.wait_ge(q_loaded, 32 * b + 32)
                    if n == H - G:
                        pe.wait_ge(q_last_loaded, 32 * b + 32)
                    k0, keys, _, _ = CHUNKS[c]
                    pe.matmul(ps[0:T, S0 + n % 3, 0:keys], q_hi[0:HD, head, :], k_hi[0:HD, kv, k0:k0 + keys],
                              start=True, stop=True).then_inc(rough_done, 1)

                def place_max_row(b, kv):
                    if kv == 0 and isinstance(b, int):
                        pe.wait_ge(preset, 4)
                        pe.wait_ge(pool_preset, 3)
                    pe.wait_ge(neg_ready, KV * b + (kv + 1))
                    pe.wait_ge(row_ready, KV * b + kv)
                    pe.wait_ge(normal, KV * b + max(kv - 1, 0))
                    for i in range(G):
                        mm = pe.matmul(ps[0:HD + 1, B_BANK, i * T:(i + 1) * T], neg_max[:, i, :],
                                       keep["ident"][0:T, 0:T], start=True, stop=True)
                    mm.then_inc(row_placed, 1)

                def project(b, gi, first):
                    c, i = GROUP_OF[gi]
                    k0, n, t0, _ = CHUNKS[c]
                    slot = c % 2
                    if i == 0:
                        pe.wait_ge(chunk_ready, NCH * b + (c + 1))
                    pe.wait_ge(proj_lo, PIECES * b + PIECES_BEFORE[max(gi - 1, 0)])
                    for k in range(NK):
                        if i < KG:
                            w = slice(i * 128, (i + 1) * 128)
                            mm = split_product(pe, ps[:, M0 + gi % 2, 0:n], keep["wk_hi"][:, k, w], keep["wk_lo"][:, k, w],
                                               c_hi[:, slot, k, 0:n], c_lo[:, slot, k, 0:n], k == 0, k == NK - 1)
                        else:
                            key0, rows = KEY_TILES[t0 + i - KG]
                            keys = slice(key0 - k0, key0 - k0 + rows)
                            mm = split_product(pe, ps[0:rows, M0 + gi % 2, 0:KV * HD], c_hi[:, slot, k, keys],
                                               c_lo[:, slot, k, keys], keep["wv_hi"][:, k, :], keep["wv_lo"][:, k, :],
                                               k == 0, k == NK - 1)
                        if (i, k) in ROUGH_AT:
                            for head in ROUGH_AT[i, k]:
                                rough_scores(b, c, head)
                        if (gi, k) == (GROUPS - 1, 1):
                            place_max_row(b, 0)
                        if gi == 0 and k < LAG and not first:
                            weigh_values(b - 1, STEPS - LAG + k)
                    mm.then_inc(proj_done, 1)

                def score(b, g):
                    kv, t = g // NT, g % NT
                    k0, n = KEY_TILES[t]
                    pe.wait_ge(exp_done, STEPS * b + max(g - 2, 0))
                    if g == 0:
                        pe.wait_ge(rough_max, MAXIMA * b + MAXIMA)
                        pe.wait_ge(proj_lo, PIECES * b + PIECES_BEFORE[FIRST_GROUP[NCH - 1] + KG])
                    if t == 0:
                        pe.wait_ge(row_ready, KV * b + (kv + 1))
                    q = slice(kv * G, (kv + 1) * G)
                    split_product(pe, ps[0:n, S0 + g % 3, 0:G * T], k_hi[:, kv, k0:k0 + n], k_lo[:, kv, k0:k0 + n],
                                  q_hi[:, q, :], q_lo[:, q, :], True, True).then_inc(scores, 1)

                def weigh_values(b, g):
                    kv, t = g // NT, g % NT
                    n = KEY_TILES[t][1]
                    pe.wait_ge(p_lo_ready, STEPS * b + (g + 1))
                    if g == 0:
                        pe.wait_ge(proj_lo, PIECES * b + PIECES)
                    if t == 0:
                        pe.wait_ge(o_copied, KV * b + max(kv - 1, 0))
                    split_product(pe, ps[0:HD + 1, o_bank(kv), 0:G * T], v_hi[0:n, t, kv, :], v_lo[0:n, t, kv, :],
                                  p_hi[0:n, g % RING, :], p_lo[0:n, g % RING, :], t == 0, t == NT - 1).then_inc(pv_done, 1)

                def turn_sums(b, kv):
                    pe.wait_ge(o_copied, KV * b + (kv + 1))
                    pe.wait_ge(row_ready, KV * b + min(kv + 2, KV))
                    for i in range(G):
                        mm = pe.matmul(ps[0:T, B_BANK, G * T + i:G * T + i + 1], o_sb[HD:HD + 1, i * T:(i + 1) * T],
                                       ones[HD:HD + 1, 0:1], start=True, stop=True)
                    mm.then_inc(sums_turned, 1)

                def spread_recip(b, kv):
                    pe.wait_ge(diag_ready, KV * b + (kv + 1))
                    pe.matmul(ps[0:HD, B_BANK, 0:G * T], ones[0:T, :], diag[:, :, :],
                              start=True, stop=True).then_inc(spread, 1)

                def project_out(b, kv):
                    pe.wait_ge(normal, KV * b + (kv + 1))
                    if kv == 0:
                        pe.wait_ge(wo_loaded, 16)
                        pe.wait_ge(yn_ready, b)
                    for i in range(G):
                        mm = pe.matmul(ps[0:T, Y_BANK, :], o_sb[0:HD, i * T:(i + 1) * T], wo[:, kv * G + i, :],
                                       start=(kv == 0 and i == 0), stop=(kv == KV - 1 and i == G - 1))
                    mm.then_inc(wo_done, 1)

                def hyper_part(b, at):
                    if at == HY_TURN:
                        pe.wait_ge(xn_ready, b + 1)
                        for k in range(NK):
                            mm = pe.transpose(ps[:, Y_BANK, k * T:(k + 1) * T], xn[:, k * 128:(k + 1) * 128],
                                              keep["ident"][0:T, 0:T])
                        mm.then_inc(x_turned, 1)
                    if at == HY_LOGITS:
                        pe.wait_ge(xnT_ready, b + 1)
                        for k in range(NK):
                            mm = pe.matmul(ps[0:T, B_BANK, LOGITS:LOGITS + 24], xnT[:, k, :], w_h[:, k, :],
                                           start=(k == 0), stop=(k == NK - 1))
                        mm.then_inc(logits_done, 1)
                        for k in range(NK):
                            mm = pe.matmul(ps[0:T, Y_BANK, k * SW:(k + 1) * SW], xnT[:, k, :], w_branch[:, :],
                                           start=True, stop=True)
                        mm.then_inc(branch_done, 1)

                def batch(b, first):
                    for gi in range(GROUPS):
                        project(b, gi, first)
                        for end, at in ((turn_sums, END_TURN), (spread_recip, END_SPREAD), (project_out, END_OUT)):
                            if not first and gi == at:
                                end(b - 1, KV - 1)
                        if not first:
                            hyper_part(b - 1, gi)
                    for s in range(STEPS):
                        kv, t = s // NT, s % NT
                        score(b, s)
                        if kv < KV - 1 and t == MAX_ROW_AT:
                            place_max_row(b, kv + 1)
                        if s >= LAG:
                            weigh_values(b, s - LAG)
                        if 0 < kv < KV and t == TURN_AT:
                            turn_sums(b, kv - 1)
                        if 0 < kv < KV and t == SPREAD_AT:
                            spread_recip(b, kv - 1)
                        if 0 < kv < KV and t == OUT_AT:
                            project_out(b, kv - 1)

                batch(0, True)
                pe.wait_ge(weights_in, 48)
                with pe.Fori(1, B) as b:
                    batch(b, False)
                for s in range(STEPS - LAG, STEPS):
                    weigh_values(B - 1, s)
                for end in (turn_sums, spread_recip, project_out):
                    end(B - 1, KV - 1)
                for at in range(GROUPS):
                    hyper_part(B - 1, at)


def hyper_connection(nc, whole, io, keep):
    with ExitStack() as ctx:
        def sb(name, shape, dt=F32):
            return ctx.enter_context(nc.sbuf_tensor("b_" + name, shape, dt))

        def sem(name):
            return whole.enter_context(nc.semaphore("b_" + name))

        x_rows = keep["x_rows"]
        xn = sb("xn", [T, B, D])
        yn = sb("yn", [T, B, STREAMS, SW])
        y = sb("y", [T, B, SW])
        pool_y, pool_term = sb("pool_y", [T, SW]), sb("pool_term", [T, STREAMS, SW])
        mixer = sb("mixer", [T, 2])
        h_res = sb("res", [T, B, 4, 4])
        raw = sb("raw", [128, 2, NK, D])
        raw_loaded, small_loaded, w_hi_ready, w_lo_ready = (sem(n) for n in ("raw", "small", "w_hi", "w_lo"))
        step, weights_ready, pool_step = (sem(n) for n in ("step", "weights", "pool_step"))
        loaded = [sem("in%d" % i) for i in range(2)]
        sk = Sinkhorn(keep, 1, EARLY, B)
        POOL_BATCHES = (3, 4, 5)

        with nc.Block() as block:
            @block.sync
            def _(sp):
                for i, part in enumerate((slice(0, EARLY), slice(EARLY, B))):
                    for to, of in ((x_rows, "x1_4"), (xn, "xn_4"), (yn[:, :, :, :].rearrange("p b n c -> p b (n c)"), "yn_4")):
                        sp.dma_start(to[:, part, :], io[of][part].rearrange("b t d -> t b d")).then_inc(loaded[i], 16)
                sp.dma_start(raw[:, 0, :, :], io["wq1T"]).then_inc(raw_loaded, 16)
                sp.dma_start(raw[:, 1, :, :], io["wk1"]).then_inc(raw_loaded, 16)
                sp.dma_start(keep["bq1"][:, :], io["bq1"]).then_inc(small_loaded, 16)
                sp.dma_start(keep["bk1"][:, :], io["bk1"]).then_inc(small_loaded, 16)
                sp.wait_ge(small_loaded, 32)

            @block.scalar
            def _(act):
                for at in (SK_EXP, SK_LN, SK_EXP2):
                    sk.exponentials(nc, act, at)
                act.wait_ge(raw_loaded, 32)
                for i, name in enumerate(("wq1", "wk1")):
                    nc.scalar.activation(keep[name + "_hi"][:, :, :], raw[:, i, :, :], ACT.Copy).then_inc(w_hi_ready, 1)

            @block.gpsimd
            def _(pool):
                done = [0]

                def link(ins):
                    done[0] += 1
                    ins.then_inc(pool_step, 1)
                    pool.wait_ge(pool_step, done[0])

                pool.wait_ge(loaded[0], 48)
                pool.wait_ge(weights_ready, 1)
                for i, b in enumerate(POOL_BATCHES):
                    for j in range(STREAMS):
                        by = keep["h_pp"][:, b, 0, j:j + 1].to_broadcast([T, SW])
                        link(nc.gpsimd.tensor_tensor((pool_term[:, 0, :] if j else pool_y[:, :]), yn[:, b, j, :], by, ALU.mult))
                        if j:
                            link(nc.gpsimd.tensor_tensor(pool_y[:, :], pool_y[:, :], pool_term[:, 0, :], ALU.add))
                    streams = x_rows[:, b, :].rearrange("p (n c) -> p n c", c=SW)
                    for j in range(STREAMS + 1):
                        of, by = ((pool_y[:, :], keep["h_pp"][:, b, 1, :]) if j == STREAMS else
                                  (xn[:, b, j * SW:(j + 1) * SW], h_res[:, b, :, j]))
                        link(nc.gpsimd.tensor_tensor(pool_term[:, :, :], of.unsqueeze(1).to_broadcast([T, STREAMS, SW]),
                                                     by.unsqueeze(2).to_broadcast([T, STREAMS, SW]), ALU.mult))
                        link(nc.gpsimd.tensor_tensor(streams, streams, pool_term[:, :, :], ALU.add))
                    if i < 2:
                        name = ("wq1", "wk1")[i]
                        pool.wait_ge(w_hi_ready, i + 1)
                        nc.gpsimd.tensor_tensor(keep[name + "_lo"][:, :, :], raw[:, i, :, :],
                                                keep[name + "_hi"][:, :, :].bitcast(F32), ALU.subtract).then_inc(w_lo_ready, 1)
                pool.wait_ge(w_lo_ready, 2)

            @block.vector
            def _(dve):
                done = [0]

                def step_of(ins):
                    done[0] += 1
                    ins.then_inc(step, 1)

                def link(ins):
                    step_of(ins)
                    dve.wait_ge(step, done[0])

                def weights(part):
                    flat = h_res[:, part, :, :].rearrange("p b i j -> p b (i j)")
                    link(nc.vector.tensor_scalar(h_res[:, part, :, :], keep["sink"][:, part, :, :], mixer[:, 0:1], None, ALU.mult))
                    nc.vector.tensor_scalar(flat[:, :, 0:16:5], flat[:, :, 0:16:5], mixer[:, 1:2], None, ALU.add).then_inc(weights_ready, 1)

                def mixing(batches):
                    for b in batches:
                        for j in range(STREAMS):
                            if j == 0:
                                yield lambda: nc.vector.tensor_scalar(y[:, b, :], yn[:, b, 0, :], keep["h_pp"][:, b, 0, 0:1], None, ALU.mult)
                            else:
                                yield lambda: nc.vector.scalar_tensor_tensor(
                                    out=y[:, b, :], in0=yn[:, b, j, :], scalar=keep["h_pp"][:, b, 0, j:j + 1], in1=y[:, b, :],
                                    op0=ALU.mult, op1=ALU.add)
                            for i in range(STREAMS):
                                stream = slice(i * SW, (i + 1) * SW)
                                yield lambda: nc.vector.scalar_tensor_tensor(
                                    out=x_rows[:, b, stream], in0=xn[:, b, j * SW:(j + 1) * SW], scalar=h_res[:, b, i, j:j + 1],
                                    in1=x_rows[:, b, stream], op0=ALU.mult, op1=ALU.add)
                        for i in range(STREAMS):
                            stream = slice(i * SW, (i + 1) * SW)
                            yield lambda: nc.vector.scalar_tensor_tensor(
                                out=x_rows[:, b, stream], in0=y[:, b, :], scalar=keep["h_pp"][:, b, 1, i:i + 1],
                                in1=x_rows[:, b, stream], op0=ALU.mult, op1=ALU.add)

                link(nc.vector.tensor_scalar(mixer[:, :], keep["sigmoid"][0:T, :], keep["tanh"][0:T, 2:3], None, ALU.mult))
                weights(slice(0, EARLY))
                for at in (SK_ROWS, SK_SUMS, SK_COLS):
                    sk.softmax_rows(nc, dve, at)
                dve.wait_ge(weights_ready, 1)
                dve.wait_ge(sk.e2_ready, 2)
                beside = mixing([b for b in range(EARLY) if b not in POOL_BATCHES])

                def linked(ins, mix):
                    step_of(ins)
                    mine = done[0]
                    other = next(beside, None) if mix else None
                    if other is not None:
                        step_of(other())
                    dve.wait_ge(step, mine)

                MIX_FROM = 20
                for n in range(NORMS):
                    mix = n >= MIX_FROM
                    if n == MIX_FROM:
                        dve.wait_ge(loaded[0], 48)
                    m, spread = ((sk.sink.rearrange("p b i j -> p b j i"), sk.along_cols) if n % 2 == 0 else
                                 (sk.sink, sk.along_rows))
                    linked(nc.vector.tensor_reduce(sk.marginal, m, AX.X, ALU.add), mix)
                    linked(nc.vector.reciprocal(sk.inverse, sk.marginal), mix)
                    linked(nc.vector.tensor_tensor(sk.sink, sk.sink, spread(sk.inverse), ALU.mult), mix)
                for other in beside:
                    dve.wait_ge(step, done[0] - 1)
                    step_of(other())
                weights(slice(EARLY, B))
                dve.wait_ge(weights_ready, 2)
                dve.wait_ge(loaded[1], 48)
                for other in mixing(range(EARLY, B)):
                    dve.wait_ge(step, done[0] - 1)
                    step_of(other())
                dve.wait_ge(step, done[0])


LN_SEMS = ("step", "var", "sd", "xn", "turned", "hi", "lo")


def layer_norm_turned(nc, name, keep, turn, x_nT, sync_beside=None, scalar_beside=None, gpsimd_beside=None):
    with ExitStack() as ctx:
        def sb(n, shape, dt=F32):
            return ctx.enter_context(nc.sbuf_tensor(name + n, shape, dt))

        x_rows = keep["x_rows"]
        xn = sb("xn", [T, B, D])
        stats, mv = sb("stats", [T, B, 6]), sb("mv", [T, B, 2])
        var, sd, tmp, rstd = (sb("s%d" % i, [T, B]) for i in range(4))
        ps = ctx.enter_context(nc.psum_tensor(name + "ps", [128, 8, BANK], F32))
        step, var_ready, sd_ready, xn_ready, turned, hi_ready, lo_ready = keep["ln_sems"]
        before = B * turn
        TURN_BANKS = 4

        with nc.Block() as block:
            if sync_beside:
                block.sync(sync_beside)
            if gpsimd_beside:
                block.gpsimd(gpsimd_beside)

            @block.scalar
            def _(act):
                act.wait_ge(var_ready, turn + 1)
                nc.scalar.activation(sd[:, :], var[:, :], ACT.Sqrt).then_inc(sd_ready, 1)
                if scalar_beside:
                    scalar_beside(act)
                for b in range(B):
                    act.wait_ge(turned, before + b + 1)
                    nc.scalar.activation(x_nT[0][:, :, b * T:(b + 1) * T],
                                         ps[:, b % TURN_BANKS, 0:NK * T].rearrange("p (k t) -> p k t", t=T),
                                         ACT.Copy).then_inc(hi_ready, 1)

            @block.vector
            def _(dve):
                done = [(2 * B + 5) * turn]

                def link(ins):
                    done[0] += 1
                    ins.then_inc(step, 1)
                    dve.wait_ge(step, done[0])

                for b in range(B):
                    nc.vector.bn_stats(stats[:, b, :], x_rows[:, b, :]).then_inc(step, 1)
                    done[0] += 1
                for b in range(B):
                    dve.wait_ge(step, done[0] - (B - 1))
                    nc.vector.bn_aggr(mv[:, b, :], stats[:, b, :]).then_inc(step, 1)
                    done[0] += 1
                dve.wait_ge(step, done[0])
                nc.vector.tensor_scalar(var[:, :], mv[:, :, 1], LN_EPS, None, ALU.add).then_inc(var_ready, 1)
                dve.wait_ge(var_ready, turn + 1)
                dve.wait_ge(sd_ready, turn + 1)
                refined_rsqrt(nc, link, rstd[:, :], sd[:, :], var[:, :], tmp[:, :])
                for b in range(B):
                    nc.vector.tensor_scalar(xn[:, b, :], x_rows[:, b, :], mv[:, b, 0:1], rstd[:, b:b + 1],
                                            ALU.subtract, ALU.mult).then_inc(xn_ready, 1)
                for b in range(B):
                    cols = slice(b * T, (b + 1) * T)
                    dve.wait_ge(hi_ready, before + b + 1)
                    nc.vector.tensor_tensor(x_nT[1][:, :, cols],
                                            ps[:, b % TURN_BANKS, 0:NK * T].rearrange("p (k t) -> p k t", t=T),
                                            x_nT[0][:, :, cols].bitcast(F32), ALU.subtract).then_inc(lo_ready, 1)

            @block.tensor
            def _(pe):
                for b in range(B):
                    pe.wait_ge(xn_ready, before + b + 1)
                    if b >= TURN_BANKS:
                        pe.wait_ge(lo_ready, before + b - TURN_BANKS + 1)
                    for k in range(NK):
                        mm = pe.transpose(ps[:, b % TURN_BANKS, k * T:(k + 1) * T], xn[:, b, k * 128:(k + 1) * 128],
                                          keep["ident"][0:T, 0:T])
                    mm.then_inc(turned, 1)


def project_features(nc, whole, io, keep):
    with ExitStack() as ctx:
        def sb(name, shape, dt=F32):
            return ctx.enter_context(nc.sbuf_tensor("c_" + name, shape, dt))

        def sem(name):
            return whole.enter_context(nc.semaphore("c_" + name))

        x_nT = [sb(n, [128, NK, NTOK], F32R) for n in ("xnT_hi", "xnT_lo")]

        def load_first_features(sp):
            for b in range(2):
                for c, (f0, n) in enumerate(SB):
                    if b:
                        sp.wait_ge(keep["feats_loaded"][c], 16)
                    sp.dma_start(keep["feats"][:, b, :, f0:f0 + n], io["ctxT"][b, :, :, f0:f0 + n]).then_inc(keep["feats_loaded"][c], 16)

        layer_norm_turned(nc, "cn_", keep, 0, x_nT, sync_beside=load_first_features)
        q = sb("q", [128, NK, NTOK])
        q_hi, q_lo = (sb(n, [128, NK, NTOK], F32R) for n in ("q_hi", "q_lo"))
        ps = ctx.enter_context(nc.psum_tensor("c_ps", [128, 8, BANK], F32))
        Q_BANKS, QBK = 6, 7
        q_done, q_copied, q_hi_ready, q_lo_ready, f_done, f_copied, qbk_done, qbk_ready = (
            sem(n) for n in ("q", "q_copied", "qh", "ql", "f", "f_copied", "qbk", "qbk_ready"))
        PRODUCTS = [(half, m) for half in range(2) for m in range(NK)]

        with nc.Block() as block:
            @block.scalar
            def _(act):
                for i, (half, m) in enumerate(PRODUCTS):
                    cols = slice(half * HALF, (half + 1) * HALF)
                    act.wait_ge(q_done, i + 1)
                    nc.scalar.activation(q[:, m, cols], ps[:, i % Q_BANKS, 0:HALF], ACT.Identity,
                                         bias=keep["bq1"][:, m:m + 1]).then_inc(q_copied, 1)
                for i, (half, m) in enumerate(PRODUCTS):
                    cols = slice(half * HALF, (half + 1) * HALF)
                    act.wait_ge(f_done, i + 1)
                    nc.scalar.activation(keep["queries"][:, m, cols], ps[:, (i + len(PRODUCTS)) % Q_BANKS, 0:HALF],
                                         ACT.Copy).then_inc(f_copied, 1)
                act.wait_ge(qbk_done, 1)
                nc.scalar.activation(keep["qbk"][:, :], ps[0:T, QBK, 0:B], ACT.Copy).then_inc(qbk_ready, 1)

            @block.vector
            def _(dve):
                for i, (half, m) in enumerate(PRODUCTS):
                    cols = slice(half * HALF, (half + 1) * HALF)
                    dve.wait_ge(q_copied, i + 1)
                    nc.vector.tensor_copy(q_hi[:, m, cols], q[:, m, cols]).then_inc(q_hi_ready, 1)
                    dve.wait_ge(q_hi_ready, i + 1)
                    nc.vector.tensor_tensor(q_lo[:, m, cols], q[:, m, cols], q_hi[:, m, cols].bitcast(F32),
                                            ALU.subtract).then_inc(q_lo_ready, 1)

            @block.tensor
            def _(pe):
                def product(i, w, of, done):
                    half, m = PRODUCTS[i % len(PRODUCTS)]
                    cols = slice(half * HALF, (half + 1) * HALF)
                    for k in range(NK):
                        to = slice(m * 128, (m + 1) * 128)
                        mm = split_product(pe, ps[:, i % Q_BANKS, 0:HALF], keep[w + "_hi"][:, k, to], keep[w + "_lo"][:, k, to],
                                           of[0][:, k, cols], of[1][:, k, cols], k == 0, k == NK - 1)
                    mm.then_inc(done, 1)

                for i in range(len(PRODUCTS)):
                    if i >= Q_BANKS:
                        pe.wait_ge(q_copied, i - Q_BANKS + 1)
                    product(i, "wq1", x_nT, q_done)
                for i in range(len(PRODUCTS)):
                    pe.wait_ge(q_lo_ready, NK * (PRODUCTS[i][0] + 1))
                    if i + len(PRODUCTS) - Q_BANKS < len(PRODUCTS):
                        pe.wait_ge(q_copied, i + len(PRODUCTS) - Q_BANKS + 1)
                    else:
                        pe.wait_ge(f_copied, i - Q_BANKS + 1)
                    product(i + len(PRODUCTS), "wk1", (q_hi, q_lo), f_done)
                for b in range(B):
                    for k in range(NK):
                        mm = pe.matmul(ps[0:T, QBK, b:b + 1], q[:, k, b * T:(b + 1) * T], keep["bk1"][:, k:k + 1],
                                       start=(k == 0), stop=(k == NK - 1))
                mm.then_inc(qbk_done, 1)


FT = [(128 * i, 128) for i in range(10)] + [(1280, 82), (1362, 82)]
NF = len(FT)
SB = chunk_sizes(CTX, BANK)
NSB = len(SB)
TG = NF // NSB
SCORES_AT, WEIGH_LAG, NATURAL_RING = 3, 3, 6
SCORE_PRODUCTS = [(k, part) for k in range(NK) for part in range(3)]
PER_STEP = len(SCORE_PRODUCTS) // ((NF - SCORES_AT) // NSB)
TURN_STEPS = (2, 6, 10)
EXP_STEP, QUERY_STEP, GAIN_STEP, UPDATE_STEP = 0, 1, 4, 3
MAX_STEPS = {6: 0, 9: 1}
SPLIT_STEPS = {1: (1, 1), 4: (2, 1), 9: (0, 2)}


def attend_features(nc, whole, io, keep):
    scale = float(D) ** -0.5
    with ExitStack() as ctx:
        def sb(name, shape, dt=F32):
            return ctx.enter_context(nc.sbuf_tensor("f_" + name, shape, dt))

        def sem(name):
            return whole.enter_context(nc.semaphore("f_" + name))

        x_rows = keep["x_rows"]
        feats, loaded = keep["feats"], keep["feats_loaded"]
        c_hi, c_lo = (sb(n, [128, NSB, NK, BANK], F32R) for n in ("c_hi", "c_lo"))
        qs_hi, qs_lo = (sb(n, [128, NK, T], F32R) for n in ("q_hi", "q_lo"))
        n_hi, n_lo = (sb(n, [128, NATURAL_RING, D], F32R) for n in ("n_hi", "n_lo"))
        p = sb("p", [T, CTX])
        pT_hi, pT_lo = (sb(n, [128, NSB, TG, T], F32R) for n in ("pT_hi", "pT_lo"))
        bank_max = sb("bmax", [T, NSB])
        top, bias = sb("top", [T, 1]), sb("bias", [T, 1])
        sums, total, recip, gain = sb("sums", [T, NSB]), sb("total", [T, 1]), sb("recip", [T, 1]), sb("gain", [T, 1])
        ps = ctx.enter_context(nc.psum_tensor("f_ps", [128, 8, BANK], F32))
        S0, N0, P_BANK, O0 = 0, 3, 5, 6

        c_hi_ready, c_ready, qs_hi_ready, qs_ready, scored, maxed, top_ready, shifted, bias_ready = (
            sem(n) for n in ("c_hi", "c", "qs_hi", "qs", "scored", "maxed", "top", "shifted", "bias"))
        exp_done, p_turned, pT_hi_ready, pT_ready, n_turned, n_hi_ready, n_ready, weighed = (
            sem(n) for n in ("exp", "p_turned", "pT_hi", "pT", "n_turned", "n_hi", "n", "weighed"))
        total_ready, recip_ready, gain_ready, x3_ready = (sem(n) for n in ("total", "recip", "gain", "x3"))

        def run(engine, batch):
            batch(0, 0, True, False)
            with engine.Fori(0, (B - 4) // 2) as pair:
                for i in range(2):
                    batch(2 * pair + (i + 1), (i + 1) % 2, False, False)
            for b in range(B - 3, B):
                batch(b, b % 2, False, b == B - 1)

        with nc.Block() as block:
            @block.sync
            def _(sp):
                def load(b, slot, c):
                    f0, n = SB[c]
                    sp.dma_start(feats[:, slot, :, f0:f0 + n], io["ctxT"][b, :, :, f0:f0 + n]).then_inc(loaded[c], 16)

                def reload(b, slot):
                    for c in range(NSB):
                        sp.wait_ge(scored, NSB * b - (NSB - c - 1))
                        load(b, slot, c)

                with sp.Fori(1, B // 2) as pair:
                    for i in range(2):
                        reload(2 * pair + i, i)

            @block.gpsimd
            def _(pool):
                def pair_of_batches(pair, first):
                    for slot in range(2):
                        for c, (f0, n) in enumerate(SB):
                            if first and slot == 0 and c == 0:
                                continue
                            number = 2 * NSB * pair + (NSB * slot + c + 1)
                            pool.wait_ge(c_hi_ready, number)
                            nc.gpsimd.tensor_tensor(c_lo[:, c, :, 0:n], feats[:, slot, :, f0:f0 + n],
                                                    c_hi[:, c, :, 0:n].bitcast(F32), ALU.subtract).then_inc(c_ready, 1)

                pair_of_batches(0, True)
                with pool.Fori(1, B // 2) as pair:
                    pair_of_batches(pair, False)

            @block.scalar
            def _(act):
                def take_queries(b, start):
                    act.wait_ge(scored, NSB * b)
                    nc.scalar.activation(qs_hi[:, :, :], keep["queries"][:, :, start:start + T] if isinstance(start, int)
                                         else keep["queries"][:, :, bass.ds(start, T)], ACT.Copy).then_inc(qs_hi_ready, 1)

                def batch(b, slot, first, last):
                    for t in range(NF):
                        n = FT[t][1]
                        act.wait_ge(n_turned, NF * b + (t + 1))
                        if not first or t >= NATURAL_RING:
                            act.wait_ge(weighed, NF * b + (t - NATURAL_RING + 1))
                        nc.scalar.activation(n_hi[0:n, t % NATURAL_RING, :], ps[0:n, N0 + t % 2, :], ACT.Copy).then_inc(n_hi_ready, 1)
                        if t == EXP_STEP:
                            act.wait_ge(bias_ready, b + 1)
                            for c, (f0, n) in enumerate(SB):
                                nc.scalar.activation(p[:, f0:f0 + n], ps[0:T, S0 + c, 0:n], ACT.Exp, scale=scale, bias=bias[:, :],
                                                     accum_out=sums[:, c:c + 1]).then_inc(exp_done, 1)
                        if t == QUERY_STEP and not last:
                            take_queries(b + 1, b * T + T)
                        if t in TURN_STEPS:
                            g = TURN_STEPS.index(t)
                            act.wait_ge(p_turned, NSB * b + (g + 1))
                            act.wait_ge(weighed, NF * b)
                            nc.scalar.activation(pT_hi[:, g, :, :], ps[:, P_BANK, 0:TG * T].rearrange("p (i t) -> p i t", t=T),
                                                 ACT.Copy).then_inc(pT_hi_ready, 1)

                take_queries(0, 0)
                run(act, batch)

            @block.vector
            def _(dve):
                def round_bank(b, slot, c):
                    f0, n = SB[c]
                    dve.wait_ge(loaded[c], 16 * b + 16)
                    if not (isinstance(b, int) and b == 0):
                        dve.wait_ge(scored, NSB * b + (c + 1 - NSB))
                    nc.vector.tensor_copy(c_hi[:, c, :, 0:n], feats[:, slot, :, f0:f0 + n]).then_inc(c_hi_ready, 1)

                def split_queries(b, start):
                    dve.wait_ge(qs_hi_ready, b + 1)
                    nc.vector.tensor_tensor(qs_lo[:, :, :], keep["queries"][:, :, start:start + T] if isinstance(start, int)
                                            else keep["queries"][:, :, bass.ds(start, T)],
                                            qs_hi[:, :, :].bitcast(F32), ALU.subtract).then_inc(qs_ready, 1)

                def bank_maximum(b, c):
                    dve.wait_ge(scored, NSB * b + (c + 1))
                    nc.vector.tensor_reduce(bank_max[:, c:c + 1], ps[0:T, S0 + c, 0:SB[c][1]], AX.X, ALU.max).then_inc(maxed, 1)

                def softmax_bias(b):
                    qbk = keep["qbk"][:, b:b + 1] if isinstance(b, int) else keep["qbk"][:, bass.ds(b, 1)]
                    dve.wait_ge(maxed, NSB * b + NSB)
                    nc.vector.tensor_reduce(top[:, :], bank_max[:, :], AX.X, ALU.max).then_inc(top_ready, 1)
                    dve.wait_ge(top_ready, b + 1)
                    nc.vector.tensor_tensor(top[:, :], top[:, :], qbk, ALU.add).then_inc(shifted, 1)
                    dve.wait_ge(shifted, 2 * b + 1)
                    nc.vector.tensor_tensor(top[:, :], qbk, top[:, :], ALU.subtract).then_inc(shifted, 1)
                    dve.wait_ge(shifted, 2 * b + 2)
                    dve.wait_ge(exp_done, NSB * b)
                    nc.vector.tensor_scalar(bias[:, :], top[:, :], scale, None, ALU.mult).then_inc(bias_ready, 1)

                def softmax_gain(b):
                    dve.wait_ge(exp_done, NSB * b + NSB)
                    nc.vector.tensor_reduce(total[:, :], sums[:, :], AX.X, ALU.add).then_inc(total_ready, 1)
                    dve.wait_ge(total_ready, b + 1)
                    nc.vector.reciprocal(recip[:, :], total[:, :]).then_inc(recip_ready, 1)
                    dve.wait_ge(recip_ready, b + 1)
                    dve.wait_ge(x3_ready, b)
                    nc.vector.tensor_scalar(gain[:, :], recip[:, :], keep["tanh"][0:T, 1:2], None, ALU.mult).then_inc(gain_ready, 1)

                def update(b, slot):
                    rows = x_rows[:, b, :]
                    dve.wait_ge(weighed, NF * b + NF)
                    dve.wait_ge(gain_ready, b + 1)
                    nc.vector.scalar_tensor_tensor(out=rows, in0=ps[0:T, O0 + slot, :], scalar=gain[:, :], in1=rows,
                                                   op0=ALU.mult, op1=ALU.add).then_inc(x3_ready, 1)

                def batch(b, slot, first, last):
                    bank_maximum(b, NSB - 1)
                    softmax_bias(b)
                    for t in range(NF):
                        n = FT[t][1]
                        dve.wait_ge(n_hi_ready, NF * b + (t + 1))
                        nc.vector.tensor_tensor(n_lo[0:n, t % NATURAL_RING, :], ps[0:n, N0 + t % 2, :],
                                                n_hi[0:n, t % NATURAL_RING, :].bitcast(F32), ALU.subtract).then_inc(n_ready, 1)
                        if t == QUERY_STEP and not last:
                            split_queries(b + 1, b * T + T)
                        if t in TURN_STEPS:
                            g = TURN_STEPS.index(t)
                            dve.wait_ge(pT_hi_ready, NSB * b + (g + 1))
                            nc.vector.tensor_tensor(pT_lo[:, g, :, :], ps[:, P_BANK, 0:TG * T].rearrange("p (i t) -> p i t", t=T),
                                                    pT_hi[:, g, :, :].bitcast(F32), ALU.subtract).then_inc(pT_ready, 1)
                        if t == UPDATE_STEP and not first:
                            update(b - 1, 1 - slot)
                        if t == GAIN_STEP:
                            softmax_gain(b)
                        if t in SPLIT_STEPS:
                            c, ahead = SPLIT_STEPS[t]
                            if not last and not (isinstance(b, int) and b + ahead >= B):
                                round_bank(b + ahead, (slot + ahead) % 2, c)
                        if t in MAX_STEPS and not last:
                            bank_maximum(b + 1, MAX_STEPS[t])

                for c in range(NSB):
                    round_bank(0, 0, c)
                    if c == 0:
                        dve.wait_ge(c_hi_ready, 1)
                        nc.vector.tensor_tensor(c_lo[:, 0, :, 0:SB[0][1]], feats[:, 0, :, 0:SB[0][1]],
                                                c_hi[:, 0, :, 0:SB[0][1]].bitcast(F32), ALU.subtract).then_inc(c_ready, 1)
                        split_queries(0, 0)
                for c in range(NSB - 1):
                    bank_maximum(0, c)
                round_bank(1, 1, 0)
                run(dve, batch)
                update(B - 1, (B - 1) % 2)
                dve.wait_ge(x3_ready, B)

            @block.tensor
            def _(pe):
                def scores(b, c, products):
                    f0, n = SB[c]
                    for i in products:
                        k, part = SCORE_PRODUCTS[i]
                        if i == 0:
                            pe.wait_ge(c_ready, NSB * b + (c + 1))
                            if c == 0:
                                pe.wait_ge(qs_ready, b + 1)
                            pe.wait_ge(exp_done, NSB * b)
                        mm = pe.matmul(ps[0:T, S0 + c, 0:n], (qs_lo if part == 2 else qs_hi)[:, k, :],
                                       (c_lo if part == 1 else c_hi)[:, c, k, 0:n],
                                       start=(i == 0), stop=(i == len(SCORE_PRODUCTS) - 1))
                        if i == len(SCORE_PRODUCTS) - 1:
                            mm.then_inc(scored, 1)

                def weigh(b, slot, t, first=False):
                    n, g = FT[t][1], t // TG
                    pe.wait_ge(n_ready, NF * b + (t + 1))
                    if t % TG == 0:
                        pe.wait_ge(pT_ready, NSB * b + (g + 1))
                    if t == 0 and not first:
                        pe.wait_ge(gain_ready, b)
                    split_product(pe, ps[0:T, O0 + slot, :], pT_hi[0:n, g, t % TG, :], pT_lo[0:n, g, t % TG, :],
                                  n_hi[0:n, t % NATURAL_RING, :], n_lo[0:n, t % NATURAL_RING, :], t == 0, t == NF - 1).then_inc(weighed, 1)

                def batch(b, slot, first, last):
                    for t in range(NF):
                        f0, n = FT[t]
                        if not first or t >= 2:
                            pe.wait_ge(n_ready, NF * b + (t - 1))
                        for k in range(NK):
                            mm = pe.transpose(ps[0:n, N0 + t % 2, k * 128:(k + 1) * 128], feats[:, slot, k, f0:f0 + n],
                                              keep["ident"][:, :])
                        mm.then_inc(n_turned, 1)
                        if t in TURN_STEPS:
                            g = TURN_STEPS.index(t)
                            pe.wait_ge(exp_done, NSB * b + min(NSB, g + 1))
                            pe.wait_ge(pT_ready, NSB * b + g)
                            for i in range(TG):
                                g0, rows = FT[g * TG + i]
                                mm = pe.transpose(ps[0:rows, P_BANK, i * T:(i + 1) * T], p[:, g0:g0 + rows],
                                                  keep["ident"][0:T, 0:T])
                            mm.then_inc(p_turned, 1)
                        if t >= SCORES_AT and not last:
                            at = (t - SCORES_AT) * PER_STEP
                            c, start = at // len(SCORE_PRODUCTS), at % len(SCORE_PRODUCTS)
                            scores(b + 1, c, range(start, start + PER_STEP))
                        if t >= WEIGH_LAG:
                            weigh(b, slot, t - WEIGH_LAG, first)
                        elif not first:
                            weigh(b - 1, 1 - slot, NF - WEIGH_LAG + t)

                for c in range(NSB):
                    scores(0, c, range(len(SCORE_PRODUCTS)))
                run(pe, batch)
                for t in range(NF - WEIGH_LAG, NF):
                    weigh(B - 1, (B - 1) % 2, t)


FC = chunk_sizes(FF, 128)
NFC = len(FC)
W_RING, H_RING = 2, 3


def feed_forward(nc, whole, io, keep):
    with ExitStack() as ctx:
        def sb(name, shape, dt=F32):
            return ctx.enter_context(nc.sbuf_tensor("d_" + name, shape, dt))

        def sem(name):
            return whole.enter_context(nc.semaphore("d_" + name))

        x_rows = keep["x_rows"]
        x_nT = [sb(n, [128, NK, NTOK], F32R) for n in ("xnT_hi", "xnT_lo")]
        raw_in = sb("raw_in", [128, W_RING, 2, NK, 128])
        raw_down = sb("raw_down", [128, W_RING, D])
        win_hi, win_lo = (sb(n, [128, NFC, 2, NK, 128], F32R) for n in ("win_hi", "win_lo"))
        loaded = [sem("in%d" % i) for i in range(W_RING)]
        w_hi_ready, w_ready = sem("w_hi"), sem("w")

        def load_weights(sp, f):
            (f0, n), slot = FC[f], f % W_RING
            for i, w in enumerate(("wgT", "wuT")):
                sp.dma_start(raw_in[:, slot, i, :, 0:n], io[w][:, :, f0:f0 + n]).then_inc(loaded[slot], 16)
            sp.dma_start(raw_down[0:n, slot, :], io["wdT"][f0:f0 + n, :]).then_inc(loaded[slot], 16)

        def split_in(pool, f):
            n, slot = FC[f][1], f % W_RING
            pool.wait_ge(w_hi_ready, 2 * f + 1)
            nc.gpsimd.tensor_tensor(win_lo[:, f, :, :, 0:n], raw_in[:, slot, :, :, 0:n],
                                    win_hi[:, f, :, :, 0:n].bitcast(F32), ALU.subtract).then_inc(w_ready, 1)

        def split_down(pool, f):
            n, slot = FC[f][1], f % W_RING
            pool.wait_ge(w_hi_ready, 2 * f + 2)
            nc.gpsimd.tensor_tensor(wd_lo[0:n, f, :], raw_down[0:n, slot, :],
                                    wd_hi[0:n, f, :].bitcast(F32), ALU.subtract).then_inc(w_ready, 1)

        def load_first(sp):
            for f in range(W_RING):
                load_weights(sp, f)

        def round_first(act):
            n = FC[0][1]
            act.wait_ge(loaded[0], 48)
            nc.scalar.activation(win_hi[:, 0, :, :, 0:n], raw_in[:, 0, :, :, 0:n], ACT.Copy).then_inc(w_hi_ready, 1)

        layer_norm_turned(nc, "dn_", keep, 1, x_nT, sync_beside=load_first, scalar_beside=round_first,
                          gpsimd_beside=lambda pool: split_in(pool, 0))
        wd_hi, wd_lo = (sb(n, [128, NFC, D], F32R) for n in ("wd_hi", "wd_lo"))
        h = sb("h", [128, 2, HALF])
        h_hi, h_lo = (sb(n, [128, H_RING, HALF], F32R) for n in ("h_hi", "h_lo"))
        yT = sb("yT", [128, NK, HALF])
        ps = ctx.enter_context(nc.psum_tensor("d_ps", [128, 8, BANK], F32))
        G0, Y0 = 0, 4

        gu_done, gate_ready, h_ready, h_hi_ready, h_lo_ready, down_done = (
            sem(n) for n in ("gu", "gate", "h", "h_hi", "h_lo", "down"))
        y_copied, y_turned, out_ready, stored = (sem(n) for n in ("y", "y_turned", "out_ready", "out"))

        with nc.Block() as block:
            @block.sync
            def _(sp):
                for f in range(W_RING, NFC):
                    sp.wait_ge(w_ready, 2 * (f - W_RING + 1))
                    load_weights(sp, f)
                for b in range(B):
                    sp.wait_ge(out_ready, b + 1)
                    sp.dma_start(io["out4"][b], x_rows[:, b, :]).then_inc(stored, 16)
                sp.wait_ge(stored, 16 * B)

            @block.gpsimd
            def _(pool):
                for f in range(NFC):
                    if f:
                        split_in(pool, f)
                    split_down(pool, f)

            @block.scalar
            def _(act):
                def copy_half(half):
                    for d in range(NK):
                        act.wait_ge(down_done, NFC * (half + 1))
                        act.wait_ge(y_turned, half * (B // 2))
                        nc.scalar.activation(yT[:, d, :], ps[:, Y0 + d, 0:HALF], ACT.Copy).then_inc(y_copied, 1)

                for i in range(2 * NFC):
                    n = FC[i % NFC][1]
                    act.wait_ge(gu_done, i + 1)
                    if i >= 2:
                        act.wait_ge(h_lo_ready, i - 1)
                    nc.scalar.activation(h[0:n, i % 2, :], ps[0:n, G0 + 2 * (i % 2), 0:HALF], ACT.Silu).then_inc(gate_ready, 1)
                    act.wait_ge(h_ready, i + 1)
                    if i >= H_RING:
                        act.wait_ge(down_done, i - H_RING + 1)
                    nc.scalar.activation(h_hi[0:n, i % H_RING, :], h[0:n, i % 2, :], ACT.Copy).then_inc(h_hi_ready, 1)
                    if i == NFC:
                        copy_half(0)
                copy_half(1)

            @block.vector
            def _(dve):
                def round_weights(f):
                    n, slot = FC[f][1], f % W_RING
                    dve.wait_ge(loaded[slot], 48 * (f // W_RING + 1))
                    if f:
                        nc.vector.tensor_copy(win_hi[:, f, :, :, 0:n], raw_in[:, slot, :, :, 0:n]).then_inc(w_hi_ready, 1)
                    nc.vector.tensor_copy(wd_hi[0:n, f, :], raw_down[0:n, slot, :]).then_inc(w_hi_ready, 1)

                def add_half(half):
                    for b in range(half * (B // 2), (half + 1) * (B // 2)):
                        dve.wait_ge(y_turned, b + 1)
                        nc.vector.scalar_tensor_tensor(out=x_rows[:, b, :], in0=ps[0:T, G0 + b % 4, :], scalar=keep["tanh"][0:T, 3:4],
                                                       in1=x_rows[:, b, :], op0=ALU.mult, op1=ALU.add).then_inc(out_ready, 1)

                for f in range(W_RING):
                    round_weights(f)
                for i in range(2 * NFC):
                    n = FC[i % NFC][1]
                    dve.wait_ge(gate_ready, i + 1)
                    nc.vector.tensor_tensor(h[0:n, i % 2, :], ps[0:n, G0 + 2 * (i % 2) + 1, 0:HALF], h[0:n, i % 2, :],
                                            ALU.mult).then_inc(h_ready, 1)
                    dve.wait_ge(h_hi_ready, i + 1)
                    nc.vector.tensor_tensor(h_lo[0:n, i % H_RING, :], h[0:n, i % 2, :], h_hi[0:n, i % H_RING, :].bitcast(F32),
                                            ALU.subtract).then_inc(h_lo_ready, 1)
                    if i + W_RING < NFC:
                        round_weights(i + W_RING)
                    if i == NFC + 1:
                        add_half(0)
                add_half(1)

            @block.tensor
            def _(pe):
                def gate_up(i):
                    half, f, n = i // NFC, i % NFC, FC[i % NFC][1]
                    pe.wait_ge(w_ready, 2 * f + 1)
                    if i >= 2:
                        pe.wait_ge(h_ready, i - 1)
                    cols = slice(half * HALF, (half + 1) * HALF)
                    for j in range(2):
                        for k in range(NK):
                            mm = split_product(pe, ps[0:n, G0 + 2 * (i % 2) + j, 0:HALF], win_hi[:, f, j, k, 0:n], win_lo[:, f, j, k, 0:n],
                                               x_nT[0][:, k, cols], x_nT[1][:, k, cols], k == 0, k == NK - 1)
                    mm.then_inc(gu_done, 1)

                def down(i):
                    f, n = i % NFC, FC[i % NFC][1]
                    pe.wait_ge(w_ready, 2 * f + 2)
                    pe.wait_ge(h_lo_ready, i + 1)
                    for d in range(NK):
                        if i == NFC:
                            pe.wait_ge(y_copied, d + 1)
                        to = slice(d * 128, (d + 1) * 128)
                        mm = split_product(pe, ps[:, Y0 + d, 0:HALF], wd_hi[0:n, f, to], wd_lo[0:n, f, to],
                                           h_hi[0:n, i % H_RING, :], h_lo[0:n, i % H_RING, :], f == 0, f == NFC - 1)
                    mm.then_inc(down_done, 1)

                def turn_back(half):
                    for b in range(half * (B // 2), (half + 1) * (B // 2)):
                        i = b % (B // 2)
                        if i == 0:
                            pe.wait_ge(y_copied, NK * (half + 1))
                            pe.wait_ge(h_ready, NFC + 2 if half == 0 else 2 * NFC)
                        for d in range(NK):
                            mm = pe.transpose(ps[0:T, G0 + i, d * 128:(d + 1) * 128], yT[:, d, i * T:(i + 1) * T], keep["ident"][:, :])
                        mm.then_inc(y_turned, 1)

                for i in range(2 * NFC):
                    if i == NFC + 2:
                        turn_back(0)
                        pe.wait_ge(out_ready, B // 2)
                    gate_up(i)
                    if i:
                        down(i - 1)
                down(2 * NFC - 1)
                turn_back(1)


def flamingo(nc, a, out):
    with ExitStack() as whole:
        def dram(name, shape, dt=F32):
            return nc.dram_tensor(name, shape, dt, kind="Internal").ap()

        def keep_sb(stack, name, shape, dt=F32):
            keep[name] = stack.enter_context(nc.sbuf_tensor("keep_" + name, shape, dt))

        latT = dram("latT_scratch", [128, NK, NTOK])
        q_hi, q_lo = (dram(n, [HD, B, H, T]) for n in ("q_hi_scratch", "q_lo_scratch"))
        rows = {n: dram(n + "_scratch", [NTOK, D]) for n in ("x1", "xn", "yn")}
        io = dict(a)
        io.update(
            latT=latT, latT4=latT.rearrange("p k (b t) -> b p k t", t=T),
            q_hi=q_hi, q_lo=q_lo, q_hi4=q_hi.rearrange("d b h t -> b d h t"), q_lo4=q_lo.rearrange("d b h t -> b d h t"),
            x4=a["x"].rearrange("(b t) d -> b t d", t=T),
            **{n + "_4": r.rearrange("(b t) d -> b t d", t=T) for n, r in rows.items()},
            out4=out.rearrange("(b t) d -> b t d", t=T))
        keep = {"sinkhorn_sems": [whole.enter_context(nc.semaphore("sk_" + n)) for n in SK_SEMS],
                "ln_sems": [whole.enter_context(nc.semaphore("ln_" + n)) for n in LN_SEMS]}
        for n, s in (("ident", [128, 128]), ("gates", [128, 8]), ("tanh", [128, 4]), ("sigmoid", [128, 2])):
            keep_sb(whole, n, s)
        with ExitStack() as early:
            for n, s in (("logits", [T, B * 24]), ("row_max", [T, B, 6]), ("row_sum", [T, B, 6]), ("row_ln", [T, B, 4]),
                         ("h_pp", [T, B, 2, 4]), ("log_res", [T, B, 4, 4]), ("sink", [T, B, 4, 4]), ("pairs", [T, B, 8]),
                         ("marginal", [T, B, 4]), ("inverse", [T, B, 4])):
                keep_sb(whole, n, s)
            for n in ("wk_hi", "wk_lo", "wv_hi", "wv_lo"):
                keep_sb(early, n, [128, NK, KV * HD], F32R)
            keep_sb(early, "raw", [128, NK, CHUNK_MAX])
            for n in ("c_hi", "c_lo"):
                keep_sb(early, n, [128, 2, NK, CHUNK_MAX], F32R)
            for n in ("raw_loaded", "chunk_hi", "chunk_ready"):
                keep[n] = whole.enter_context(nc.semaphore(n))
            project_queries(nc, whole, io, keep)
            attend_context(nc, whole, io, keep)
        keep_sb(whole, "x_rows", [T, B, D])
        with ExitStack() as late:
            for n in ("bq1", "bk1"):
                keep_sb(late, n, [128, NK])
            keep_sb(late, "queries", [128, NK, NTOK])
            keep_sb(late, "qbk", [T, B])
            keep_sb(late, "feats", [128, 2, NK, CTX])
            keep["feats_loaded"] = [whole.enter_context(nc.semaphore("feats_loaded%d" % c)) for c in range(NSB)]
            with ExitStack() as weights:
                for n in ("wq1_hi", "wq1_lo", "wk1_hi", "wk1_lo"):
                    keep_sb(weights, n, [128, NK, D], F32R)
                hyper_connection(nc, whole, io, keep)
                project_features(nc, whole, io, keep)
            attend_features(nc, whole, io, keep)
        feed_forward(nc, whole, io, keep)


def kernel(x, ctx_4096, g_xattn, g_ffn, L0_xattn_Wq, L0_xattn_Wk, L0_xattn_Wv, L0_xattn_Wo, L0_ffn_W_res,
           L0_ffn_W_pre, L0_ffn_W_post, L0_ffn_H_res_base, L0_ffn_H_pre_base, L0_ffn_H_post_base, L0_ffn_gate,
           L0_ffn_W_branch, L1_xattn_Wq, L1_xattn_bq, L1_xattn_Wk, L1_xattn_bk, L1_ffn_W_gate, L1_ffn_W_up,
           L1_ffn_W_down):
    import numpy as np
    import concourse.bacc as bacc
    from concourse.bass_utils import run_bass_kernel_spmd

    def by_k(w):
        w = np.asarray(w)
        return np.ascontiguousarray(w.T.reshape(w.shape[1] // 128, 128, w.shape[0]).transpose(1, 0, 2))

    def column(v):
        return np.ascontiguousarray(np.asarray(v).reshape(-1, 128).T)

    flat = [np.asarray(v).reshape(-1) for v in (g_xattn, g_ffn, L0_ffn_gate)]
    packed = np.concatenate([np.r_[i * HD:(i + 1) * HD, 3 * HD + 32 * i:3 * HD + 32 * (i + 1)] for i in range(KV - 1)])
    arrays = {
        "x": np.asarray(x).reshape(NTOK, D),
        "ctxT": np.ascontiguousarray(np.asarray(ctx_4096).transpose(0, 2, 1).reshape(B, NK, 128, CTX).transpose(0, 2, 1, 3)),
        "gates": np.concatenate(flat).reshape(1, 5),
        "wqT": by_k(L0_xattn_Wq), "wkT": by_k(np.asarray(L0_xattn_Wk)[packed]), "wvT": by_k(L0_xattn_Wv),
        "woT": np.ascontiguousarray(np.asarray(L0_xattn_Wo).T.reshape(H, HD, D).transpose(1, 0, 2)),
        "whT": by_k(np.concatenate([np.asarray(w) for w in (L0_ffn_W_res, L0_ffn_W_pre, L0_ffn_W_post)])),
        "h_base": np.concatenate([np.asarray(v).reshape(-1) for v in
                                  (L0_ffn_H_res_base, L0_ffn_H_pre_base, L0_ffn_H_post_base)]).reshape(1, 24),
        "w_branch": np.asarray(L0_ffn_W_branch),
        "wq1T": by_k(L1_xattn_Wq), "wk1": np.ascontiguousarray(np.asarray(L1_xattn_Wk).reshape(NK, 128, D).transpose(1, 0, 2)),
        "bq1": column(L1_xattn_bq), "bk1": column(L1_xattn_bk),
        "wgT": by_k(L1_ffn_W_gate), "wuT": by_k(L1_ffn_W_up),
        "wdT": np.ascontiguousarray(np.asarray(L1_ffn_W_down).T),
    }
    nc = bacc.Bacc("TRN2", target_bir_lowering=False, num_devices=1)
    maps, aps = {}, {}
    for name, a in arrays.items():
        maps[f"in_{name}"] = a
        aps[name] = nc.dram_tensor(f"in_{name}", a.shape, mybir.dt.from_np(a.dtype), kind="ExternalInput").ap()
    out = nc.dram_tensor("out_0", (NTOK, D), F32, kind="ExternalOutput").ap()
    flamingo(nc, aps, out)
    r = run_bass_kernel_spmd(nc, [maps], core_ids=[0])
    return r.results[0]["out_0"].reshape(B, T, D)
```

```python
from contextlib import ExitStack

import concourse.bass as bass
from concourse import mybir

ALU = mybir.AluOpType
ACT = mybir.ActivationFunctionType
AX = mybir.AxisListType
F32 = mybir.dt.float32
F32R = mybir.dt.float32r

B, T, D, CTX = 8, 100, 512, 1444
H, KV, HD = 16, 4, 96
G = H // KV
STREAMS, SW = 4, 128
SINKHORN_STEPS, TAU = 50, 0.1
RMS_EPS, LN_EPS = 1.1920929e-07, 1e-05
FF = 1376
NTOK = B * T
NK = D // 128
HALF = NTOK // 2
BANK = 512


def split_product(pe, out, a_hi, a_lo, b_hi, b_lo, start, stop):
    pe.matmul(out, a_hi, b_hi, start=start, stop=False)
    pe.matmul(out, a_hi, b_lo, start=False, stop=False)
    return pe.matmul(out, a_lo, b_hi, start=False, stop=stop)


def chunk_sizes(n, size):
    return [(i, min(size, n - i)) for i in range(0, n, size)]


def layer_norm_stats(nc, dve, link, stats, mv, var, x_of, loaded, eps):
    for b in range(B):
        dve.wait_ge(loaded, 16 * (b + 1))
        link(nc.vector.bn_stats(stats[:, b, :], x_of(b)))
        link(nc.vector.bn_aggr(mv[:, b, :], stats[:, b, :]))
    return link(nc.vector.tensor_scalar(var, mv[:, :, 1], eps, None, ALU.add))


def refined_rsqrt(nc, link, rstd, sd, var, tmp):
    link(nc.vector.reciprocal(rstd, sd))
    link(nc.vector.tensor_tensor(tmp, rstd, rstd, ALU.mult))
    link(nc.vector.tensor_tensor(tmp, tmp, var, ALU.mult))
    link(nc.vector.tensor_scalar(tmp, tmp, -0.5, 1.5, ALU.mult, ALU.add))
    link(nc.vector.tensor_tensor(rstd, rstd, tmp, ALU.mult))


NKEY = CTX + T
KEY_TILES = [(128 * i, 128) for i in range(11)] + [(1408, 68), (1476, 68)]
NT = len(KEY_TILES)
CHUNKS = [(256 * c, 256, 2 * c, 2) for c in range(5)] + [(1280, 264, 10, 3)]
NCH = len(CHUNKS)
CHUNK_MAX = max(n for _, n, _, _ in CHUNKS)
KG = KV - 1
GROUP_OF = [(c, i) for c in range(NCH) for i in range(KG + CHUNKS[c][3])]
GROUPS = len(GROUP_OF)
FIRST_GROUP = [GROUP_OF.index((c, 0)) for c in range(NCH)] + [GROUPS]
PIECES_BEFORE = [sum(2 if i < KG else 1 for _, i in GROUP_OF[:g]) for g in range(GROUPS + 1)]
PIECES = PIECES_BEFORE[GROUPS]
STEPS = KV * NT
RING = 3
LAG = 3
TURN_AT, SPREAD_AT, OUT_AT, MAX_ROW_AT = 5, 7, 9, 10
NEGATE_AT = 8
COPY_AT, ROW_COPY_AT = 3, 10
END_TURN, END_SPREAD, END_OUT = 1, 2, 4
PAIRS = [tuple(range(h, h + 2)) for h in range(0, H, 2)]
SINGLES = [(h,) for h in range(H)]
UNITS = [PAIRS if 2 * n <= BANK else SINGLES for _, n, _, _ in CHUNKS]
PAIRS_AT = {(1, 1): (0,), (1, 3): (1,), (2, 2): (2,), (3, 0): (3,), (3, 2): (4,), (4, 0): (5,), (4, 1): (6,), (4, 3): (7,)}
SINGLES_AT = {(1, 1): (0,), (1, 2): (1,), (1, 3): (2,), (2, 1): (3,), (2, 2): (4,), (2, 3): (5,), (3, 0): (6,), (3, 1): (7,),
              (3, 2): (8, 9), (3, 3): (10,), (4, 0): (11,), (4, 1): (12,), (4, 2): (13, 14), (4, 3): (15,)}
ROUGH_AT = [PAIRS_AT if units is PAIRS else SINGLES_AT for units in UNITS]
MAXIMA_BEFORE = [sum(len(units) for units in UNITS[:c]) for c in range(NCH + 1)]
MAXIMA = MAXIMA_BEFORE[NCH]
ROUND_AFTER = {FIRST_GROUP[c + 1] - 1: c + 2 for c in range(NCH - 2)}
AHEAD = (6, 14)
HY_RESIDUAL, HY_STATS, HY_RSTD, HY_NORM, HY_TURN, HY_COPY, HY_LOGITS, HY_MEAN, HY_YN, HY_RSTD2, HY_LOGIT_ROWS = (
    5, 9, 10, 14, 17, 18, 19, 20, 20, 21, 24)
OP_STATS, OP_NEWTON, OP_NEWTON2, HYPER_OPS = 0, 2, 6, 10
EARLY = B - 2
SK_ROWS, SK_EXP, SK_SUMS, SK_LN, SK_COLS, SK_EXP2, SK_START = 25, 26, 27, 28, 29, 30, 31
NORMS = 1 + 2 * (SINKHORN_STEPS - 1)
SK_GROUPS = [("group", b, gi) for b in (B - 2, B - 1) for gi in range(GROUPS)
             if (b, gi) >= (B - 2, SK_START) and gi not in ROUND_AFTER]
IN_TILES = NORMS - len(SK_GROUPS)
SK_TILES = [("tile", B - 2 + s // STEPS, s % STEPS) for s in (i * (2 * STEPS - 2) // IN_TILES for i in range(IN_TILES))]
SK_SLOTS = sorted(SK_GROUPS + SK_TILES, key=lambda slot: (slot[1], slot[0], slot[2]))
assert len(SK_SLOTS) == NORMS
assert sum(n for _, n in KEY_TILES) == NKEY


def load_chunk(sp, io, keep, b, c):
    k0, n, _, _ = CHUNKS[c]
    own = min(n, CTX - k0)
    if not (isinstance(b, int) and b + c == 0):
        sp.wait_ge(keep["chunk_ready"], NCH * b + c)
    sp.dma_start(keep["raw"][:, :, 0:own], io["ctxT"][b, :, :, k0:k0 + own]).then_inc(keep["raw_loaded"], 16)
    if own < n:
        sp.dma_start(keep["raw"][:, :, own:n], io["latT4"][b]).then_inc(keep["raw_loaded"], 16)


def round_chunk(nc, dve, keep, b, c):
    loads = NCH + 1
    n, slot = CHUNKS[c][1], c % 2
    dve.wait_ge(keep["raw_loaded"], 16 * loads * b + 16 * (loads if c == NCH - 1 else c + 1))
    nc.vector.tensor_copy(keep["c_hi"][:, slot, :, 0:n], keep["raw"][:, :, 0:n]).then_inc(keep["chunk_hi"], 1)


def split_chunk(nc, pool, keep, b, c):
    n, slot = CHUNKS[c][1], c % 2
    pool.wait_ge(keep["chunk_hi"], NCH * b + (c + 1))
    nc.gpsimd.tensor_tensor(keep["c_lo"][:, slot, :, 0:n], keep["raw"][:, :, 0:n],
                            keep["c_hi"][:, slot, :, 0:n].bitcast(F32), ALU.subtract).then_inc(keep["chunk_ready"], 1)

SK_SEMS = ("chain", "z", "kept", "e", "sums", "ln", "m", "e2", "pairs", "marginal", "inverse", "norm")
SK_LINKS = 7


class Sinkhorn:

    def __init__(self, keep, turn, first, last):
        part, n = slice(first, last), last - first
        self.n, self.tanh = n, keep["tanh"][0:T, 2:3]
        self.z = keep["logits"][:, first * 24:last * 24].rearrange("p (b i j) -> p b i j", i=6, j=4)
        self.zf = keep["logits"][:, first * 24:last * 24].rearrange("p (b n) -> p b n", n=24)
        self.row_max, self.row_sum, self.row_ln = (keep[k][:, part, :] for k in ("row_max", "row_sum", "row_ln"))
        self.h_pp, self.log_res, self.sink = (keep[k][:, part, :, :] for k in ("h_pp", "log_res", "sink"))
        self.pairs, self.marginal, self.inverse = (keep[k][:, part, :] for k in ("pairs", "marginal", "inverse"))
        (self.chain, self.z_ready, self.kept, self.e_ready, self.sums_ready, self.ln_ready, self.m_ready, self.e2_ready,
         self.pairs_ready, self.marginal_ready, self.inverse_ready, self.norm_done) = keep["sinkhorn_sems"]
        self.turn, self.links = turn, SK_LINKS * turn

    def link(self, dve, ins):
        self.links += 1
        ins.then_inc(self.chain, 1)
        dve.wait_ge(self.chain, self.links)

    def along_rows(self, v):
        return v.unsqueeze(3).to_broadcast([T, self.n, v.shape[2], 4])

    def along_cols(self, v):
        return v.unsqueeze(2).to_broadcast([T, self.n, 4, 4])

    def softmax_rows(self, nc, dve, at):
        if at == SK_ROWS:
            self.link(dve, nc.vector.tensor_scalar(self.zf[:, :, 0:16], self.zf[:, :, 0:16], 1.0 / TAU, None, ALU.mult))
            self.link(dve, nc.vector.tensor_reduce(self.row_max, self.z, AX.X, ALU.max))
            nc.vector.tensor_tensor(self.z, self.z, self.along_rows(self.row_max), ALU.subtract).then_inc(self.z_ready, 1)
            dve.wait_ge(self.z_ready, self.turn + 1)
            nc.vector.tensor_copy(self.log_res, self.z[:, :, 0:4, :]).then_inc(self.kept, 1)
        if at == SK_SUMS:
            dve.wait_ge(self.e_ready, self.turn + 1)
            nc.vector.tensor_reduce(self.row_sum, self.z, AX.X, ALU.add).then_inc(self.sums_ready, 1)
            dve.wait_ge(self.sums_ready, self.turn + 1)
            self.link(dve, nc.vector.reciprocal(self.row_max[:, :, 4:6], self.row_sum[:, :, 4:6]))
            self.link(dve, nc.vector.tensor_tensor(self.h_pp, self.z[:, :, 4:6, :], self.along_rows(self.row_max[:, :, 4:6]), ALU.mult))
            self.link(dve, nc.vector.tensor_scalar(self.h_pp[:, :, 1, :], self.h_pp[:, :, 1, :], self.tanh, None, ALU.mult))
        if at == SK_COLS:
            dve.wait_ge(self.ln_ready, self.turn + 1)
            self.link(dve, nc.vector.tensor_tensor(self.log_res, self.log_res, self.along_rows(self.row_ln), ALU.subtract))
            self.link(dve, nc.vector.tensor_reduce(self.marginal, self.log_res.rearrange("p b i j -> p b j i"), AX.X, ALU.max))
            nc.vector.tensor_tensor(self.log_res, self.log_res, self.along_cols(self.marginal), ALU.subtract).then_inc(self.m_ready, 1)

    def exponentials(self, nc, act, at):
        if at == SK_EXP:
            act.wait_ge(self.kept, self.turn + 1)
            nc.scalar.activation(self.z, self.z, ACT.Exp).then_inc(self.e_ready, 1)
        if at == SK_LN:
            act.wait_ge(self.sums_ready, self.turn + 1)
            nc.scalar.activation(self.row_ln, self.row_sum[:, :, 0:4], ACT.Ln).then_inc(self.ln_ready, 1)
        if at == SK_EXP2:
            act.wait_ge(self.m_ready, self.turn + 1)
            nc.scalar.activation(self.sink, self.log_res, ACT.Exp).then_inc(self.e2_ready, 1)

    def normalise(self, nc, pool, n):
        if n == 0:
            pool.wait_ge(self.e2_ready, self.turn + 1)
        else:
            pool.wait_ge(self.norm_done, n)
        if n % 2 == 0:
            halves = self.sink[:, :, 0:2, :], self.sink[:, :, 2:4, :]
            pairs = self.pairs.rearrange("p b (i j) -> p b i j", j=4)
            ends, inverses = (pairs[:, :, 0, :], pairs[:, :, 1, :]), self.along_cols(self.inverse)
        else:
            halves = self.sink[:, :, :, 0:2], self.sink[:, :, :, 2:4]
            pairs = self.pairs.rearrange("p b (i j) -> p b i j", j=2)
            ends, inverses = (pairs[:, :, :, 0], pairs[:, :, :, 1]), self.along_rows(self.inverse)
        nc.gpsimd.tensor_tensor(pairs, halves[0], halves[1], ALU.add).then_inc(self.pairs_ready, 1)
        pool.wait_ge(self.pairs_ready, n + 1)
        nc.gpsimd.tensor_tensor(self.marginal, ends[0], ends[1], ALU.add).then_inc(self.marginal_ready, 1)
        pool.wait_ge(self.inverse_ready, n + 1)
        nc.gpsimd.tensor_tensor(self.sink, self.sink, inverses, ALU.mult).then_inc(self.norm_done, 1)

    def invert(self, nc, dve, n):
        dve.wait_ge(self.marginal_ready, n + 1)
        nc.vector.reciprocal(self.inverse, self.marginal).then_inc(self.inverse_ready, 1)


WB = 4
BH = H // WB
Q_GROUPS = [(h, half) for block in range(WB) for half in range(2) for h in range(block * BH, (block + 1) * BH)]


def project_queries(nc, whole, io, keep):
    with ExitStack() as ctx:
        def sb(name, shape, dt=F32):
            return ctx.enter_context(nc.sbuf_tensor(name, shape, dt))

        def sem(name):
            return whole.enter_context(nc.semaphore(name))

        x_rows = sb("q_x", [T, B, D])
        xnT = sb("q_xnT", [128, NK, NTOK])
        xnT_hi = sb("q_xnT_hi", [128, NK, NTOK], F32R)
        xnT_lo = sb("q_xnT_lo", [128, NK, NTOK], F32R)
        wq = sb("q_wq", [128, NK, H * HD])
        wq_hi = sb("q_wq_hi", [128, NK, H * HD], F32R)
        wq_lo = sb("q_wq_lo", [128, NK, H * HD], F32R)
        wkv = sb("q_wkv", [128, 2, NK, KV * HD])
        QR = 4
        q_hi = sb("q_q_hi", [HD, QR, HALF], F32R)
        q_lo = sb("q_q_lo", [HD, QR, HALF], F32R)
        stats = sb("q_stats", [T, B, 6])
        mv = sb("q_mv", [T, B, 2])
        var, sd, rstd, tmp = (sb("q_" + n, [T, B]) for n in ("var", "sd", "rstd", "tmp"))
        ps = ctx.enter_context(nc.psum_tensor("q_ps", [128, 8, BANK], F32))

        x_loaded = [sem("q_x_in%d" % i) for i in range(2)]
        wq_loaded = [sem("q_wq_in%d" % k) for k in range(WB)]
        wkv_loaded, small_loaded = sem("q_wkv_in"), sem("q_small_in")
        step, var_ready, sd_ready, xn_ready = (sem("q_" + n) for n in ("step", "var", "sd", "xn"))
        ident_ready, turned, xnT_ready, xnT_hi_ready, xnT_lo_ready = (
            sem("q_" + n) for n in ("ident", "turned", "xnT", "xnT_hi", "xnT_lo"))
        stats_ready, aggregated = sem("q_stats"), sem("q_aggr")
        wq_hi_ready, wkv_hi_ready, wkv_lo_ready = (sem("q_" + n) for n in ("wqh", "wkvh", "wkvl"))
        wq_lo_ready = [sem("q_wql%d" % i) for i in range(2)]
        q_done, q_hi_ready, q_lo_ready, lat_stored, gate_ready = (
            sem("q_" + n) for n in ("done", "qh", "ql", "lat", "gate"))
        q_stored = [sem(f"q_stored{i}") for i in range(QR)]

        def block_cols(j):
            return slice(j * BH * HD, (j + 1) * BH * HD)

        with nc.Block() as block:
            @block.sync
            def _(sp):
                def load_x(i):
                    part = slice(i * (B // 2), (i + 1) * (B // 2))
                    sp.dma_start(x_rows[:, part, :], io["x4"][part].rearrange("b t d -> t b d")).then_inc(x_loaded[i], 16)

                load_x(0)
                for j in range(WB):
                    sp.dma_start(wq[:, :, block_cols(j)], io["wqT"][:, :, block_cols(j)]).then_inc(wq_loaded[j], 16)
                    if j == 0:
                        load_x(1)
                load_chunk(sp, io, keep, 0, 0)
                sp.dma_start(wkv[:, 0, :, :], io["wkT"]).then_inc(wkv_loaded, 16)
                sp.dma_start(wkv[:, 1, :, :], io["wvT"]).then_inc(wkv_loaded, 16)
                sp.wait_ge(xnT_ready, B)
                sp.dma_start(io["latT"], xnT[:, :, :]).then_inc(lat_stored, 16)
                for i in range(2 * H):
                    (h, half), slot = Q_GROUPS[i], i % QR
                    if i == H:
                        load_chunk(sp, io, keep, 0, 1)
                    sp.wait_ge(q_lo_ready, i + 1)
                    for q, to in ((q_hi, io["q_hi"]), (q_lo, io["q_lo"])):
                        sp.dma_start(to[:, half * (B // 2):(half + 1) * (B // 2), h, :],
                                     q[:, slot, :].bitcast(F32).rearrange("d (b t) -> d b t", t=T)).then_inc(q_stored[slot], 16)
                sp.wait_ge(small_loaded, 16)
                sp.wait_ge(lat_stored, 16)
                for i in range(QR):
                    sp.wait_ge(q_stored[i], 32 * (2 * H // QR))

            @block.gpsimd
            def _(pool):
                nc.gpsimd.memset(keep["ident"][:, :], 0.0).then_inc(ident_ready, 1)
                pool.wait_ge(ident_ready, 1)
                nc.gpsimd.affine_select(out=keep["ident"][:, :], in_=keep["ident"][:, :], compare_op=ALU.not_equal,
                                        fill=1.0, base=0, pattern=[[-1, 128]], channel_multiplier=1).then_inc(ident_ready, 1)
                for j in (0, 2):
                    pool.wait_ge(wq_hi_ready, j + 1)
                    nc.gpsimd.tensor_tensor(wq_lo[:, :, block_cols(j)], wq[:, :, block_cols(j)],
                                            wq_hi[:, :, block_cols(j)].bitcast(F32), ALU.subtract).then_inc(wq_lo_ready[0], 1)
                pool.wait_ge(wkv_loaded, 32)
                for i, name in enumerate(("wk", "wv")):
                    nc.gpsimd.tensor_copy(keep[name + "_hi"][:, :, :], wkv[:, i, :, :]).then_inc(wkv_hi_ready, 1)
                    pool.wait_ge(wkv_hi_ready, i + 1)
                    nc.gpsimd.tensor_tensor(keep[name + "_lo"][:, :, :], wkv[:, i, :, :],
                                            keep[name + "_hi"][:, :, :].bitcast(F32), ALU.subtract).then_inc(wkv_lo_ready, 1)
                    split_chunk(nc, pool, keep, 0, i)

            @block.scalar
            def _(act):
                act.dma_start(keep["gates"][:, 0:5], io["gates"].partition_broadcast(128)).then_inc(small_loaded, 16)
                def root(i):
                    part = slice(i * (B // 2), (i + 1) * (B // 2))
                    act.wait_ge(var_ready, i + 1)
                    nc.scalar.activation(sd[:, part], var[:, part], ACT.Sqrt).then_inc(sd_ready, 1)

                root(0)
                def round_block(j):
                    act.wait_ge(wq_loaded[j], 16)
                    nc.scalar.activation(wq_hi[:, :, block_cols(j)], wq[:, :, block_cols(j)], ACT.Copy).then_inc(wq_hi_ready, 1)

                round_block(0)
                for b in range(B):
                    if b == B // 2:
                        root(1)
                        round_block(1)
                        round_block(2)
                    act.wait_ge(turned, b + 1)
                    nc.scalar.activation(xnT[:, :, b * T:(b + 1) * T],
                                         ps[:, b % 2, 0:NK * T].rearrange("p (k t) -> p k t", t=T),
                                         ACT.Copy).then_inc(xnT_ready, 1)
                round_block(3)
                act.wait_ge(small_loaded, 16)
                nc.scalar.activation(keep["tanh"][:, 0:4], keep["gates"][:, 0:4], ACT.Tanh).then_inc(gate_ready, 1)
                nc.scalar.activation(keep["gates"][:, 5:6], keep["gates"][:, 4:5], ACT.Exp, scale=-1.0).then_inc(gate_ready, 1)
                for i in range(2 * H):
                    act.wait_ge(q_done, i + 1)
                    if i >= QR:
                        act.wait_ge(q_stored[i % QR], 32 * (i // QR))
                    nc.scalar.activation(q_hi[:, i % QR, :], ps[0:HD, 2 + i % 4, 0:HALF], ACT.Copy).then_inc(q_hi_ready, 1)

            @block.vector
            def _(dve):
                done = [0]

                def link(ins):
                    done[0] += 1
                    ins.then_inc(step, 1)
                    dve.wait_ge(step, done[0])

                def split_latents(batches):
                    for b in batches:
                        cols = slice(b * T, (b + 1) * T)
                        dve.wait_ge(xnT_ready, b + 1)
                        nc.vector.tensor_copy(xnT_hi[:, :, cols], xnT[:, :, cols]).then_inc(xnT_hi_ready, 1)
                        dve.wait_ge(xnT_hi_ready, b + 1)
                        nc.vector.tensor_tensor(xnT_lo[:, :, cols], xnT[:, :, cols], xnT_hi[:, :, cols].bitcast(F32),
                                                ALU.subtract).then_inc(xnT_lo_ready, 1)

                for i in range(2):
                    part = slice(i * (B // 2), (i + 1) * (B // 2))
                    dve.wait_ge(x_loaded[i], 16)
                    for b in range(part.start, part.stop):
                        nc.vector.bn_stats(stats[:, b, :], x_rows[:, b, :]).then_inc(stats_ready, 1)
                    for b in range(part.start, part.stop):
                        dve.wait_ge(stats_ready, b + 1)
                        nc.vector.bn_aggr(mv[:, b, :], stats[:, b, :]).then_inc(aggregated, 1)
                    dve.wait_ge(aggregated, part.stop)
                    nc.vector.tensor_scalar(var[:, part], mv[:, part, 1], LN_EPS, None, ALU.add).then_inc(var_ready, 1)
                    dve.wait_ge(var_ready, i + 1)
                    dve.wait_ge(sd_ready, i + 1)
                    refined_rsqrt(nc, link, rstd[:, part], sd[:, part], var[:, part], tmp[:, part])
                    for b in range(part.start, part.stop):
                        nc.vector.tensor_scalar(x_rows[:, b, :], x_rows[:, b, :], mv[:, b, 0:1], rstd[:, b:b + 1],
                                                ALU.subtract, ALU.mult).then_inc(xn_ready, 1)
                    split_latents(range(part.start, part.stop))
                for i in range(2 * H):
                    if i in (BH, 3 * BH):
                        j = i // BH
                        dve.wait_ge(wq_hi_ready, j + 1)
                        nc.vector.tensor_tensor(wq_lo[:, :, block_cols(j)], wq[:, :, block_cols(j)],
                                                wq_hi[:, :, block_cols(j)].bitcast(F32), ALU.subtract).then_inc(wq_lo_ready[1], 1)
                    if i in (H // 2, H):
                        round_chunk(nc, dve, keep, 0, 0 if i < H else 1)
                    dve.wait_ge(q_hi_ready, i + 1)
                    nc.vector.tensor_tensor(q_lo[:, i % QR, :], ps[0:HD, 2 + i % 4, 0:HALF],
                                            q_hi[:, i % QR, :].bitcast(F32), ALU.subtract).then_inc(q_lo_ready, 1)
                dve.wait_ge(gate_ready, 2)
                link(nc.vector.tensor_scalar(keep["gates"][:, 6:7], keep["gates"][:, 5:6], 1.0, None, ALU.add))
                link(nc.vector.reciprocal(keep["sigmoid"][:, 0:1], keep["gates"][:, 6:7]))
                link(nc.vector.tensor_scalar(keep["sigmoid"][:, 1:2], keep["sigmoid"][:, 0:1], -1.0, 1.0, ALU.mult, ALU.add))

            @block.tensor
            def _(pe):
                def turn(batches):
                    for b in batches:
                        pe.wait_ge(xn_ready, b + 1)
                        if b >= 2:
                            pe.wait_ge(xnT_ready, b - 1)
                        for k in range(NK):
                            mm = pe.transpose(ps[:, b % 2, k * T:(k + 1) * T], x_rows[:, b, k * 128:(k + 1) * 128],
                                              keep["ident"][0:T, 0:T])
                        mm.then_inc(turned, 1)

                pe.wait_ge(ident_ready, 2)
                turn(range(B // 2))
                for i in range(2 * H):
                    h, half = Q_GROUPS[i]
                    j = h // BH
                    if i == BH // 2:
                        turn(range(B // 2, B))
                    pe.wait_ge(xnT_lo_ready, (half + 1) * (B // 2) if i < 2 * BH else B)
                    pe.wait_ge(wq_lo_ready[j % 2], j // 2 + 1)
                    if i >= 4:
                        pe.wait_ge(q_lo_ready, i - 3)
                    for k in range(NK):
                        w, t = slice(h * HD, (h + 1) * HD), slice(half * HALF, (half + 1) * HALF)
                        mm = split_product(pe, ps[0:HD, 2 + i % 4, 0:HALF], wq_hi[:, k, w], wq_lo[:, k, w],
                                           xnT_hi[:, k, t], xnT_lo[:, k, t], k == 0, k == NK - 1)
                    mm.then_inc(q_done, 1)


def attend_context(nc, whole, io, keep):
    scale = float(HD) ** -0.5
    with ExitStack() as ctx:
        def sb(name, shape, dt=F32):
            return ctx.enter_context(nc.sbuf_tensor(name, shape, dt))

        def sem(name):
            return whole.enter_context(nc.semaphore("a_" + name))

        c_hi, c_lo = keep["c_hi"], keep["c_lo"]
        k_hi = sb("a_k_hi", [HD + 1, KV, NKEY], F32R)
        k_lo = sb("a_k_lo", [HD + 1, KV, NKEY], F32R)
        v_hi = sb("a_v_hi", [128, NT, KV, HD + 1], F32R)
        v_lo = sb("a_v_lo", [128, NT, KV, HD + 1], F32R)
        q_hi = sb("a_q_hi", [HD + 1, H, T], F32R)
        q_lo = sb("a_q_lo", [HD + 1, H, T], F32R)
        p = sb("a_p", [128, 2, G * T])
        p_hi = sb("a_p_hi", [128, RING, G * T], F32R)
        p_lo = sb("a_p_lo", [128, RING, G * T], F32R)
        maxima = sb("a_max", [T, H, NCH])
        head_max = sb("a_hmax", [T, G])
        neg_max = sb("a_nmax", [T, G, HD + 1])
        ones = sb("a_ones", [128, HD])
        recip = sb("a_recip", [T, G])
        diag = sb("a_diag", [T, G, T])
        o_sb = sb("a_o", [HD + 1, G * T])
        x_rows = sb("a_x", [T, D])
        xn = sb("h_xn", [T, D])
        xnT = sb("h_xnT", [128, NK, T])
        yn = sb("h_yn", [T, STREAMS, SW])
        w_h = sb("h_w", [128, NK, 24])
        w_branch = sb("h_wb", [SW, SW])
        h_base = sb("h_base", [T, 24])
        stats, mv = sb("h_stats", [T, 6]), sb("h_mv", [T, 2])
        var, root, newton_t, rstd, square_sum, mean_sq, rstd2 = (sb("h_s%d" % i, [T, 1]) for i in range(7))
        wo = sb("a_wo", [HD, H, D])
        ps = ctx.enter_context(nc.psum_tensor("a_ps", [128, 8, BANK], F32))
        S0, M0, O_BANK, B_BANK, Y_BANK = 0, 3, 5, 6, 7
        LOGITS = G * T + 8

        chunk_ready = keep["chunk_ready"]
        preset, pool_preset, wo_loaded = (sem(n) for n in ("preset", "pool_preset", "wo_in"))
        q_loaded, q_last_loaded, x_loaded, x1_ready, stored = (sem(n) for n in ("q_in", "q_last_in", "x_in", "x1", "stored"))
        proj_done, proj_hi, proj_lo = sem("proj"), sem("proj_hi"), sem("proj_lo")
        rough_done, rough_max, max_ready, neg_ready, row_placed, row_ready = (
            sem(n) for n in ("rough", "rough_max", "max", "neg", "row_placed", "row"))
        scores, exp_done, p_hi_ready, p_lo_ready, pv_done = (sem(n) for n in ("scores", "exp", "p_hi", "p_lo", "pv"))
        o_copied, sums_turned, recip_ready, diag_ready, spread, normal, wo_done = (
            sem(n) for n in ("o_copied", "turned", "recip", "diag", "spread", "normal", "wo"))

        weights_in, hyper, settled, var_ready, root_ready, xn_ready, x_turned, xnT_ready, square_ready = (
            sem("h_" + n) for n in ("w_in", "ops", "settled", "var", "root", "xn", "xturn", "xnT", "sq"))
        mean_ready, root2_ready, logits_done, branch_done, yn_ready, logit_rows_ready = (
            sem("h_" + n) for n in ("mean", "root2", "logits", "branch", "yn", "z"))
        sk = Sinkhorn(keep, 0, 0, EARLY)

        def o_bank(kv):
            return O_BANK if kv % 2 else M0 + 1

        def group_pieces(gi):
            c, i = GROUP_OF[gi]
            k0, n, t0, _ = CHUNKS[c]
            bank = ps[:, M0 + gi % 3, :]
            if i < KG:
                keys, last = slice(k0, k0 + n), slice(32 * i, 32 * (i + 1))
                return [(bank[0:HD, 0:n], k_hi[0:HD, i, keys], k_lo[0:HD, i, keys]),
                        (bank[HD:128, 0:n], k_hi[last, KV - 1, keys], k_lo[last, KV - 1, keys])]
            t = t0 + i - KG
            rows = KEY_TILES[t][1]
            return [(bank[0:rows, 0:KV * HD].rearrange("p (h d) -> p h d", d=HD), v_hi[0:rows, t, :, 0:HD], v_lo[0:rows, t, :, 0:HD])]

        with nc.Block() as block:
            @block.sync
            def _(sp):
                def load_queries(b, first=False):
                    for heads, loaded, after in ((slice(0, H - G), q_loaded, STEPS * b - NT), (slice(H - G, H), q_last_loaded, STEPS * b)):
                        if not first:
                            sp.wait_ge(scores, after)
                        for q, name in ((q_hi, "q_hi4"), (q_lo, "q_lo4")):
                            sp.dma_start(q[0:HD, heads, :].bitcast(F32), io[name][b, :, heads, :]).then_inc(loaded, 16)

                def store(b, ready, what, to):
                    sp.wait_ge(ready, b + 1)
                    sp.dma_start(to[b], what).then_inc(stored, 16)

                def batch(b, first, last):
                    load_chunk(sp, io, keep, b, 2)
                    if not first:
                        store(b - 1, x1_ready, x_rows[:, :], io["x1_4"])
                    load_chunk(sp, io, keep, b, 3)
                    load_chunk(sp, io, keep, b, 4)
                    if not first:
                        store(b - 1, xn_ready, xn[:, :], io["xn_4"])
                    load_chunk(sp, io, keep, b, NCH - 1)
                    if not first:
                        store(b - 1, yn_ready, yn[:, :, :].rearrange("p n c -> p (n c)"), io["yn_4"])
                        sp.wait_ge(stored, 48 * b)
                    sp.dma_start(x_rows[:, :], io["x4"][b]).then_inc(x_loaded, 16)
                    if first:
                        sp.dma_start(wo[:, :, :], io["woT"]).then_inc(wo_loaded, 16)
                        sp.dma_start(w_h[:, :, :], io["whT"]).then_inc(weights_in, 16)
                        sp.dma_start(w_branch[:, :], io["w_branch"]).then_inc(weights_in, 16)
                        sp.dma_start(h_base[:, :], io["h_base"].partition_broadcast(T)).then_inc(weights_in, 16)
                    if not last:
                        load_chunk(sp, io, keep, b + 1, 0)
                        load_chunk(sp, io, keep, b + 1, 1)
                        load_queries(b + 1)

                load_queries(0, True)
                batch(0, True, False)
                with sp.Fori(1, B - 1) as b:
                    batch(b, False, False)
                batch(B - 1, False, True)
                store(B - 1, x1_ready, x_rows[:, :], io["x1_4"])
                store(B - 1, xn_ready, xn[:, :], io["xn_4"])
                store(B - 1, yn_ready, yn[:, :, :].rearrange("p n c -> p (n c)"), io["yn_4"])
                sp.wait_ge(stored, 48 * B)

            @block.gpsimd
            def _(pool):
                for i, row in enumerate((k_lo[HD:HD + 1, :, :], q_lo[HD:HD + 1, :, :], v_lo[:, :, :, HD:HD + 1])):
                    nc.gpsimd.memset(row.bitcast(F32), 0.0).then_inc(pool_preset, 1)
                    pool.wait_ge(pool_preset, i + 1)

                def batch(b, last):
                    for gi in range(GROUPS):
                        if gi in ROUND_AFTER:
                            split_chunk(nc, pool, keep, b, ROUND_AFTER[gi])
                            if isinstance(b, int) and b == 0 and ROUND_AFTER[gi] == 2:
                                pool.wait_ge(keep["chunk_ready"], 3)
                                nc.gpsimd.memset(k_hi[HD:HD + 1, :, :].bitcast(F32), 1.0).then_inc(pool_preset, 1)
                                pool.wait_ge(pool_preset, 4)
                        if isinstance(b, int) and ("group", b, gi) in SK_SLOTS:
                            sk.normalise(nc, pool, SK_SLOTS.index(("group", b, gi)))
                    for s in range(STEPS):
                        if not last and s in AHEAD:
                            split_chunk(nc, pool, keep, b + 1, AHEAD.index(s))
                        if isinstance(b, int) and ("tile", b, s) in SK_SLOTS:
                            sk.normalise(nc, pool, SK_SLOTS.index(("tile", b, s)))

                batch(0, False)
                with pool.Fori(1, EARLY) as b:
                    batch(b, False)
                batch(B - 2, False)
                batch(B - 1, True)

            @block.scalar
            def _(act):
                def project(b, gi):
                    act.wait_ge(proj_done, GROUPS * b + (gi + 1))
                    for place, out_hi, _ in group_pieces(gi):
                        nc.scalar.activation(out_hi, place, ACT.Copy).then_inc(proj_hi, 1)

                def max_row(b, kv):
                    act.wait_ge(row_placed, KV * b + (kv + 1))
                    nc.scalar.activation(q_hi[HD:HD + 1, kv * G:(kv + 1) * G, :],
                                         ps[HD:HD + 1, B_BANK, 0:G * T].rearrange("p (g t) -> p g t", t=T),
                                         ACT.Copy).then_inc(row_ready, 1)

                def copy_last_o(b):
                    kv = KV - 1
                    act.wait_ge(pv_done, STEPS * b + NT * (kv + 1))
                    act.wait_ge(wo_done, KV * b + kv)
                    nc.scalar.activation(o_sb[:, :], ps[0:HD + 1, o_bank(kv), 0:G * T], ACT.Copy).then_inc(o_copied, 1)

                def power(to, of, ready, wanted, b):
                    act.wait_ge(wanted, b + 1)
                    nc.scalar.activation(to, of, ACT.Ln).then_inc(ready, 1)
                    act.wait_ge(ready, 2 * b + 1)
                    nc.scalar.activation(to, to, ACT.Exp, scale=-0.5).then_inc(ready, 1)

                def hyper_part(b, at):
                    if at == HY_RSTD:
                        power(root[:, :], var[:, :], root_ready, var_ready, b)
                    if at == HY_COPY:
                        act.wait_ge(xn_ready, b + 1)
                        nc.scalar.activation(yn[:, :, :], xn[:, :].rearrange("p (n c) -> p n c", c=SW), ACT.Square,
                                             accum_out=square_sum[:, :]).then_inc(square_ready, 1)
                        act.wait_ge(x_turned, b + 1)
                        nc.scalar.activation(xnT[:, :, :], ps[:, Y_BANK, 0:NK * T].rearrange("p (k t) -> p k t", t=T),
                                             ACT.Copy).then_inc(xnT_ready, 1)
                    if at == HY_YN:
                        act.wait_ge(branch_done, b + 1)
                        act.wait_ge(square_ready, b + 1)
                        nc.scalar.activation(yn[:, :, :], ps[0:T, Y_BANK, :].rearrange("p (n c) -> p n c", c=SW),
                                             ACT.Copy).then_inc(yn_ready, 1)
                    if at == HY_RSTD2:
                        power(root[:, :], mean_sq[:, :], root2_ready, mean_ready, b)

                def batch(b, first):
                    if not first:
                        copy_last_o(b - 1)
                    for gi in range(GROUPS):
                        if gi == GROUPS - 1:
                            max_row(b, 0)
                        project(b, gi)
                        if gi in ROUND_AFTER:
                            c = ROUND_AFTER[gi]
                            n = CHUNKS[c][1]
                            act.wait_ge(keep["raw_loaded"], 16 * (NCH + 1) * b + 16 * (NCH + 1 if c == NCH - 1 else c + 1))
                            nc.scalar.activation(c_hi[:, c % 2, :, 0:n], keep["raw"][:, :, 0:n], ACT.Copy).then_inc(keep["chunk_hi"], 1)
                        if not first:
                            hyper_part(b - 1, gi)
                        if isinstance(b, int) and b == EARLY:
                            sk.exponentials(nc, act, gi)
                    for g in range(STEPS):
                        kv, t, n = g // NT, g % NT, KEY_TILES[g % NT][1]
                        act.wait_ge(scores, STEPS * b + (g + 1))
                        act.wait_ge(p_lo_ready, STEPS * b + max(g - 1, 0))
                        nc.scalar.activation(p[0:n, g % 2, :], ps[0:n, S0 + g % 3, 0:G * T], ACT.Exp,
                                             scale=scale).then_inc(exp_done, 1)
                        act.wait_ge(exp_done, STEPS * b + (g + 1))
                        act.wait_ge(pv_done, STEPS * b + max(g - RING + 1, 0))
                        nc.scalar.activation(p_hi[0:n, g % RING, :], p[0:n, g % 2, :], ACT.Copy).then_inc(p_hi_ready, 1)

                nc.scalar.preload_act_table_set("natural_log_exp_and_others")
                batch(0, True)
                with act.Fori(1, EARLY) as b:
                    batch(b, False)
                for b in range(EARLY, B):
                    batch(b, False)
                copy_last_o(B - 1)
                for at in range(GROUPS):
                    hyper_part(B - 1, at)

            @block.vector
            def _(dve):
                nc.vector.memset(ones[:, :], 1.0).then_inc(preset, 1)
                nc.vector.memset(neg_max[:, :, :], 0.0).then_inc(preset, 1)
                nc.vector.memset(v_hi[:, :, :, HD:HD + 1].bitcast(F32), 1.0).then_inc(preset, 1)

                def project(b, gi):
                    for i, (place, out_hi, out_lo) in enumerate(group_pieces(gi)):
                        dve.wait_ge(proj_hi, PIECES * b + (PIECES_BEFORE[gi] + i + 1))
                        nc.vector.tensor_tensor(out_lo, place, out_hi.bitcast(F32), ALU.subtract).then_inc(proj_lo, 1)

                def round_next(b, c, before):
                    dve.wait_ge(proj_done, GROUPS * before + GROUPS)
                    round_chunk(nc, dve, keep, b, c)

                def rough_maximum(b, c, unit):
                    n, heads = MAXIMA_BEFORE[c] + unit, UNITS[c][unit]
                    dve.wait_ge(rough_done, MAXIMA * b + (n + 1))
                    nc.vector.tensor_reduce(maxima[:, heads[0]:heads[-1] + 1, c],
                                            ps[0:T, S0 + n % 3, 0:len(heads) * CHUNKS[c][1]].rearrange("p (h k) -> p h k", h=len(heads)),
                                            AX.X, ALU.max).then_inc(rough_max, 1)

                def negate(b, kv):
                    if kv == 0:
                        dve.wait_ge(rough_max, MAXIMA * b + MAXIMA)
                    nc.vector.tensor_reduce(head_max[:, :], maxima[:, kv * G:(kv + 1) * G, :], AX.X,
                                            ALU.max).then_inc(max_ready, 1)
                    dve.wait_ge(max_ready, KV * b + (kv + 1))
                    dve.wait_ge(row_placed, KV * b + kv)
                    nc.vector.tensor_scalar(neg_max[:, :, HD], head_max[:, :], -1.0, None, ALU.mult).then_inc(neg_ready, 1)

                def copy_o(b, kv):
                    dve.wait_ge(pv_done, STEPS * b + NT * (kv + 1))
                    dve.wait_ge(wo_done, KV * b + kv)
                    nc.vector.tensor_copy(o_sb[:, :], ps[0:HD + 1, o_bank(kv), 0:G * T]).then_inc(o_copied, 1)

                def max_row(b, kv):
                    dve.wait_ge(row_placed, KV * b + (kv + 1))
                    nc.vector.tensor_copy(q_hi[HD:HD + 1, kv * G:(kv + 1) * G, :],
                                          ps[HD:HD + 1, B_BANK, 0:G * T].rearrange("p (g t) -> p g t", t=T)).then_inc(row_ready, 1)

                def invert_sums(b, kv):
                    dve.wait_ge(sums_turned, KV * b + (kv + 1))
                    nc.vector.reciprocal(recip[:, :], ps[0:T, B_BANK, G * T:G * T + G]).then_inc(recip_ready, 1)
                    dve.wait_ge(recip_ready, KV * b + (kv + 1))
                    nc.vector.tensor_tensor(diag[:, :, :], keep["ident"][0:T, 0:T].unsqueeze(1).to_broadcast([T, G, T]),
                                            recip[:, :].unsqueeze(2).to_broadcast([T, G, T]), ALU.mult).then_inc(diag_ready, 1)

                def normalise(b, kv):
                    dve.wait_ge(spread, KV * b + (kv + 1))
                    nc.vector.tensor_tensor(o_sb[0:HD, :], ps[0:HD, B_BANK, 0:G * T], o_sb[0:HD, :], ALU.mult).then_inc(normal, 1)

                def residual(b):
                    dve.wait_ge(wo_done, KV * b + KV)
                    dve.wait_ge(x_loaded, 16 * b + 16)
                    nc.vector.scalar_tensor_tensor(out=x_rows[:, :], in0=ps[0:T, Y_BANK, :], scalar=keep["tanh"][0:T, 0:1],
                                                   in1=x_rows[:, :], op0=ALU.mult, op1=ALU.add).then_inc(x1_ready, 1)

                def newton(b, op, result, of):
                    for i, (to, a, c) in enumerate(((newton_t, root, root), (newton_t, newton_t, of))):
                        nc.vector.tensor_tensor(to[:, :], a[:, :], c[:, :], ALU.mult).then_inc(hyper, 1)
                        dve.wait_ge(hyper, HYPER_OPS * b + (op + i + 1))
                    nc.vector.tensor_scalar(newton_t[:, :], newton_t[:, :], -0.5, 1.5, ALU.mult, ALU.add).then_inc(hyper, 1)
                    dve.wait_ge(hyper, HYPER_OPS * b + (op + 3))
                    nc.vector.tensor_tensor(result[:, :], root[:, :], newton_t[:, :], ALU.mult).then_inc(hyper, 1)
                    dve.wait_ge(hyper, HYPER_OPS * b + (op + 4))

                def hyper_part(b, at):
                    base = HYPER_OPS * b
                    if at == HY_RESIDUAL:
                        residual(b)
                    if at == HY_STATS:
                        dve.wait_ge(x1_ready, b + 1)
                        nc.vector.bn_stats(stats[:, :], x_rows[:, :]).then_inc(hyper, 1)
                        dve.wait_ge(hyper, base + (OP_STATS + 1))
                        dve.sem_inc(settled, 1)
                        nc.vector.bn_aggr(mv[:, :], stats[:, :]).then_inc(hyper, 1)
                        dve.wait_ge(hyper, base + (OP_STATS + 2))
                        nc.vector.tensor_scalar(var[:, :], mv[:, 1:2], LN_EPS, None, ALU.add).then_inc(var_ready, 1)
                    if at == HY_NORM:
                        dve.wait_ge(var_ready, b + 1)
                        dve.wait_ge(root_ready, 2 * b + 2)
                        newton(b, OP_NEWTON, rstd, var)
                        nc.vector.tensor_scalar(xn[:, :], x_rows[:, :], mv[:, 0:1], rstd[:, :], ALU.subtract,
                                                ALU.mult).then_inc(xn_ready, 1)
                    if at == HY_MEAN:
                        dve.wait_ge(square_ready, b + 1)
                        nc.vector.tensor_scalar(mean_sq[:, :], square_sum[:, :], 1.0 / D, RMS_EPS, ALU.mult,
                                                ALU.add).then_inc(mean_ready, 1)
                    if at == HY_LOGIT_ROWS:
                        dve.wait_ge(mean_ready, b + 1)
                        dve.wait_ge(root2_ready, 2 * b + 2)
                        newton(b, OP_NEWTON2, rstd2, mean_sq)
                        dve.wait_ge(logits_done, b + 1)
                        start = b * 24
                        rows = keep["logits"][:, start:start + 24] if isinstance(b, int) else keep["logits"][:, bass.ds(start, 24)]
                        nc.vector.scalar_tensor_tensor(out=rows, in0=ps[0:T, B_BANK, LOGITS:LOGITS + 24], scalar=rstd2[:, :],
                                                       in1=h_base[:, :], op0=ALU.mult, op1=ALU.add).then_inc(logit_rows_ready, 1)

                def batch(b, first, last):
                    for gi in range(GROUPS):
                        c, i = GROUP_OF[gi]
                        for k in range(NK):
                            for unit in ROUGH_AT[c].get((i, k), ()):
                                rough_maximum(b, c, unit)
                        if gi == GROUPS - 2:
                            negate(b, 0)
                        project(b, gi)
                        if not first and gi == END_TURN:
                            invert_sums(b - 1, KV - 1)
                        if not first and gi == END_SPREAD:
                            normalise(b - 1, KV - 1)
                        if not first:
                            hyper_part(b - 1, gi)
                        if isinstance(b, int) and b == EARLY:
                            if gi == SK_ROWS:
                                dve.wait_ge(logit_rows_ready, EARLY)
                            sk.softmax_rows(nc, dve, gi)
                        if isinstance(b, int) and ("group", b, gi) in SK_SLOTS:
                            sk.invert(nc, dve, SK_SLOTS.index(("group", b, gi)))
                    for s in range(STEPS):
                        kv, t, n = s // NT, s % NT, KEY_TILES[s % NT][1]
                        dve.wait_ge(p_hi_ready, STEPS * b + (s + 1))
                        nc.vector.tensor_tensor(p_lo[0:n, s % RING, :], p[0:n, s % 2, :],
                                                p_hi[0:n, s % RING, :].bitcast(F32), ALU.subtract).then_inc(p_lo_ready, 1)
                        if not last and s in AHEAD:
                            round_next(b + 1, AHEAD.index(s), b)
                        if kv and t == COPY_AT:
                            copy_o(b, kv - 1)
                        if kv < KV - 1 and t == ROW_COPY_AT:
                            max_row(b, kv + 1)
                        if kv < KV - 1 and t == NEGATE_AT:
                            negate(b, kv + 1)
                        if kv and t == TURN_AT:
                            invert_sums(b, kv - 1)
                        if kv and t == SPREAD_AT:
                            normalise(b, kv - 1)
                        if isinstance(b, int) and ("tile", b, s) in SK_SLOTS:
                            sk.invert(nc, dve, SK_SLOTS.index(("tile", b, s)))

                batch(0, True, False)
                dve.wait_ge(weights_in, 48)
                with dve.Fori(1, EARLY) as b:
                    batch(b, False, False)
                batch(B - 2, False, False)
                batch(B - 1, False, True)
                invert_sums(B - 1, KV - 1)
                normalise(B - 1, KV - 1)
                for at in range(GROUPS):
                    hyper_part(B - 1, at)
                dve.wait_ge(logit_rows_ready, B)

            @block.tensor
            def _(pe):

                def rough_scores(b, c, unit):
                    n, heads = MAXIMA_BEFORE[c] + unit, UNITS[c][unit]
                    kv = heads[0] // G
                    pe.wait_ge(rough_max, MAXIMA * b + max(n - 2, 0))
                    if heads[0] % G == 0:
                        g = FIRST_GROUP[c] + kv
                        pe.wait_ge(proj_hi, PIECES * b + (PIECES_BEFORE[g] + 1 if kv < KG else PIECES_BEFORE[g]))
                    if n == 0:
                        pe.wait_ge(exp_done, STEPS * b)
                        pe.wait_ge(q_loaded, 32 * b + 32)
                    if c == 0 and heads[0] == H - G:
                        pe.wait_ge(q_last_loaded, 32 * b + 32)
                    k0, keys, _, _ = CHUNKS[c]
                    for i, head in enumerate(heads):
                        mm = pe.matmul(ps[0:T, S0 + n % 3, i * keys:(i + 1) * keys], q_hi[0:HD, head, :],
                                       k_hi[0:HD, kv, k0:k0 + keys], start=True, stop=True)
                    mm.then_inc(rough_done, 1)

                def place_max_row(b, kv):
                    if kv == 0 and isinstance(b, int):
                        pe.wait_ge(preset, 3)
                        pe.wait_ge(pool_preset, 4)
                    pe.wait_ge(neg_ready, KV * b + (kv + 1))
                    pe.wait_ge(row_ready, KV * b + kv)
                    pe.wait_ge(normal, KV * b + max(kv - 1, 0))
                    for i in range(G):
                        mm = pe.matmul(ps[0:HD + 1, B_BANK, i * T:(i + 1) * T], neg_max[:, i, :],
                                       keep["ident"][0:T, 0:T], start=True, stop=True)
                    mm.then_inc(row_placed, 1)

                def project(b, gi, first):
                    c, i = GROUP_OF[gi]
                    k0, n, t0, _ = CHUNKS[c]
                    slot = c % 2
                    if i == 0:
                        pe.wait_ge(chunk_ready, NCH * b + (c + 1))
                    pe.wait_ge(proj_lo, PIECES * b + PIECES_BEFORE[max(gi - 2, 0)])
                    for k in range(NK):
                        if i < KG:
                            w = slice(i * 128, (i + 1) * 128)
                            mm = split_product(pe, ps[:, M0 + gi % 3, 0:n], keep["wk_hi"][:, k, w], keep["wk_lo"][:, k, w],
                                               c_hi[:, slot, k, 0:n], c_lo[:, slot, k, 0:n], k == 0, k == NK - 1)
                        else:
                            key0, rows = KEY_TILES[t0 + i - KG]
                            keys = slice(key0 - k0, key0 - k0 + rows)
                            mm = split_product(pe, ps[0:rows, M0 + gi % 3, 0:KV * HD], c_hi[:, slot, k, keys],
                                               c_lo[:, slot, k, keys], keep["wv_hi"][:, k, :], keep["wv_lo"][:, k, :],
                                               k == 0, k == NK - 1)
                        for unit in ROUGH_AT[c].get((i, k), ()):
                            rough_scores(b, c, unit)
                        if (gi, k) == (GROUPS - 1, 1):
                            place_max_row(b, 0)
                        if gi == 0 and k < LAG and not first:
                            weigh_values(b - 1, STEPS - LAG + k)
                    mm.then_inc(proj_done, 1)

                def score(b, g):
                    kv, t = g // NT, g % NT
                    k0, n = KEY_TILES[t]
                    pe.wait_ge(exp_done, STEPS * b + max(g - 2, 0))
                    if g == 0:
                        pe.wait_ge(rough_max, MAXIMA * b + MAXIMA)
                        pe.wait_ge(proj_lo, PIECES * b + PIECES_BEFORE[FIRST_GROUP[NCH - 1] + KG])
                    if t == 0:
                        pe.wait_ge(row_ready, KV * b + (kv + 1))
                    q = slice(kv * G, (kv + 1) * G)
                    split_product(pe, ps[0:n, S0 + g % 3, 0:G * T], k_hi[:, kv, k0:k0 + n], k_lo[:, kv, k0:k0 + n],
                                  q_hi[:, q, :], q_lo[:, q, :], True, True).then_inc(scores, 1)

                def weigh_values(b, g):
                    kv, t = g // NT, g % NT
                    n = KEY_TILES[t][1]
                    pe.wait_ge(p_lo_ready, STEPS * b + (g + 1))
                    if g == 0:
                        pe.wait_ge(proj_lo, PIECES * b + PIECES)
                    if t == 0:
                        pe.wait_ge(o_copied, KV * b + max(kv - 1, 0))
                    split_product(pe, ps[0:HD + 1, o_bank(kv), 0:G * T], v_hi[0:n, t, kv, :], v_lo[0:n, t, kv, :],
                                  p_hi[0:n, g % RING, :], p_lo[0:n, g % RING, :], t == 0, t == NT - 1).then_inc(pv_done, 1)

                def turn_sums(b, kv):
                    pe.wait_ge(o_copied, KV * b + (kv + 1))
                    pe.wait_ge(row_ready, KV * b + min(kv + 2, KV))
                    for i in range(G):
                        mm = pe.matmul(ps[0:T, B_BANK, G * T + i:G * T + i + 1], o_sb[HD:HD + 1, i * T:(i + 1) * T],
                                       ones[HD:HD + 1, 0:1], start=True, stop=True)
                    mm.then_inc(sums_turned, 1)

                def spread_recip(b, kv):
                    pe.wait_ge(diag_ready, KV * b + (kv + 1))
                    pe.matmul(ps[0:HD, B_BANK, 0:G * T], ones[0:T, :], diag[:, :, :],
                              start=True, stop=True).then_inc(spread, 1)

                def project_out(b, kv):
                    pe.wait_ge(normal, KV * b + (kv + 1))
                    if kv == 0:
                        pe.wait_ge(wo_loaded, 16)
                        pe.wait_ge(yn_ready, b)
                    for i in range(G):
                        mm = pe.matmul(ps[0:T, Y_BANK, :], o_sb[0:HD, i * T:(i + 1) * T], wo[:, kv * G + i, :],
                                       start=(kv == 0 and i == 0), stop=(kv == KV - 1 and i == G - 1))
                    mm.then_inc(wo_done, 1)

                def hyper_part(b, at):
                    if at == HY_TURN:
                        pe.wait_ge(xn_ready, b + 1)
                        for k in range(NK):
                            mm = pe.transpose(ps[:, Y_BANK, k * T:(k + 1) * T], xn[:, k * 128:(k + 1) * 128],
                                              keep["ident"][0:T, 0:T])
                        mm.then_inc(x_turned, 1)
                    if at == HY_LOGITS:
                        pe.wait_ge(xnT_ready, b + 1)
                        for k in range(NK):
                            mm = pe.matmul(ps[0:T, B_BANK, LOGITS:LOGITS + 24], xnT[:, k, :], w_h[:, k, :],
                                           start=(k == 0), stop=(k == NK - 1))
                        mm.then_inc(logits_done, 1)
                        for k in range(NK):
                            mm = pe.matmul(ps[0:T, Y_BANK, k * SW:(k + 1) * SW], xnT[:, k, :], w_branch[:, :],
                                           start=True, stop=True)
                        mm.then_inc(branch_done, 1)

                def batch(b, first):
                    for gi in range(GROUPS):
                        project(b, gi, first)
                        for end, at in ((turn_sums, END_TURN), (spread_recip, END_SPREAD), (project_out, END_OUT)):
                            if not first and gi == at:
                                end(b - 1, KV - 1)
                        if not first:
                            hyper_part(b - 1, gi)
                    for s in range(STEPS):
                        kv, t = s // NT, s % NT
                        score(b, s)
                        if kv < KV - 1 and t == MAX_ROW_AT:
                            place_max_row(b, kv + 1)
                        if s >= LAG:
                            weigh_values(b, s - LAG)
                        if 0 < kv < KV and t == TURN_AT:
                            turn_sums(b, kv - 1)
                        if 0 < kv < KV and t == SPREAD_AT:
                            spread_recip(b, kv - 1)
                        if 0 < kv < KV and t == OUT_AT:
                            project_out(b, kv - 1)

                batch(0, True)
                pe.wait_ge(weights_in, 48)
                with pe.Fori(1, B) as b:
                    batch(b, False)
                for s in range(STEPS - LAG, STEPS):
                    weigh_values(B - 1, s)
                for end in (turn_sums, spread_recip, project_out):
                    end(B - 1, KV - 1)
                for at in range(GROUPS):
                    hyper_part(B - 1, at)


def hyper_connection(nc, whole, io, keep):
    with ExitStack() as ctx:
        def sb(name, shape, dt=F32):
            return ctx.enter_context(nc.sbuf_tensor("b_" + name, shape, dt))

        def sem(name):
            return whole.enter_context(nc.semaphore("b_" + name))

        x_rows = keep["x_rows"]
        xn = sb("xn", [T, B, D])
        yn = sb("yn", [T, B, STREAMS, SW])
        y = sb("y", [T, B, SW])
        pool_term = sb("pool_term", [T, STREAMS, SW])
        mixer = sb("mixer", [T, 2])
        stats, mv = sb("stats", [T, HB, 6]), sb("mv", [T, HB, 2])
        var, sd, tmp, rstd = (sb("s%d" % i, [T, HB]) for i in range(4))
        ps = ctx.enter_context(nc.psum_tensor("b_ps", [128, 8, BANK], F32))
        _, var_ready, sd_ready, xn_ready, turned, hi_ready, lo_ready = keep["ln_sems"]
        x_nT = keep["xnT_hi"], keep["xnT_lo"]
        queries = FeatureQueries(nc, keep, ps, 0)
        h_res = sb("res", [T, B, 4, 4])
        raw = sb("raw", [128, NK, D])
        raw_loaded, small_loaded, w_hi_ready, w_lo_ready = (sem(n) for n in ("raw", "small", "w_hi", "w_lo"))
        step, weights_ready, pool_step = (sem(n) for n in ("step", "weights", "pool_step"))
        loaded = [sem("in%d" % i) for i in range(2)]
        sk = Sinkhorn(keep, 1, EARLY, B)
        POOL_BATCHES = (2, 3, 4, 5)
        LATE_STREAMS = 2
        POOL_OPS = 2 * STREAMS - 1 + 2 * (STREAMS + 1)

        with nc.Block() as block:
            @block.sync
            def _(sp):
                for i, part in enumerate((slice(0, EARLY), slice(EARLY, B))):
                    for to, of in ((x_rows, "x1_4"), (xn, "xn_4"), (yn[:, :, :, :].rearrange("p b n c -> p b (n c)"), "yn_4")):
                        sp.dma_start(to[:, part, :], io[of][part].rearrange("b t d -> t b d")).then_inc(loaded[i], 16)
                sp.dma_start(raw[:, :, :], io["wq1T"]).then_inc(raw_loaded, 16)
                sp.dma_start(keep["bq1"][:, :], io["bq1"]).then_inc(small_loaded, 16)
                sp.dma_start(keep["bk1"][:, :], io["bk1"]).then_inc(small_loaded, 16)
                sp.wait_ge(w_lo_ready, 1)
                sp.dma_start(raw[:, :, :], io["wk1"]).then_inc(raw_loaded, 16)
                sp.wait_ge(small_loaded, 32)

            @block.scalar
            def _(act):
                for at in (SK_EXP, SK_LN, SK_EXP2):
                    sk.exponentials(nc, act, at)
                for i, name in enumerate(("wq1", "wk1")):
                    act.wait_ge(raw_loaded, 16 * (i + 1))
                    nc.scalar.activation(keep[name + "_hi"][:, :, :], raw[:, :, :], ACT.Copy).then_inc(w_hi_ready, 1)
                act.wait_ge(var_ready, 1)
                nc.scalar.activation(sd[:, :], var[:, :], ACT.Sqrt).then_inc(sd_ready, 1)
                for b in range(HB):
                    act.wait_ge(turned, b + 1)
                    nc.scalar.activation(x_nT[0][:, :, columns(b)], turned_rows(ps, b), ACT.Copy).then_inc(hi_ready, 1)
                act.wait_ge(small_loaded, 32)
                queries.scalar_queries(act)
                queries.scalar_features(act)

            @block.gpsimd
            def _(pool):
                done = [0]

                def link(ins):
                    done[0] += 1
                    ins.then_inc(pool_step, 1)
                    pool.wait_ge(pool_step, done[0])

                pool.wait_ge(loaded[0], 48)
                pool.wait_ge(weights_ready, 1)
                def branch_sum(b):
                    for j in range(STREAMS):
                        by = keep["h_pp"][:, b, 0, j:j + 1].to_broadcast([T, SW])
                        link(nc.gpsimd.tensor_tensor((pool_term[:, 0, :] if j else y[:, b, :]), yn[:, b, j, :], by, ALU.mult))
                        if j:
                            link(nc.gpsimd.tensor_tensor(y[:, b, :], y[:, b, :], pool_term[:, 0, :], ALU.add))

                def mix(b, first):
                    count = STREAMS - first
                    streams = x_rows[:, b, first * SW:].rearrange("p (n c) -> p n c", c=SW)
                    term = pool_term[:, 0:count, :]
                    for j in range(STREAMS + 1):
                        of, by = ((y[:, b, :], keep["h_pp"][:, b, 1, first:]) if j == STREAMS else
                                  (xn[:, b, j * SW:(j + 1) * SW], h_res[:, b, first:, j]))
                        link(nc.gpsimd.tensor_tensor(term, of.unsqueeze(1).to_broadcast([T, count, SW]),
                                                     by.unsqueeze(2).to_broadcast([T, count, SW]), ALU.mult))
                        link(nc.gpsimd.tensor_tensor(streams, streams, term, ALU.add))

                for i, b in enumerate(POOL_BATCHES):
                    branch_sum(b)
                    mix(b, 0)
                    if i < 2:
                        name = ("wq1", "wk1")[i]
                        pool.wait_ge(w_hi_ready, i + 1)
                        nc.gpsimd.tensor_tensor(keep[name + "_lo"][:, :, :], raw[:, :, :],
                                                keep[name + "_hi"][:, :, :].bitcast(F32), ALU.subtract).then_inc(w_lo_ready, 1)
                pool.wait_ge(w_lo_ready, 2)
                pool.wait_ge(loaded[1], 48)
                for b in range(EARLY, B):
                    branch_sum(b)
                pool.wait_ge(weights_ready, 2)
                mix(B - 1, STREAMS - LATE_STREAMS)

            @block.tensor
            def _(pe):
                for b in range(HB):
                    pe.wait_ge(xn_ready, b + 1)
                    for k in range(NK):
                        mm = pe.transpose(ps[:, b, k * T:(k + 1) * T], xn[:, b, k * 128:(k + 1) * 128], keep["ident"][0:T, 0:T])
                    mm.then_inc(turned, 1)
                pe.wait_ge(w_lo_ready, 2)
                pe.wait_ge(lo_ready, HB)
                queries.tensor(pe, x_nT)

            @block.vector
            def _(dve):
                done = [0]

                def step_of(ins):
                    done[0] += 1
                    ins.then_inc(step, 1)

                def link(ins):
                    step_of(ins)
                    dve.wait_ge(step, done[0])

                def weights(part):
                    flat = h_res[:, part, :, :].rearrange("p b i j -> p b (i j)")
                    link(nc.vector.tensor_scalar(h_res[:, part, :, :], keep["sink"][:, part, :, :], mixer[:, 0:1], None, ALU.mult))
                    nc.vector.tensor_scalar(flat[:, :, 0:16:5], flat[:, :, 0:16:5], mixer[:, 1:2], None, ALU.add).then_inc(weights_ready, 1)

                def streams_of(b):
                    return STREAMS - (LATE_STREAMS if b == B - 1 else 0)

                def mixing(batches):
                    for b in batches:
                        for j in range(STREAMS):
                            if b >= EARLY:
                                pass
                            elif j == 0:
                                yield lambda: nc.vector.tensor_scalar(y[:, b, :], yn[:, b, 0, :], keep["h_pp"][:, b, 0, 0:1], None, ALU.mult)
                            else:
                                yield lambda: nc.vector.scalar_tensor_tensor(
                                    out=y[:, b, :], in0=yn[:, b, j, :], scalar=keep["h_pp"][:, b, 0, j:j + 1], in1=y[:, b, :],
                                    op0=ALU.mult, op1=ALU.add)
                            for i in range(streams_of(b)):
                                stream = slice(i * SW, (i + 1) * SW)
                                yield lambda: nc.vector.scalar_tensor_tensor(
                                    out=x_rows[:, b, stream], in0=xn[:, b, j * SW:(j + 1) * SW], scalar=h_res[:, b, i, j:j + 1],
                                    in1=x_rows[:, b, stream], op0=ALU.mult, op1=ALU.add)
                        for i in range(streams_of(b)):
                            stream = slice(i * SW, (i + 1) * SW)
                            yield lambda: nc.vector.scalar_tensor_tensor(
                                out=x_rows[:, b, stream], in0=y[:, b, :], scalar=keep["h_pp"][:, b, 1, i:i + 1],
                                in1=x_rows[:, b, stream], op0=ALU.mult, op1=ALU.add)

                link(nc.vector.tensor_scalar(mixer[:, :], keep["sigmoid"][0:T, :], keep["tanh"][0:T, 2:3], None, ALU.mult))
                weights(slice(0, EARLY))
                for at in (SK_ROWS, SK_SUMS, SK_COLS):
                    sk.softmax_rows(nc, dve, at)
                dve.wait_ge(weights_ready, 1)
                dve.wait_ge(sk.e2_ready, 2)

                def settle(op):
                    dve.wait_ge(step, done[0])
                    return op()

                def half_queries():
                    for b in range(HB):
                        if b in POOL_BATCHES:
                            for _ in range(20):
                                yield None
                            dve.wait_ge(pool_step, POOL_OPS * (POOL_BATCHES.index(b) + 1))
                        yield lambda: settle(lambda: nc.vector.bn_stats(stats[:, b, :], x_rows[:, b, :]))
                        yield lambda: settle(lambda: nc.vector.bn_aggr(mv[:, b, :], stats[:, b, :]))
                    yield lambda: settle(lambda: nc.vector.tensor_scalar(var[:, :], mv[:, :, 1], LN_EPS, None, ALU.add))
                    dve.wait_ge(step, done[0])
                    dve.sem_inc(var_ready, 1)
                    for _ in range(12):
                        yield None
                    dve.wait_ge(sd_ready, 1)
                    for op in (lambda: nc.vector.reciprocal(rstd[:, :], sd[:, :]),
                               lambda: nc.vector.tensor_tensor(tmp[:, :], rstd[:, :], rstd[:, :], ALU.mult),
                               lambda: nc.vector.tensor_tensor(tmp[:, :], tmp[:, :], var[:, :], ALU.mult),
                               lambda: nc.vector.tensor_scalar(tmp[:, :], tmp[:, :], -0.5, 1.5, ALU.mult, ALU.add),
                               lambda: nc.vector.tensor_tensor(rstd[:, :], rstd[:, :], tmp[:, :], ALU.mult)):
                        yield lambda: settle(op)
                    for b in range(HB):
                        yield lambda: settle(lambda: nc.vector.tensor_scalar(xn[:, b, :], x_rows[:, b, :], mv[:, b, 0:1],
                                                                             rstd[:, b:b + 1], ALU.subtract, ALU.mult))
                        yield None
                        dve.wait_ge(step, done[0])
                        dve.sem_inc(xn_ready, 1)
                    for _ in range(4):
                        yield None
                    for b in range(HB):
                        dve.wait_ge(hi_ready, b + 1)
                        nc.vector.tensor_tensor(x_nT[1][:, :, columns(b)], turned_rows(ps, b),
                                                x_nT[0][:, :, columns(b)].bitcast(F32), ALU.subtract).then_inc(lo_ready, 1)
                        yield None
                        yield None
                    for m in range(NK):
                        for _ in range(12):
                            yield None
                        queries.vector_hi(dve, m)
                        yield None
                        queries.vector_lo(dve, m)
                        yield None

                def all_beside():
                    yield from mixing([b for b in range(EARLY) if b not in POOL_BATCHES])
                    yield from half_queries()

                beside = all_beside()

                def linked(ins, mix):
                    step_of(ins)
                    mine = done[0]
                    other = next(beside, None) if mix else None
                    if other is not None:
                        step_of(other())
                    dve.wait_ge(step, mine)

                MIX_FROM = 20
                for n in range(NORMS):
                    mix = n >= MIX_FROM
                    if n == MIX_FROM:
                        dve.wait_ge(loaded[0], 48)
                    m, spread = ((sk.sink.rearrange("p b i j -> p b j i"), sk.along_cols) if n % 2 == 0 else
                                 (sk.sink, sk.along_rows))
                    linked(nc.vector.tensor_reduce(sk.marginal, m, AX.X, ALU.add), mix)
                    linked(nc.vector.reciprocal(sk.inverse, sk.marginal), mix)
                    linked(nc.vector.tensor_tensor(sk.sink, sk.sink, spread(sk.inverse), ALU.mult), mix)
                for other in beside:
                    if other is not None:
                        dve.wait_ge(step, done[0] - 1)
                        step_of(other())
                weights(slice(EARLY, B))
                dve.wait_ge(weights_ready, 2)
                dve.wait_ge(loaded[1], 48)
                whole_batches, rest = mixing(range(EARLY, B - 1)), mixing([B - 1])
                dve.wait_ge(pool_step, POOL_OPS * len(POOL_BATCHES) + (2 * STREAMS - 1) * (B - EARLY))
                for _ in range((B - 1 - EARLY) * STREAMS * (STREAMS + 1) // 2):
                    for batch in (whole_batches, whole_batches, rest):
                        op = next(batch, None)
                        if op is not None:
                            dve.wait_ge(step, done[0] - 1)
                            step_of(op())
                dve.wait_ge(step, done[0])


LN_SEMS = ("step", "var", "sd", "xn", "turned", "hi", "lo")
HB = B // 2


def turned_rows(ps, b):
    return ps[:, b % HB, 0:NK * T].rearrange("p (k t) -> p k t", t=T)


def columns(b):
    return slice(b * T, (b + 1) * T)


def layer_norm_turned(nc, name, keep, batches, turn, before, links, x_nT, sync_beside=None, scalar_beside=None, gpsimd_beside=None):
    with ExitStack() as ctx:
        def sb(n, shape, dt=F32):
            return ctx.enter_context(nc.sbuf_tensor(name + n, shape, dt))

        x_rows = keep["x_rows"]
        first, nb = batches[0], len(batches)
        xn = sb("xn", [T, nb, D])
        stats, mv = sb("stats", [T, nb, 6]), sb("mv", [T, nb, 2])
        var, sd, tmp, rstd = (sb("s%d" % i, [T, nb]) for i in range(4))
        ps = ctx.enter_context(nc.psum_tensor(name + "ps", [128, 8, BANK], F32))
        step, var_ready, sd_ready, xn_ready, turned, hi_ready, lo_ready = keep["ln_sems"]

        with nc.Block() as block:
            if sync_beside:
                block.sync(sync_beside)
            if gpsimd_beside:
                block.gpsimd(gpsimd_beside)

            @block.scalar
            def _(act):
                act.wait_ge(var_ready, turn + 1)
                nc.scalar.activation(sd[:, :], var[:, :], ACT.Sqrt).then_inc(sd_ready, 1)
                if scalar_beside:
                    scalar_beside(act)
                for i in range(nb):
                    act.wait_ge(turned, before + i + 1)
                    nc.scalar.activation(x_nT[0][:, :, columns(first + i)], turned_rows(ps, i), ACT.Copy).then_inc(hi_ready, 1)

            @block.vector
            def _(dve):
                done = [links]

                def link(ins):
                    done[0] += 1
                    ins.then_inc(step, 1)
                    dve.wait_ge(step, done[0])

                for i in range(nb):
                    nc.vector.bn_stats(stats[:, i, :], x_rows[:, first + i, :]).then_inc(step, 1)
                    done[0] += 1
                for i in range(nb):
                    dve.wait_ge(step, done[0] - (nb - 1))
                    nc.vector.bn_aggr(mv[:, i, :], stats[:, i, :]).then_inc(step, 1)
                    done[0] += 1
                dve.wait_ge(step, done[0])
                nc.vector.tensor_scalar(var[:, :], mv[:, :, 1], LN_EPS, None, ALU.add).then_inc(var_ready, 1)
                dve.wait_ge(var_ready, turn + 1)
                dve.wait_ge(sd_ready, turn + 1)
                refined_rsqrt(nc, link, rstd[:, :], sd[:, :], var[:, :], tmp[:, :])
                for i in range(nb):
                    nc.vector.tensor_scalar(xn[:, i, :], x_rows[:, first + i, :], mv[:, i, 0:1], rstd[:, i:i + 1],
                                            ALU.subtract, ALU.mult).then_inc(xn_ready, 1)
                for i in range(nb):
                    dve.wait_ge(hi_ready, before + i + 1)
                    nc.vector.tensor_tensor(x_nT[1][:, :, columns(first + i)], turned_rows(ps, i),
                                            x_nT[0][:, :, columns(first + i)].bitcast(F32), ALU.subtract).then_inc(lo_ready, 1)

            @block.tensor
            def _(pe):
                for i in range(nb):
                    pe.wait_ge(xn_ready, before + i + 1)
                    if i >= HB:
                        pe.wait_ge(lo_ready, before + i - HB + 1)
                    for k in range(NK):
                        mm = pe.transpose(ps[:, i % HB, k * T:(k + 1) * T], xn[:, i, k * 128:(k + 1) * 128], keep["ident"][0:T, 0:T])
                    mm.then_inc(turned, 1)


Q_SEMS = ("q", "q_copied", "q_hi", "q_lo", "f", "f_copied", "qbk", "qbk_copied")
QBK = 0
Q0 = 4


class FeatureQueries:

    def __init__(self, nc, keep, ps, half):
        self.nc, self.keep, self.ps, self.half = nc, keep, ps, half
        self.cols = slice(half * HALF, (half + 1) * HALF)
        self.q_done, self.q_copied, self.q_hi_ready, self.q_lo_ready, self.f_done, self.f_copied, self.qbk_done, self.qbk_copied = (
            keep["q_sems"])

    def scalar_queries(self, act):
        for m in range(NK):
            act.wait_ge(self.q_done, NK * self.half + m + 1)
            self.nc.scalar.activation(self.keep["q1"][:, m, self.cols], self.ps[:, Q0 + m, 0:HALF], ACT.Identity,
                                      bias=self.keep["bq1"][:, m:m + 1]).then_inc(self.q_copied, 1)

    def scalar_features(self, act):
        act.wait_ge(self.qbk_done, self.half + 1)
        self.nc.scalar.activation(self.keep["qbk"][:, self.half * HB:(self.half + 1) * HB], self.ps[0:T, QBK, 0:HB],
                                  ACT.Copy).then_inc(self.qbk_copied, 1)
        for m in range(NK):
            act.wait_ge(self.f_done, NK * self.half + m + 1)
            self.nc.scalar.activation(self.keep["queries"][:, m, self.cols], self.ps[:, Q0 + m, 0:HALF],
                                      ACT.Copy).then_inc(self.f_copied, 1)

    def vector_hi(self, dve, m):
        dve.wait_ge(self.q_copied, NK * self.half + m + 1)
        self.nc.vector.tensor_copy(self.keep["q1_hi"][:, m, :], self.keep["q1"][:, m, self.cols]).then_inc(self.q_hi_ready, 1)

    def vector_lo(self, dve, m):
        dve.wait_ge(self.q_hi_ready, NK * self.half + m + 1)
        self.nc.vector.tensor_tensor(self.keep["q1_lo"][:, m, :], self.keep["q1"][:, m, self.cols],
                                     self.keep["q1_hi"][:, m, :].bitcast(F32), ALU.subtract).then_inc(self.q_lo_ready, 1)

    def product(self, pe, m, w, of, cols, done):
        for k in range(NK):
            to = slice(m * 128, (m + 1) * 128)
            mm = split_product(pe, self.ps[:, Q0 + m, 0:HALF], self.keep[w + "_hi"][:, k, to], self.keep[w + "_lo"][:, k, to],
                               of[0][:, k, cols], of[1][:, k, cols], k == 0, k == NK - 1)
        mm.then_inc(done, 1)

    def tensor(self, pe, x_nT):
        for m in range(NK):
            if self.half:
                pe.wait_ge(self.f_copied, NK * self.half)
            self.product(pe, m, "wq1", x_nT, self.cols, self.q_done)
        pe.wait_ge(self.q_lo_ready, NK * (self.half + 1))
        for i in range(HB):
            for k in range(NK):
                mm = pe.matmul(self.ps[0:T, QBK, i:i + 1], self.keep["q1"][:, k, columns(self.half * HB + i)],
                               self.keep["bk1"][:, k:k + 1], start=(k == 0), stop=(k == NK - 1))
        mm.then_inc(self.qbk_done, 1)
        for m in range(NK):
            self.product(pe, m, "wk1", (self.keep["q1_hi"], self.keep["q1_lo"]), slice(0, HALF), self.f_done)


def project_features(nc, whole, io, keep):
    with ExitStack() as ctx:
        def load_first_features(sp):
            for b in range(2):
                for c, (f0, n) in enumerate(SB):
                    if b:
                        sp.wait_ge(keep["feats_loaded"][c], 16)
                    sp.dma_start(keep["feats"][:, b, :, f0:f0 + n], io["ctxT"][b, :, :, f0:f0 + n]).then_inc(keep["feats_loaded"][c], 16)

        x_nT = keep["xnT_hi"], keep["xnT_lo"]
        layer_norm_turned(nc, "cn_", keep, range(HB, B), 1, HB, 0, x_nT, sync_beside=load_first_features)
        ps = ctx.enter_context(nc.psum_tensor("c_ps", [128, 8, BANK], F32))
        queries = FeatureQueries(nc, keep, ps, 1)

        with nc.Block() as block:
            @block.scalar
            def _(act):
                queries.scalar_queries(act)
                queries.scalar_features(act)

            @block.vector
            def _(dve):
                for m in range(NK):
                    queries.vector_hi(dve, m)
                    queries.vector_lo(dve, m)

            @block.tensor
            def _(pe):
                queries.tensor(pe, x_nT)


FT = [(128 * i, 128) for i in range(10)] + [(1280, 82), (1362, 82)]
NF = len(FT)
SB = chunk_sizes(CTX, BANK)
NSB = len(SB)
TG = NF // NSB
SCORES_AT, WEIGH_LAG, NATURAL_RING = 3, 3, 6
SCORE_PRODUCTS = [(k, part) for k in range(NK) for part in range(3)]
PER_STEP = len(SCORE_PRODUCTS) // ((NF - SCORES_AT) // NSB)
TURN_STEPS = (2, 6, 10)
EXP_STEPS = (1, 2, 3)
QUERY_STEP, GAIN_STEP, UPDATE_STEP = 0, 4, 3
MAX_STEPS = {6: 0, 9: 1}
SPLIT_STEPS = {1: (1, 1), 4: (2, 1), 9: (0, 2)}


def attend_features(nc, whole, io, keep):
    scale = float(D) ** -0.5
    with ExitStack() as ctx:
        def sb(name, shape, dt=F32):
            return ctx.enter_context(nc.sbuf_tensor("f_" + name, shape, dt))

        def sem(name):
            return whole.enter_context(nc.semaphore("f_" + name))

        x_rows = keep["x_rows"]
        feats, loaded = keep["feats"], keep["feats_loaded"]
        c_hi, c_lo = (sb(n, [128, NSB, NK, BANK], F32R) for n in ("c_hi", "c_lo"))
        qs_hi, qs_lo = (sb(n, [128, NK, T], F32R) for n in ("q_hi", "q_lo"))
        n_hi, n_lo = (sb(n, [128, NATURAL_RING, D], F32R) for n in ("n_hi", "n_lo"))
        p = sb("p", [T, CTX])
        pT_hi, pT_lo = (sb(n, [128, NSB, TG, T], F32R) for n in ("pT_hi", "pT_lo"))
        bank_max = sb("bmax", [T, NSB])
        top, bias = sb("top", [T, 1]), sb("bias", [T, 1])
        sums, total, recip, gain = sb("sums", [T, NSB]), sb("total", [T, 1]), sb("recip", [T, 1]), sb("gain", [T, 1])
        ps = ctx.enter_context(nc.psum_tensor("f_ps", [128, 8, BANK], F32))
        S0, N0, P_BANK, O0 = 0, 3, 5, 6

        c_hi_ready, c_ready, qs_hi_ready, qs_ready, scored, maxed, top_ready, shifted, bias_ready = (
            sem(n) for n in ("c_hi", "c", "qs_hi", "qs", "scored", "maxed", "top", "shifted", "bias"))
        exp_done, p_turned, pT_hi_ready, pT_ready, n_turned, n_hi_ready, n_ready, weighed = (
            sem(n) for n in ("exp", "p_turned", "pT_hi", "pT", "n_turned", "n_hi", "n", "weighed"))
        total_ready, recip_ready, gain_ready, x3_ready = (sem(n) for n in ("total", "recip", "gain", "x3"))

        def run(engine, batch):
            batch(0, 0, True, False)
            with engine.Fori(0, (B - 4) // 2) as pair:
                for i in range(2):
                    batch(2 * pair + (i + 1), (i + 1) % 2, False, False)
            for b in range(B - 3, B):
                batch(b, b % 2, False, b == B - 1)

        with nc.Block() as block:
            @block.sync
            def _(sp):
                def load(b, slot, c):
                    f0, n = SB[c]
                    sp.dma_start(feats[:, slot, :, f0:f0 + n], io["ctxT"][b, :, :, f0:f0 + n]).then_inc(loaded[c], 16)

                def reload(b, slot):
                    for c in range(NSB):
                        sp.wait_ge(scored, NSB * b - (NSB - c - 1))
                        load(b, slot, c)

                with sp.Fori(1, B // 2) as pair:
                    for i in range(2):
                        reload(2 * pair + i, i)

            @block.gpsimd
            def _(pool):
                def pair_of_batches(pair, first):
                    for slot in range(2):
                        for c, (f0, n) in enumerate(SB):
                            if first and slot == 0 and c == 0:
                                continue
                            number = 2 * NSB * pair + (NSB * slot + c + 1)
                            pool.wait_ge(c_hi_ready, number)
                            nc.gpsimd.tensor_tensor(c_lo[:, c, :, 0:n], feats[:, slot, :, f0:f0 + n],
                                                    c_hi[:, c, :, 0:n].bitcast(F32), ALU.subtract).then_inc(c_ready, 1)

                pair_of_batches(0, True)
                with pool.Fori(1, B // 2) as pair:
                    pair_of_batches(pair, False)

            @block.scalar
            def _(act):
                def take_queries(b, start):
                    act.wait_ge(scored, NSB * b)
                    nc.scalar.activation(qs_hi[:, :, :], keep["queries"][:, :, start:start + T] if isinstance(start, int)
                                         else keep["queries"][:, :, bass.ds(start, T)], ACT.Copy).then_inc(qs_hi_ready, 1)

                def batch(b, slot, first, last):
                    for t in range(NF):
                        n = FT[t][1]
                        act.wait_ge(n_turned, NF * b + (t + 1))
                        if not first or t >= NATURAL_RING:
                            act.wait_ge(weighed, NF * b + (t - NATURAL_RING + 1))
                        nc.scalar.activation(n_hi[0:n, t % NATURAL_RING, :], ps[0:n, N0 + t % 2, :], ACT.Copy).then_inc(n_hi_ready, 1)
                        if t in EXP_STEPS:
                            c = EXP_STEPS.index(t)
                            f0, n = SB[c]
                            act.wait_ge(bias_ready, b + 1)
                            nc.scalar.activation(p[:, f0:f0 + n], ps[0:T, S0 + c, 0:n], ACT.Exp, scale=scale, bias=bias[:, :],
                                                 accum_out=sums[:, c:c + 1]).then_inc(exp_done, 1)
                        if t == QUERY_STEP and not last:
                            take_queries(b + 1, b * T + T)
                        if t in TURN_STEPS:
                            g = TURN_STEPS.index(t)
                            act.wait_ge(p_turned, NSB * b + (g + 1))
                            act.wait_ge(weighed, NF * b)
                            nc.scalar.activation(pT_hi[:, g, :, :], ps[:, P_BANK, 0:TG * T].rearrange("p (i t) -> p i t", t=T),
                                                 ACT.Copy).then_inc(pT_hi_ready, 1)

                take_queries(0, 0)
                run(act, batch)

            @block.vector
            def _(dve):
                def round_bank(b, slot, c):
                    f0, n = SB[c]
                    dve.wait_ge(loaded[c], 16 * b + 16)
                    if not (isinstance(b, int) and b == 0):
                        dve.wait_ge(scored, NSB * b + (c + 1 - NSB))
                    nc.vector.tensor_copy(c_hi[:, c, :, 0:n], feats[:, slot, :, f0:f0 + n]).then_inc(c_hi_ready, 1)

                def split_queries(b, start):
                    dve.wait_ge(qs_hi_ready, b + 1)
                    nc.vector.tensor_tensor(qs_lo[:, :, :], keep["queries"][:, :, start:start + T] if isinstance(start, int)
                                            else keep["queries"][:, :, bass.ds(start, T)],
                                            qs_hi[:, :, :].bitcast(F32), ALU.subtract).then_inc(qs_ready, 1)

                def bank_maximum(b, c):
                    dve.wait_ge(scored, NSB * b + (c + 1))
                    nc.vector.tensor_reduce(bank_max[:, c:c + 1], ps[0:T, S0 + c, 0:SB[c][1]], AX.X, ALU.max).then_inc(maxed, 1)

                def softmax_bias(b):
                    qbk = keep["qbk"][:, b:b + 1] if isinstance(b, int) else keep["qbk"][:, bass.ds(b, 1)]
                    dve.wait_ge(maxed, NSB * b + NSB)
                    nc.vector.tensor_reduce(top[:, :], bank_max[:, :], AX.X, ALU.max).then_inc(top_ready, 1)
                    dve.wait_ge(top_ready, b + 1)
                    nc.vector.tensor_tensor(top[:, :], top[:, :], qbk, ALU.add).then_inc(shifted, 1)
                    dve.wait_ge(shifted, 2 * b + 1)
                    nc.vector.tensor_tensor(top[:, :], qbk, top[:, :], ALU.subtract).then_inc(shifted, 1)
                    dve.wait_ge(shifted, 2 * b + 2)
                    dve.wait_ge(exp_done, NSB * b)
                    nc.vector.tensor_scalar(bias[:, :], top[:, :], scale, None, ALU.mult).then_inc(bias_ready, 1)

                def softmax_gain(b):
                    dve.wait_ge(exp_done, NSB * b + NSB)
                    nc.vector.tensor_reduce(total[:, :], sums[:, :], AX.X, ALU.add).then_inc(total_ready, 1)
                    dve.wait_ge(total_ready, b + 1)
                    nc.vector.reciprocal(recip[:, :], total[:, :]).then_inc(recip_ready, 1)
                    dve.wait_ge(recip_ready, b + 1)
                    dve.wait_ge(x3_ready, b)
                    nc.vector.tensor_scalar(gain[:, :], recip[:, :], keep["tanh"][0:T, 1:2], None, ALU.mult).then_inc(gain_ready, 1)

                def update(b, slot):
                    rows = x_rows[:, b, :]
                    dve.wait_ge(weighed, NF * b + NF)
                    dve.wait_ge(gain_ready, b + 1)
                    nc.vector.scalar_tensor_tensor(out=rows, in0=ps[0:T, O0 + slot, :], scalar=gain[:, :], in1=rows,
                                                   op0=ALU.mult, op1=ALU.add).then_inc(x3_ready, 1)

                def batch(b, slot, first, last):
                    bank_maximum(b, NSB - 1)
                    softmax_bias(b)
                    for t in range(NF):
                        n = FT[t][1]
                        dve.wait_ge(n_hi_ready, NF * b + (t + 1))
                        nc.vector.tensor_tensor(n_lo[0:n, t % NATURAL_RING, :], ps[0:n, N0 + t % 2, :],
                                                n_hi[0:n, t % NATURAL_RING, :].bitcast(F32), ALU.subtract).then_inc(n_ready, 1)
                        if t == QUERY_STEP and not last:
                            split_queries(b + 1, b * T + T)
                        if t in TURN_STEPS:
                            g = TURN_STEPS.index(t)
                            dve.wait_ge(pT_hi_ready, NSB * b + (g + 1))
                            nc.vector.tensor_tensor(pT_lo[:, g, :, :], ps[:, P_BANK, 0:TG * T].rearrange("p (i t) -> p i t", t=T),
                                                    pT_hi[:, g, :, :].bitcast(F32), ALU.subtract).then_inc(pT_ready, 1)
                        if t == UPDATE_STEP and not first:
                            update(b - 1, 1 - slot)
                        if t == GAIN_STEP:
                            softmax_gain(b)
                        if t in SPLIT_STEPS:
                            c, ahead = SPLIT_STEPS[t]
                            if not last and not (isinstance(b, int) and b + ahead >= B):
                                round_bank(b + ahead, (slot + ahead) % 2, c)
                        if t in MAX_STEPS and not last:
                            bank_maximum(b + 1, MAX_STEPS[t])

                for c in range(NSB):
                    round_bank(0, 0, c)
                    if c == 0:
                        dve.wait_ge(c_hi_ready, 1)
                        nc.vector.tensor_tensor(c_lo[:, 0, :, 0:SB[0][1]], feats[:, 0, :, 0:SB[0][1]],
                                                c_hi[:, 0, :, 0:SB[0][1]].bitcast(F32), ALU.subtract).then_inc(c_ready, 1)
                        split_queries(0, 0)
                for c in range(NSB - 1):
                    bank_maximum(0, c)
                round_bank(1, 1, 0)
                run(dve, batch)
                update(B - 1, (B - 1) % 2)
                dve.wait_ge(x3_ready, B)

            @block.tensor
            def _(pe):
                def scores(b, c, products):
                    f0, n = SB[c]
                    for i in products:
                        k, part = SCORE_PRODUCTS[i]
                        if i == 0:
                            pe.wait_ge(c_ready, NSB * b + (c + 1))
                            if c == 0:
                                pe.wait_ge(qs_ready, b + 1)
                            if not (isinstance(b, int) and b == 0):
                                pe.wait_ge(exp_done, NSB * b + (c + 1 - NSB))
                        mm = pe.matmul(ps[0:T, S0 + c, 0:n], (qs_lo if part == 2 else qs_hi)[:, k, :],
                                       (c_lo if part == 1 else c_hi)[:, c, k, 0:n],
                                       start=(i == 0), stop=(i == len(SCORE_PRODUCTS) - 1))
                        if i == len(SCORE_PRODUCTS) - 1:
                            mm.then_inc(scored, 1)

                def weigh(b, slot, t, first=False):
                    n, g = FT[t][1], t // TG
                    pe.wait_ge(n_ready, NF * b + (t + 1))
                    if t % TG == 0:
                        pe.wait_ge(pT_ready, NSB * b + (g + 1))
                    if t == 0 and not first:
                        pe.wait_ge(gain_ready, b)
                    split_product(pe, ps[0:T, O0 + slot, :], pT_hi[0:n, g, t % TG, :], pT_lo[0:n, g, t % TG, :],
                                  n_hi[0:n, t % NATURAL_RING, :], n_lo[0:n, t % NATURAL_RING, :], t == 0, t == NF - 1).then_inc(weighed, 1)

                def batch(b, slot, first, last):
                    for t in range(NF):
                        f0, n = FT[t]
                        if not first or t >= 2:
                            pe.wait_ge(n_ready, NF * b + (t - 1))
                        for k in range(NK):
                            mm = pe.transpose(ps[0:n, N0 + t % 2, k * 128:(k + 1) * 128], feats[:, slot, k, f0:f0 + n],
                                              keep["ident"][:, :])
                        mm.then_inc(n_turned, 1)
                        if t in TURN_STEPS:
                            g = TURN_STEPS.index(t)
                            pe.wait_ge(exp_done, NSB * b + min(NSB, g + 1))
                            pe.wait_ge(pT_ready, NSB * b + g)
                            for i in range(TG):
                                g0, rows = FT[g * TG + i]
                                mm = pe.transpose(ps[0:rows, P_BANK, i * T:(i + 1) * T], p[:, g0:g0 + rows],
                                                  keep["ident"][0:T, 0:T])
                            mm.then_inc(p_turned, 1)
                        if t >= SCORES_AT and not last:
                            at = (t - SCORES_AT) * PER_STEP
                            c, start = at // len(SCORE_PRODUCTS), at % len(SCORE_PRODUCTS)
                            scores(b + 1, c, range(start, start + PER_STEP))
                        if t >= WEIGH_LAG:
                            weigh(b, slot, t - WEIGH_LAG, first)
                        elif not first:
                            weigh(b - 1, 1 - slot, NF - WEIGH_LAG + t)

                for c in range(NSB):
                    scores(0, c, range(len(SCORE_PRODUCTS)))
                run(pe, batch)
                for t in range(NF - WEIGH_LAG, NF):
                    weigh(B - 1, (B - 1) % 2, t)


FC = chunk_sizes(FF, 128)
NFC = len(FC)
W_RING, H_RING = 2, 3


def feed_forward(nc, whole, io, keep):
    with ExitStack() as ctx:
        def sb(name, shape, dt=F32):
            return ctx.enter_context(nc.sbuf_tensor("d_" + name, shape, dt))

        def sem(name):
            return whole.enter_context(nc.semaphore("d_" + name))

        x_rows = keep["x_rows"]
        x_nT = [sb(n, [128, NK, NTOK], F32R) for n in ("xnT_hi", "xnT_lo")]
        raw_in = sb("raw_in", [128, W_RING, 2, NK, 128])
        raw_down = sb("raw_down", [128, W_RING, D])
        win_hi, win_lo = (sb(n, [128, NFC, 2, NK, 128], F32R) for n in ("win_hi", "win_lo"))
        loaded = [sem("in%d" % i) for i in range(W_RING)]
        w_hi_ready, w_ready = sem("w_hi"), sem("w")

        def load_weights(sp, f):
            (f0, n), slot = FC[f], f % W_RING
            for i, w in enumerate(("wgT", "wuT")):
                sp.dma_start(raw_in[:, slot, i, :, 0:n], io[w][:, :, f0:f0 + n]).then_inc(loaded[slot], 16)
            sp.dma_start(raw_down[0:n, slot, :], io["wdT"][f0:f0 + n, :]).then_inc(loaded[slot], 16)

        def split_in(pool, f):
            n, slot = FC[f][1], f % W_RING
            pool.wait_ge(w_hi_ready, 2 * f + 1)
            nc.gpsimd.tensor_tensor(win_lo[:, f, :, :, 0:n], raw_in[:, slot, :, :, 0:n],
                                    win_hi[:, f, :, :, 0:n].bitcast(F32), ALU.subtract).then_inc(w_ready, 1)

        def split_down(pool, f):
            n, slot = FC[f][1], f % W_RING
            pool.wait_ge(w_hi_ready, 2 * f + 2)
            nc.gpsimd.tensor_tensor(wd_lo[0:n, f, :], raw_down[0:n, slot, :],
                                    wd_hi[0:n, f, :].bitcast(F32), ALU.subtract).then_inc(w_ready, 1)

        def load_first(sp):
            for f in range(W_RING):
                load_weights(sp, f)

        def round_first(act):
            n = FC[0][1]
            act.wait_ge(loaded[0], 48)
            nc.scalar.activation(win_hi[:, 0, :, :, 0:n], raw_in[:, 0, :, :, 0:n], ACT.Copy).then_inc(w_hi_ready, 1)

        layer_norm_turned(nc, "dn_", keep, range(B), 2, B, 2 * HB + 5, x_nT, sync_beside=load_first, scalar_beside=round_first,
                          gpsimd_beside=lambda pool: split_in(pool, 0))
        wd_hi, wd_lo = (sb(n, [128, NFC, D], F32R) for n in ("wd_hi", "wd_lo"))
        h = sb("h", [128, 2, HALF])
        h_hi, h_lo = (sb(n, [128, H_RING, HALF], F32R) for n in ("h_hi", "h_lo"))
        yT = sb("yT", [128, NK, HALF])
        ps = ctx.enter_context(nc.psum_tensor("d_ps", [128, 8, BANK], F32))
        G0, Y0 = 0, 4

        gu_done, gate_ready, h_ready, h_hi_ready, h_lo_ready, down_done = (
            sem(n) for n in ("gu", "gate", "h", "h_hi", "h_lo", "down"))
        y_copied, y_turned, out_ready, stored = (sem(n) for n in ("y", "y_turned", "out_ready", "out"))

        with nc.Block() as block:
            @block.sync
            def _(sp):
                for f in range(W_RING, NFC):
                    sp.wait_ge(w_ready, 2 * (f - W_RING + 1))
                    load_weights(sp, f)
                for b in range(B):
                    sp.wait_ge(out_ready, b + 1)
                    sp.dma_start(io["out4"][b], x_rows[:, b, :]).then_inc(stored, 16)
                sp.wait_ge(stored, 16 * B)

            @block.gpsimd
            def _(pool):
                for f in range(NFC):
                    if f:
                        split_in(pool, f)
                    split_down(pool, f)

            @block.scalar
            def _(act):
                def copy_half(half):
                    for d in range(NK):
                        act.wait_ge(down_done, NFC * (half + 1))
                        act.wait_ge(y_turned, half * (B // 2))
                        nc.scalar.activation(yT[:, d, :], ps[:, Y0 + d, 0:HALF], ACT.Copy).then_inc(y_copied, 1)

                for i in range(2 * NFC):
                    n = FC[i % NFC][1]
                    act.wait_ge(gu_done, i + 1)
                    if i >= 2:
                        act.wait_ge(h_lo_ready, i - 1)
                    nc.scalar.activation(h[0:n, i % 2, :], ps[0:n, G0 + 2 * (i % 2), 0:HALF], ACT.Silu).then_inc(gate_ready, 1)
                    act.wait_ge(h_ready, i + 1)
                    if i >= H_RING:
                        act.wait_ge(down_done, i - H_RING + 1)
                    nc.scalar.activation(h_hi[0:n, i % H_RING, :], h[0:n, i % 2, :], ACT.Copy).then_inc(h_hi_ready, 1)
                    if i == NFC:
                        copy_half(0)
                copy_half(1)

            @block.vector
            def _(dve):
                def round_weights(f):
                    n, slot = FC[f][1], f % W_RING
                    dve.wait_ge(loaded[slot], 48 * (f // W_RING + 1))
                    if f:
                        nc.vector.tensor_copy(win_hi[:, f, :, :, 0:n], raw_in[:, slot, :, :, 0:n]).then_inc(w_hi_ready, 1)
                    nc.vector.tensor_copy(wd_hi[0:n, f, :], raw_down[0:n, slot, :]).then_inc(w_hi_ready, 1)

                def add_half(half):
                    for b in range(half * (B // 2), (half + 1) * (B // 2)):
                        dve.wait_ge(y_turned, b + 1)
                        nc.vector.scalar_tensor_tensor(out=x_rows[:, b, :], in0=ps[0:T, G0 + b % 4, :], scalar=keep["tanh"][0:T, 3:4],
                                                       in1=x_rows[:, b, :], op0=ALU.mult, op1=ALU.add).then_inc(out_ready, 1)

                for f in range(W_RING):
                    round_weights(f)
                for i in range(2 * NFC):
                    n = FC[i % NFC][1]
                    dve.wait_ge(gate_ready, i + 1)
                    nc.vector.tensor_tensor(h[0:n, i % 2, :], ps[0:n, G0 + 2 * (i % 2) + 1, 0:HALF], h[0:n, i % 2, :],
                                            ALU.mult).then_inc(h_ready, 1)
                    dve.wait_ge(h_hi_ready, i + 1)
                    nc.vector.tensor_tensor(h_lo[0:n, i % H_RING, :], h[0:n, i % 2, :], h_hi[0:n, i % H_RING, :].bitcast(F32),
                                            ALU.subtract).then_inc(h_lo_ready, 1)
                    if i + W_RING < NFC:
                        round_weights(i + W_RING)
                    if i == NFC + 1:
                        add_half(0)
                add_half(1)

            @block.tensor
            def _(pe):
                def gate_up(i):
                    half, f, n = i // NFC, i % NFC, FC[i % NFC][1]
                    pe.wait_ge(w_ready, 2 * f + 1)
                    if i >= 2:
                        pe.wait_ge(h_ready, i - 1)
                    cols = slice(half * HALF, (half + 1) * HALF)
                    for j in range(2):
                        for k in range(NK):
                            mm = split_product(pe, ps[0:n, G0 + 2 * (i % 2) + j, 0:HALF], win_hi[:, f, j, k, 0:n], win_lo[:, f, j, k, 0:n],
                                               x_nT[0][:, k, cols], x_nT[1][:, k, cols], k == 0, k == NK - 1)
                    mm.then_inc(gu_done, 1)

                def down(i):
                    f, n = i % NFC, FC[i % NFC][1]
                    pe.wait_ge(w_ready, 2 * f + 2)
                    pe.wait_ge(h_lo_ready, i + 1)
                    for d in range(NK):
                        if i == NFC:
                            pe.wait_ge(y_copied, d + 1)
                        to = slice(d * 128, (d + 1) * 128)
                        mm = split_product(pe, ps[:, Y0 + d, 0:HALF], wd_hi[0:n, f, to], wd_lo[0:n, f, to],
                                           h_hi[0:n, i % H_RING, :], h_lo[0:n, i % H_RING, :], f == 0, f == NFC - 1)
                    mm.then_inc(down_done, 1)

                def turn_back(half):
                    for b in range(half * (B // 2), (half + 1) * (B // 2)):
                        i = b % (B // 2)
                        if i == 0:
                            pe.wait_ge(y_copied, NK * (half + 1))
                            pe.wait_ge(h_ready, NFC + 2 if half == 0 else 2 * NFC)
                        for d in range(NK):
                            mm = pe.transpose(ps[0:T, G0 + i, d * 128:(d + 1) * 128], yT[:, d, i * T:(i + 1) * T], keep["ident"][:, :])
                        mm.then_inc(y_turned, 1)

                for i in range(2 * NFC):
                    if i == NFC + 2:
                        turn_back(0)
                        pe.wait_ge(out_ready, B // 2)
                    gate_up(i)
                    if i:
                        down(i - 1)
                down(2 * NFC - 1)
                turn_back(1)


def flamingo(nc, a, out):
    with ExitStack() as whole:
        def dram(name, shape, dt=F32):
            return nc.dram_tensor(name, shape, dt, kind="Internal").ap()

        def keep_sb(stack, name, shape, dt=F32):
            keep[name] = stack.enter_context(nc.sbuf_tensor("keep_" + name, shape, dt))

        latT = dram("latT_scratch", [128, NK, NTOK])
        q_hi, q_lo = (dram(n, [HD, B, H, T]) for n in ("q_hi_scratch", "q_lo_scratch"))
        rows = {n: dram(n + "_scratch", [NTOK, D]) for n in ("x1", "xn", "yn")}
        io = dict(a)
        io.update(
            latT=latT, latT4=latT.rearrange("p k (b t) -> b p k t", t=T),
            q_hi=q_hi, q_lo=q_lo, q_hi4=q_hi.rearrange("d b h t -> b d h t"), q_lo4=q_lo.rearrange("d b h t -> b d h t"),
            x4=a["x"].rearrange("(b t) d -> b t d", t=T),
            **{n + "_4": r.rearrange("(b t) d -> b t d", t=T) for n, r in rows.items()},
            out4=out.rearrange("(b t) d -> b t d", t=T))
        keep = {"sinkhorn_sems": [whole.enter_context(nc.semaphore("sk_" + n)) for n in SK_SEMS],
                "q_sems": [whole.enter_context(nc.semaphore("q1_" + n)) for n in Q_SEMS],
                "ln_sems": [whole.enter_context(nc.semaphore("ln_" + n)) for n in LN_SEMS]}
        for n, s in (("ident", [128, 128]), ("gates", [128, 8]), ("tanh", [128, 4]), ("sigmoid", [128, 2])):
            keep_sb(whole, n, s)
        with ExitStack() as early:
            for n, s in (("logits", [T, B * 24]), ("row_max", [T, B, 6]), ("row_sum", [T, B, 6]), ("row_ln", [T, B, 4]),
                         ("h_pp", [T, B, 2, 4]), ("log_res", [T, B, 4, 4]), ("sink", [T, B, 4, 4]), ("pairs", [T, B, 8]),
                         ("marginal", [T, B, 4]), ("inverse", [T, B, 4])):
                keep_sb(whole, n, s)
            for n in ("wk_hi", "wk_lo", "wv_hi", "wv_lo"):
                keep_sb(early, n, [128, NK, KV * HD], F32R)
            keep_sb(early, "raw", [128, NK, CHUNK_MAX])
            for n in ("c_hi", "c_lo"):
                keep_sb(early, n, [128, 2, NK, CHUNK_MAX], F32R)
            for n in ("raw_loaded", "chunk_hi", "chunk_ready"):
                keep[n] = whole.enter_context(nc.semaphore(n))
            project_queries(nc, whole, io, keep)
            attend_context(nc, whole, io, keep)
        keep_sb(whole, "x_rows", [T, B, D])
        with ExitStack() as late:
            for n in ("bq1", "bk1"):
                keep_sb(late, n, [128, NK])
            keep_sb(late, "queries", [128, NK, NTOK])
            keep_sb(late, "qbk", [T, B])
            keep_sb(late, "feats", [128, 2, NK, CTX])
            keep["feats_loaded"] = [whole.enter_context(nc.semaphore("feats_loaded%d" % c)) for c in range(NSB)]
            with ExitStack() as projecting:
                for n in ("wq1_hi", "wq1_lo", "wk1_hi", "wk1_lo"):
                    keep_sb(projecting, n, [128, NK, D], F32R)
                for n in ("xnT_hi", "xnT_lo"):
                    keep_sb(projecting, n, [128, NK, NTOK], F32R)
                keep_sb(projecting, "q1", [128, NK, NTOK])
                for n in ("q1_hi", "q1_lo"):
                    keep_sb(projecting, n, [128, NK, HALF], F32R)
                hyper_connection(nc, whole, io, keep)
                project_features(nc, whole, io, keep)
            attend_features(nc, whole, io, keep)
        feed_forward(nc, whole, io, keep)


def kernel(x, ctx_4096, g_xattn, g_ffn, L0_xattn_Wq, L0_xattn_Wk, L0_xattn_Wv, L0_xattn_Wo, L0_ffn_W_res,
           L0_ffn_W_pre, L0_ffn_W_post, L0_ffn_H_res_base, L0_ffn_H_pre_base, L0_ffn_H_post_base, L0_ffn_gate,
           L0_ffn_W_branch, L1_xattn_Wq, L1_xattn_bq, L1_xattn_Wk, L1_xattn_bk, L1_ffn_W_gate, L1_ffn_W_up,
           L1_ffn_W_down):
    import numpy as np
    import concourse.bacc as bacc
    from concourse.bass_utils import run_bass_kernel_spmd

    def by_k(w):
        w = np.asarray(w)
        return np.ascontiguousarray(w.T.reshape(w.shape[1] // 128, 128, w.shape[0]).transpose(1, 0, 2))

    def column(v):
        return np.ascontiguousarray(np.asarray(v).reshape(-1, 128).T)

    flat = [np.asarray(v).reshape(-1) for v in (g_xattn, g_ffn, L0_ffn_gate)]
    packed = np.concatenate([np.r_[i * HD:(i + 1) * HD, 3 * HD + 32 * i:3 * HD + 32 * (i + 1)] for i in range(KV - 1)])
    arrays = {
        "x": np.asarray(x).reshape(NTOK, D),
        "ctxT": np.ascontiguousarray(np.asarray(ctx_4096).transpose(0, 2, 1).reshape(B, NK, 128, CTX).transpose(0, 2, 1, 3)),
        "gates": np.concatenate(flat).reshape(1, 5),
        "wqT": by_k(L0_xattn_Wq), "wkT": by_k(np.asarray(L0_xattn_Wk)[packed]), "wvT": by_k(L0_xattn_Wv),
        "woT": np.ascontiguousarray(np.asarray(L0_xattn_Wo).T.reshape(H, HD, D).transpose(1, 0, 2)),
        "whT": by_k(np.concatenate([np.asarray(w) for w in (L0_ffn_W_res, L0_ffn_W_pre, L0_ffn_W_post)])),
        "h_base": np.concatenate([np.asarray(v).reshape(-1) for v in
                                  (L0_ffn_H_res_base, L0_ffn_H_pre_base, L0_ffn_H_post_base)]).reshape(1, 24),
        "w_branch": np.asarray(L0_ffn_W_branch),
        "wq1T": by_k(L1_xattn_Wq), "wk1": np.ascontiguousarray(np.asarray(L1_xattn_Wk).reshape(NK, 128, D).transpose(1, 0, 2)),
        "bq1": column(L1_xattn_bq), "bk1": column(L1_xattn_bk),
        "wgT": by_k(L1_ffn_W_gate), "wuT": by_k(L1_ffn_W_up),
        "wdT": np.ascontiguousarray(np.asarray(L1_ffn_W_down).T),
    }
    nc = bacc.Bacc("TRN2", target_bir_lowering=False, num_devices=1)
    maps, aps = {}, {}
    for name, a in arrays.items():
        maps[f"in_{name}"] = a
        aps[name] = nc.dram_tensor(f"in_{name}", a.shape, mybir.dt.from_np(a.dtype), kind="ExternalInput").ap()
    out = nc.dram_tensor("out_0", (NTOK, D), F32, kind="ExternalOutput").ap()
    flamingo(nc, aps, out)
    r = run_bass_kernel_spmd(nc, [maps], core_ids=[0])
    return r.results[0]["out_0"].reshape(B, T, D)
```
